# Optimizing a Trainium2 kernel written in Bass

```python
import numpy as np
import jax
import jax.numpy as jnp

def _softmax(x, axis=-1):
    return jax.nn.softmax(x, axis=axis)

def _gelu(x):
    return jax.nn.gelu(x, approximate=True)

def _silu(x):
    return jax.nn.silu(x)

def _sigmoid(x):
    return jax.nn.sigmoid(x)

def _layernorm(x, axis=-1, eps=1e-05):
    m = jnp.mean(x, axis=axis, keepdims=True)
    v = jnp.var(x, axis=axis, keepdims=True)
    return (x - m) / jnp.sqrt(v + eps)

def _scatter_add(tgt, idx, src, axis=0):
    return tgt.at[idx].add(src)

def _segment_sum(src, seg, n):
    return jax.ops.segment_sum(src, seg, n)
kernel_name = 'mk_xattn_ffn_d1_seqx_r4_a95ef8'

def setup_inputs(seed: int=0):
    np.random.seed(seed)
    _w = jnp.asarray

    def _rec_inputs():
        import jax
        import jax.numpy as jnp
        _rk = jax.random.key(seed)
        x = 7.22e-05 + 1 * jax.random.normal(jax.random.fold_in(_rk, 1), (8, 256, 512), jnp.float32)
        _lenS = 256 - jax.random.randint(jax.random.fold_in(_rk, 7), (8,), 0, max(1, 256 // 4) + 1, jnp.int32)
        _lenS2 = 256 - jax.random.randint(jax.random.fold_in(_rk, 8), (8,), 0, max(1, 256 // 4) + 1, jnp.int32)
        _ctx_512P = jax.random.normal(jax.random.fold_in(_rk, 11), (8, 16, 128), jnp.float32)
        _ctx_512c = jax.random.dirichlet(jax.random.fold_in(_rk, 511), 0.3 * jnp.ones((16,), jnp.float32), (8, 256))
        _ctx_512t = jnp.einsum('bsk,bkd->bsd', _ctx_512c, _ctx_512P)
        _ctx_512t = _ctx_512t * jax.lax.rsqrt(jnp.mean(jnp.square(_ctx_512t)) + 1e-12) * 0.953939
        ctx_512 = -0.000514642 + 1.00011 * (_ctx_512t + 0.3 * jax.random.normal(jax.random.fold_in(_rk, 611), (8, 256, 128), jnp.float32))
        return (x, ctx_512)
    x, ctx_512 = _rec_inputs()

    def _L0_xattn_setup():
        import jax, jax.numpy as jnp
        import numpy as np
        import math
        NUM_Q_HEADS = 32
        NUM_KV_HEADS = 8
        key = jax.random.key(seed)
        k1, k2, k3 = jax.random.split(key, 3)
        B, S, E = (2, 512, 512)
        kv_E = NUM_KV_HEADS * (E // NUM_Q_HEADS)
        q = jax.random.normal(k1, (B, S, E), dtype=jnp.float32)
        k = jax.random.normal(k2, (B, S, kv_E), dtype=jnp.float32)
        v = jax.random.normal(k3, (B, S, kv_E), dtype=jnp.float32)
        return {'q': q, 'k': k, 'v': v}
    _L0_xattn_all = _L0_xattn_setup()
    _L0_xattn_in = {k: v for k, v in _L0_xattn_all.items() if k in ()}
    del _L0_xattn_all

    def _L0_ffn_setup():
        import jax, jax.numpy as jnp
        import numpy as np
        B, S, D = (4, 128, 512)
        E, K, H = (8, 2, 352)
        HS = 2 * 352
        ALPHA = 0.001
        W_SCALE = 0.02

        def _moe_forward(hidden_states, gate_w, w_gate, w_up, w_down, sw_gate, sw_up, sw_down):
            b, s, d = hidden_states.shape
            x = hidden_states.reshape(-1, d)
            T = x.shape[0]
            logits = x @ gate_w
            scores = jax.nn.softmax(logits, axis=-1)
            topk_w, topk_idx = jax.lax.top_k(scores, K)
            mask = jax.nn.one_hot(topk_idx, E, dtype=scores.dtype).sum(axis=1)
            ce = mask.mean(axis=0)
            Pi = scores.mean(axis=0)
            aux_loss = (Pi * ce * E).sum() * ALPHA
            comb = jnp.zeros((T, E), dtype=x.dtype)
            comb = comb.at[jnp.arange(T)[:, None], topk_idx].add(topk_w)
            g = jax.nn.silu(jnp.einsum('td,edh->teh', x, w_gate)) * jnp.einsum('td,edh->teh', x, w_up)
            routed = jnp.einsum('teh,ehd,te->td', g, w_down, comb)
            shared = jax.nn.silu(x @ sw_gate) * (x @ sw_up) @ sw_down
            out = (routed + shared).reshape(b, s, d)
            return (out, aux_loss)
        key = jax.random.key(seed)
        ks = jax.random.split(key, 8)
        rn = lambda k, sh: jax.random.normal(k, sh, dtype=jnp.float32)
        return {'hidden_states': rn(ks[0], (B, S, D)), 'gate_w': rn(ks[1], (D, E)) * W_SCALE, 'w_gate': rn(ks[2], (E, D, H)) * W_SCALE, 'w_up': rn(ks[3], (E, D, H)) * W_SCALE, 'w_down': rn(ks[4], (E, H, D)) * W_SCALE, 'sw_gate': rn(ks[5], (D, HS)) * W_SCALE, 'sw_up': rn(ks[6], (D, HS)) * W_SCALE, 'sw_down': rn(ks[7], (HS, D)) * W_SCALE}
    _L0_ffn_all = _L0_ffn_setup()
    _L0_ffn_in = {k: v for k, v in _L0_ffn_all.items() if k in ('gate_w', 'w_gate', 'w_up', 'w_down', 'sw_gate', 'sw_up', 'sw_down')}
    del _L0_ffn_all
    return {'x': x, 'ctx_512': ctx_512, 'L0_ffn_gate_w': _L0_ffn_in['gate_w'], 'L0_ffn_w_gate': _L0_ffn_in['w_gate'], 'L0_ffn_w_up': _L0_ffn_in['w_up'], 'L0_ffn_w_down': _L0_ffn_in['w_down'], 'L0_ffn_sw_gate': _L0_ffn_in['sw_gate'], 'L0_ffn_sw_up': _L0_ffn_in['sw_up'], 'L0_ffn_sw_down': _L0_ffn_in['sw_down']}

def reference(x, ctx_512, L0_ffn_gate_w, L0_ffn_w_gate, L0_ffn_w_up, L0_ffn_w_down, L0_ffn_sw_gate, L0_ffn_sw_up, L0_ffn_sw_down):
    import jax
    import jax.numpy as jnp

    def _L0_xattn_ref(q, k, v):
        import jax, jax.numpy as jnp
        import numpy as np
        import math
        NUM_Q_HEADS = 32
        NUM_KV_HEADS = 8
        B, S, E = q.shape
        H, KV = (NUM_Q_HEADS, NUM_KV_HEADS)
        D = E // H
        G = H // KV
        scale = math.sqrt(D)
        qh = q.reshape(B, S, KV, G, D).transpose(0, 2, 3, 1, 4)
        kh = k.reshape(B, S, KV, D).transpose(0, 2, 1, 3)
        vh = v.reshape(B, S, KV, D).transpose(0, 2, 1, 3)
        scores = jnp.einsum('bkgsd,bktd->bkgst', qh, kh) / scale
        weights = jax.nn.softmax(scores, axis=-1)
        out = jnp.einsum('bkgst,bktd->bkgsd', weights, vh)
        return out.transpose(0, 3, 1, 2, 4).reshape(B, S, E)

    def _L0_ffn_ref(hidden_states, gate_w, w_gate, w_up, w_down, sw_gate, sw_up, sw_down):
        import jax, jax.numpy as jnp
        import numpy as np
        B, S, D = (4, 128, 512)
        E, K, H = (8, 2, 352)
        HS = 2 * 352
        ALPHA = 0.001
        W_SCALE = 0.02

        def _moe_forward(hidden_states, gate_w, w_gate, w_up, w_down, sw_gate, sw_up, sw_down):
            b, s, d = hidden_states.shape
            x = hidden_states.reshape(-1, d)
            T = x.shape[0]
            logits = x @ gate_w
            scores = jax.nn.softmax(logits, axis=-1)
            topk_w, topk_idx = jax.lax.top_k(scores, K)
            mask = jax.nn.one_hot(topk_idx, E, dtype=scores.dtype).sum(axis=1)
            ce = mask.mean(axis=0)
            Pi = scores.mean(axis=0)
            aux_loss = (Pi * ce * E).sum() * ALPHA
            comb = jnp.zeros((T, E), dtype=x.dtype)
            comb = comb.at[jnp.arange(T)[:, None], topk_idx].add(topk_w)
            g = jax.nn.silu(jnp.einsum('td,edh->teh', x, w_gate)) * jnp.einsum('td,edh->teh', x, w_up)
            routed = jnp.einsum('teh,ehd,te->td', g, w_down, comb)
            shared = jax.nn.silu(x @ sw_gate) * (x @ sw_up) @ sw_down
            out = (routed + shared).reshape(b, s, d)
            return (out, aux_loss)
        out, _aux = _moe_forward(hidden_states, gate_w, w_gate, w_up, w_down, sw_gate, sw_up, sw_down)
        return out
    x = x + _L0_xattn_ref(_layernorm(x, axis=-1), ctx_512, ctx_512)
    x = x + _L0_ffn_ref(_layernorm(x, axis=-1), L0_ffn_gate_w, L0_ffn_w_gate, L0_ffn_w_up, L0_ffn_w_down, L0_ffn_sw_gate, L0_ffn_sw_up, L0_ffn_sw_down)
    return x

_drawn_inputs = setup_inputs


def setup_inputs(seed=0):
    import zlib

    import numpy as np

    out = dict(_drawn_inputs(seed))
    spreads = {}
    factors = {'L0_ffn_gate_w': 7.254,
     'L0_ffn_w_gate': 6.399,
     'L0_ffn_w_up': 6.263,
     'L0_ffn_w_down': 6.276,
     'L0_ffn_sw_gate': 8.0,
     'L0_ffn_sw_up': 8.0,
     'L0_ffn_sw_down': 8.0}
    for name, (base, spread) in spreads.items():
        noise = np.random.default_rng([zlib.crc32(name.encode()), seed]).standard_normal(out[name].shape)
        drawn = base * np.exp(spread * noise) if base else spread * noise
        out[name] = jnp.asarray(drawn.astype(out[name].dtype))
    for name, factor in factors.items():
        out[name] = (out[name] * factor).astype(out[name].dtype)
    return out
```

```python
from contextlib import ExitStack

import concourse.bass as bass
from concourse import mybir

P = 128
F32 = mybir.dt.float32
F32R = mybir.dt.float32r
BF16 = mybir.dt.bfloat16
I32 = mybir.dt.int32
U32 = mybir.dt.uint32
ALU = mybir.AluOpType
ACT = mybir.ActivationFunctionType
AX_X = mybir.AxisListType.X

B, S, E = 8, 256, 512
KV, G, D = 8, 4, 16
H = KV * G
T = B * S
NT = T // P
ST = S // P
EC = E // P
HALF = KV // 2
SCALE = 1.0 / D ** 0.5
EPS = 1e-5
RSQRT_SEED = float(0x5F3759DF)
NEWTON = 4

NE, TOP, HID = 8, 2, 352
SETS = 2
HC = 3
HID_TAIL = HID - (HC - 1) * P
UP_AT, DOWN_AT = EC * HID, 2 * EC * HID
W_COLS = DOWN_AT + HC * E
SLOT_TILES = (TOP * T) // P + NE - 1
ZERO_TILES = -(-SLOT_TILES // B)
SLOT_ROWS = ZERO_TILES * B * P
NA = NT // 2
UNITS_A = SETS * NA

Q_PART = (0, 1, 2, 0, 1, 0)
K_PART = (0, 0, 0, 1, 1, 2)
TERMS = len(Q_PART)
Q_RUNS = ((0, 3, 0, 1), (0, 2, 3, 1), (0, 1, 5, 1))
K_RUNS = ((0, 1, 0, 3), (1, 1, 3, 2), (2, 1, 5, 1))
ROWS = TERMS * D
ROWS_MAX = ROWS + 2


def rsqrt_newton(eng, chain, out, var, t1, t2):
    chain(eng.tensor_scalar(var, var, EPS, None, ALU.add))
    chain(eng.tensor_scalar(out.bitcast(I32), var.bitcast(I32), -0.5, RSQRT_SEED, ALU.mult, ALU.add))
    for _ in range(NEWTON):
        chain(eng.tensor_tensor(t1, out, out, ALU.mult))
        chain(eng.tensor_tensor(t2, t1, var, ALU.mult))
        chain(eng.tensor_scalar(t1, t2, -0.5, 1.5, ALU.mult, ALU.add))
        chain(eng.tensor_tensor(out, out, t1, ALU.mult))


def each_batch(eng, body):
    body(0, 0)
    with eng.Fori(1, 4, 2) as i:
        body(i, 1)
        body(i + 1, 2)
    for b in (5, 6, 7):
        body(b, b)


JOBS = (
    (0, "max_b", 0),
    (1, "query_0", 2),
    (2, "key", 2),
    (3, "query_1", 2),
    (4, "out_b0", -1),
    (5, "out_b1", -1),
    (8, "max_a", 1),
    (12, "out_a0", 0),
    (13, "out_a1", 0),
)
FIRST_JOBS = (("query_0", 0), ("query_1", 0), ("key", 0), ("query_0", 1), ("query_1", 1), ("key", 1), ("max_a", 0))
LAST_JOBS = (("out_b0", B - 1), ("out_b1", B - 1))


def job_at(slot, n):
    for s, job, away in JOBS:
        if s == slot and 0 <= n + away < B:
            return job, away
    return None, 0


def job_before(slot, n):
    here = [(job, away) for s, job, away in JOBS if s < slot and 0 <= n + away < B]
    if here:
        return here[-1]
    if n == 0:
        job, b = FIRST_JOBS[-1]
        return job, b
    there = [(job, away - 1) for _, job, away in JOBS if 0 <= n - 1 + away < B]
    return there[-1]


def attention(nc, x_res, ident, ident_bf, x, ctx512, q_scr, k_scr, xg, sh, sl, shared_src):
    x_dram = x.rearrange("b (t p) e -> b p t e", p=P)
    ctx_dram = ctx512.rearrange("b (t p) e -> b p t e", p=P)

    with ExitStack() as ctx:
        def sb(name, shape, dt=F32):
            return ctx.enter_context(nc.sbuf_tensor(name, shape, dt))

        def psum(name, shape, dt=F32):
            return ctx.enter_context(nc.psum_tensor(name, shape, dt))

        def sem(name):
            return ctx.enter_context(nc.semaphore(name))

        stats = sb("stats", [P, NT, 6])
        mean_var = sb("mean_var", [P, NT, 2])
        rstd = sb("rstd", [P, NT])
        var = sb("var", [P, NT])
        newton_1 = sb("newton_1", [P, NT])
        newton_2 = sb("newton_2", [P, NT])
        xn = sb("xn", [P, ST, E])
        q_part = sb("q_part", [P, 2, EC, 3, S], BF16)
        q_rest = sb("q_rest", [P, EC, P])
        k_part = sb("k_part", [P, 3, S], BF16)
        k_rest = sb("k_rest", [P, S])
        ctx_cur = sb("ctx_cur", [P, 2, ST, KV * D])
        q_stack = sb("q_stack", [ROWS_MAX, 2, H, S], BF16)
        k_stack = sb("k_stack", [ROWS_MAX, 2, KV, S], BF16)
        v_aug = sb("v_aug", [P, 2, ST, KV, 32])
        maxes = sb("maxes", [P, 2, ST, HALF * G])
        max_part = sb("max_part", [P, ST, 2, HALF * G], BF16)
        max_rows = sb("max_rows", [2 * HALF * G, S], BF16)
        probs = sb("probs", [P, 2, ST, G, S])
        out_t = sb("out_t", [P, 2, HALF, S])
        rden = sb("rden", [P, HALF * G])
        out_norm = sb("out_norm", [P, 2, HALF * G * D])

        stage = sb("sh_stage", [P, 2, UP_AT])
        zero = sb("zero", [P, E // 2])

        ps_score = psum("ps_score", [P, 2, G, S])
        ps_max = psum("ps_max", [P, 2, 2, S])
        ps_out = psum("ps_out", [P, 2, S])
        ps_job = psum("ps_job", [P, 4 * P])
        ps_job_bf = ps_job[:].bitcast(BF16)

        x_first, x_rest = sem("x_first"), sem("x_rest")
        ctx_loaded = [sem(f"ctx_loaded{i}") for i in range(2)]
        ln_step = sem("ln_step")
        ones_set = sem("ones_set")
        zero_set, cleared, ident_set = sem("zero_set"), sem("cleared"), sem("ident_set")
        high_loaded, stage_loaded, weights_split = sem("sh_high_loaded"), [sem(f"sh_stage_loaded{i}") for i in range(2)], sem("sh_split")
        xn_ready = [sem(f"xn_ready{i}") for i in range(ST)]
        names = [job for _, job, _ in JOBS]
        job_done = {j: sem("done_" + j) for j in names}
        job_read = {j: sem("read_" + j) for j in names if not j.startswith("out")}
        q_high = [sem(f"q_high{i}") for i in range(ST)]
        k_high = sem("k_high")
        q_split = sem("q_split")
        k_split = sem("k_split")
        pool_step = sem("pool_step")
        parts_written = sem("parts_written")
        stack_ready = [sem(f"stack_ready{i}") for i in range(2)]
        v_ready = sem("v_ready")
        max_scored = sem("max_scored")
        max_taken = sem("max_taken")
        max_split = sem("max_split")
        max_sent = [sem(f"max_sent{i}") for i in range(2)]
        max_step = sem("max_step")
        scored = sem("scored")
        exp_done = sem("exp_done")
        weighted = sem("weighted")
        out_copied = sem("out_copied")
        rden_ready = sem("rden_ready")
        normed = sem("normed")
        added = sem("added")

        block = ctx.enter_context(nc.Block())

        def job_index(job):
            return (0 if job[4] == "a" else 1), int(job[5])

        @block.sync
        def _(sp):
            for b in range(2):
                sp.dma_start(x_res[:, ST * b:ST * b + ST, :], x_dram[b]).then_inc(x_first, 16)
                sp.dma_start(ctx_cur[:, b], ctx_dram[b]).then_inc(ctx_loaded[b], 16)
            for b in range(2, B):
                sp.dma_start(x_res[:, ST * b:ST * b + ST, :], x_dram[b]).then_inc(x_rest, 16)

            def write_parts(b, n):
                sp.wait_ge(q_split, 2 * b + 2)
                for part, n_parts, term, _ in Q_RUNS:
                    sp.dma_start(q_scr[bass.ds(b, 1)].rearrange("o (c p) t s -> p (o c) t s", p=P)[:, :, term:term + n_parts],
                                 q_part[:, n % 2, :, part:part + n_parts]).then_inc(parts_written, 16)
                sp.wait_ge(k_split, b + 1)
                for part, _, term, times in K_RUNS:
                    sp.dma_start(k_scr[bass.ds(b, 1)].rearrange("o p t s -> p (o t) s")[:, term:term + times],
                                 k_part[:, part:part + 1].to_broadcast([P, times, S])).then_inc(parts_written, 16)

            def read_stack(b, n, half):
                free = 16 * (b - 2) + 8 * half + 8
                if n >= 2 and not isinstance(b, int):
                    free = sp.snap(free)
                if half == 0:
                    sp.wait_ge(parts_written, 96 * b + 96)
                if n >= 2:
                    sp.wait_ge(scored, free)
                heads = slice(half * HALF * G, (half + 1) * HALF * G)
                kvs = slice(half * HALF, (half + 1) * HALF)
                sp.dma_start(q_stack[0:ROWS, n % 2, heads, :],
                             q_scr[bass.ds(b, 1)].rearrange("o (h d) t s -> (d t) (o h) s", d=D)[:, heads]).then_inc(stack_ready[half], 16)
                sp.dma_start(k_stack[0:ROWS, n % 2, kvs, :],
                             k_scr[bass.ds(b, 1)].rearrange("o (h d) t s -> (d t) (o h) s", d=D)[:, kvs]).then_inc(stack_ready[half], 16)

            def send_max(b, n, half):
                sp.wait_ge(job_read["max_a" if half == 0 else "max_b"], b + 1)
                sp.dma_start(q_stack[ROWS:ROWS_MAX, n % 2, half * HALF * G:(half + 1) * HALF * G, :],
                             max_rows[:]).then_inc(max_sent[half], 16)

            for b in range(2):
                write_parts(b, b)
                for half in range(2):
                    read_stack(b, b, half)
            send_max(0, 0, 0)

            def turn(b, n):
                send_max(b, n, 1)
                if n + 2 < B:
                    sp.wait_ge(job_done["key"], b + 1)
                    sp.wait_ge(v_ready, b + 1)
                    sp.dma_start(ctx_cur[:, n % 2], ctx_dram[bass.ds(b + 2, 1)].rearrange("o p t e -> p (o t) e")).then_inc(ctx_loaded[n % 2], 16)
                    write_parts(b + 2, n + 2)
                    read_stack(b + 2, n + 2, 0)
                if n + 1 < B:
                    send_max(b + 1, n + 1, 0)
                if n + 2 < B:
                    read_stack(b + 2, n + 2, 1)
                sp.dma_start(xg[bass.ds(b * ZERO_TILES * P, ZERO_TILES * P), :].rearrange("(p t) (f e) -> p (t f) e", p=P, f=2),
                             zero[:].unsqueeze(1).to_broadcast([P, 2 * ZERO_TILES, E // 2])).then_inc(cleared, 16)

            sp.wait_ge(zero_set, 1)
            each_batch(sp, turn)
            sp.wait_ge(cleared, 16 * B)

        @block.gpsimd
        def _(pool):
            for m in (ident, ident_bf):
                nc.gpsimd.memset(m[:], 0.0).then_inc(ident_set, 1)
            pool.wait_ge(ident_set, 2)
            for m in (ident, ident_bf):
                nc.gpsimd.affine_select(out=m[:], in_=m[:], compare_op=ALU.not_equal, fill=1.0, base=0, pattern=[[-1, P]],
                                        channel_multiplier=1).then_inc(ident_set, 1)
            nc.gpsimd.memset(zero[:], 0.0).then_inc(zero_set, 1)
            nc.gpsimd.memset(v_aug[:], 0.0).then_inc(ones_set, 1)
            pool.wait_ge(ones_set, 1)
            nc.gpsimd.memset(v_aug[:, :, :, :, D:D + 1], 1.0).then_inc(ones_set, 1)
            pool.wait_ge(ones_set, 2)
            nc.gpsimd.memset(k_stack[ROWS:ROWS_MAX], 1.0).then_inc(ones_set, 1)

            def split_queries(b, n, st):
                tokens = slice(st * P, (st + 1) * P)
                pool.wait_ge(job_read[f"query_{st}"], b + 1)
                if n >= 2:
                    pool.wait_ge(parts_written, 96 * b - 96)
                nc.gpsimd.tensor_tensor(q_part[:, n % 2, :, 1, tokens], q_rest[:], zero[:, 0:1].unsqueeze(2).to_broadcast([P, EC, P]), ALU.add).then_inc(pool_step, 1)
                pool.wait_ge(pool_step, 3 * b + (1, 3)[st])
                nc.gpsimd.tensor_tensor(q_part[:, n % 2, :, 2, tokens], q_rest[:], q_part[:, n % 2, :, 1, tokens], ALU.subtract).then_inc(q_split, 1)

            def split_keys(b, n):
                pool.wait_ge(job_read["key"], b + 1)
                if n >= 1:
                    pool.wait_ge(parts_written, 96 * b)
                nc.gpsimd.tensor_tensor(k_part[:, 1], k_rest[:], zero[:, 0:1].to_broadcast([P, S]), ALU.add).then_inc(pool_step, 1)
                pool.wait_ge(pool_step, 3 * b + 2)
                nc.gpsimd.tensor_tensor(k_part[:, 2], k_rest[:], k_part[:, 1], ALU.subtract).then_inc(k_split, 1)

            def values(b, n):
                pool.wait_ge(ctx_loaded[n % 2], 8 * (b - n % 2) + 16)
                if n >= 2:
                    pool.wait_ge(weighted, 8 * (b - 1))
                for tc in range(ST):
                    now = ctx_cur[:, n % 2, tc].rearrange("p (k d) -> p k d", d=D)
                    last = nc.gpsimd.tensor_tensor(v_aug[:, n % 2, tc, :, 0:D], now, zero[:, 0:1].unsqueeze(2).to_broadcast([P, KV, D]), ALU.add)
                last.then_inc(v_ready, 1)

            def add_out(b, n, half, st):
                k = 2 * half + st
                pool.wait_ge(normed, 4 * b + k + 1)
                cols = slice(half * HALF * G * D, (half + 1) * HALF * G * D)
                row = x_res[:, bass.ds(ST * b + st, 1), cols].rearrange("p o c -> p (o c)")
                nc.gpsimd.tensor_tensor(row, row, out_norm[:, st], ALU.add).then_inc(added, 1)

            pool.wait_ge(ones_set, 3)
            for b in range(2):
                split_queries(b, b, 0)
                split_keys(b, b)
                split_queries(b, b, 1)
            values(0, 0)

            def turn(b, n):
                if n + 2 < B:
                    split_queries(b + 2, n + 2, 0)
                    split_keys(b + 2, n + 2)
                    split_queries(b + 2, n + 2, 1)
                if n + 1 < B:
                    values(b + 1, n + 1)
                if n >= 1:
                    for st in range(ST):
                        add_out(b - 1, n - 1, 1, st)
                for st in range(ST):
                    add_out(b, n, 0, st)
                if n >= B - SETS:
                    s = n - (B - SETS)
                    g, u, d = shared_src
                    cols = slice(s * HID, (s + 1) * HID)
                    split_weights(nc, pool, sh[:, s], sl[:, s], stage, weight_pieces(g[:, cols], u[:, cols], d[cols, :]), s,
                                  high_loaded, stage_loaded, weights_split)

            each_batch(pool, turn)
            for st in range(ST):
                add_out(B - 1, B - 1, 1, st)

        @block.scalar
        def _(act):
            def query_high(b, n, st):
                act.wait_ge(job_done[f"query_{st}"], b + 1)
                if n >= 2:
                    act.wait_ge(parts_written, 96 * b - 96)
                nc.scalar.activation(q_part[:, n % 2, :, 0, st * P:(st + 1) * P], ps_job[:].rearrange("p (c s) -> p c s", s=P), ACT.Copy).then_inc(q_high[st], 1)

            def key_high(b, n):
                act.wait_ge(job_done["key"], b + 1)
                if n >= 1:
                    act.wait_ge(parts_written, 96 * b)
                nc.scalar.activation(k_part[:, 0], ps_job[:, 0:S], ACT.Copy).then_inc(k_high, 1)

            def job(slot, b, n):
                name, away = job_at(slot, n)
                if name in ("query_0", "query_1"):
                    query_high(b + away, n + away, int(name[-1]))
                if name == "key":
                    key_high(b + away, n + away)

            for b in range(2):
                query_high(b, b, 0)
                query_high(b, b, 1)
                key_high(b, b)

            def turn(b, n):
                for k in range(KV):
                    g, ng = 8 * b + k, 8 * n + k
                    if k % 2 == 1 and ng >= 3:
                        i = (k - 3) // 2
                        act.wait_ge(weighted, 8 * b + 2 * i + 2)
                        half, nb_away = ((i % 4) // 2, -1 if i < 0 else 0)
                        if n + nb_away >= 1:
                            act.wait_ge(job_done[f"out_{'ab'[half]}1"], b + nb_away)
                        nc.scalar.activation(out_t[:, half, 2 * (i % 2):2 * (i % 2) + 2, :], ps_out[:], ACT.Copy).then_inc(out_copied, 1)
                    for tc in range(ST):
                        u = 2 * g + tc
                        act.wait_ge(scored, u + 1)
                        if ng >= 2:
                            act.wait_ge(weighted, g - 1)
                        nc.scalar.activation(probs[:, k % 2, tc], ps_score[:, tc], ACT.Exp, scale=SCALE).then_inc(exp_done, 1)
                        job(2 * k + tc, b, n)

            each_batch(act, turn)
            act.wait_ge(weighted, KV * B)
            act.wait_ge(job_done["out_b1"], B - 1)
            nc.scalar.activation(out_t[:, 1, 2:4, :], ps_out[:], ACT.Copy).then_inc(out_copied, 1)

        @block.vector
        def _(dve):
            done = [0]

            def chain(ins):
                done[0] += 1
                ins.then_inc(ln_step, 1)
                dve.wait_ge(ln_step, done[0])

            def statistics(t0, t1):
                for t in range(t0, t1):
                    nc.vector.bn_stats(stats[:, t], x_res[:, t]).then_inc(ln_step, 1)
                    done[0] += 1
                dve.wait_ge(ln_step, done[0])
                for t in range(t0, t1):
                    nc.vector.bn_aggr(mean_var[:, t], stats[:, t]).then_inc(ln_step, 1)
                    done[0] += 1
                dve.wait_ge(ln_step, done[0])
                some = slice(t0, t1)
                chain(nc.vector.tensor_copy(var[:, some], mean_var[:, some, 1]))
                rsqrt_newton(nc.vector, chain, rstd[:, some], var[:, some], newton_1[:, some], newton_2[:, some])

            def normalize(b, n, st):
                if n >= 1:
                    dve.wait_ge(job_done[f"query_{st}"], b)
                t = ST * b + st
                nc.vector.tensor_scalar(xn[:, st], x_res[:, bass.ds(t, 1), :].rearrange("p o c -> p (o c)"), mean_var[:, bass.ds(t, 1), 0],
                                        rstd[:, bass.ds(t, 1)], ALU.subtract, ALU.mult).then_inc(xn_ready[st], 1)

            def query_rest(b, n, st):
                dve.wait_ge(q_high[st], b + 1)
                if n >= 1 or st == 1:
                    dve.wait_ge(q_split, 2 * b + st)
                nc.vector.tensor_tensor(q_rest[:], ps_job[:].rearrange("p (c s) -> p c s", s=P), q_part[:, n % 2, :, 0, st * P:(st + 1) * P],
                                        ALU.subtract).then_inc(job_read[f"query_{st}"], 1)

            def key_rest(b, n):
                dve.wait_ge(k_high, b + 1)
                if n >= 1:
                    dve.wait_ge(k_split, b)
                nc.vector.tensor_tensor(k_rest[:], ps_job[:, 0:S], k_part[:, 0], ALU.subtract).then_inc(job_read["key"], 1)

            def take_max(b, n, k, st):
                for pair in range(2):
                    i = 32 * b + 4 * k + 2 * st + pair
                    dve.wait_ge(max_scored, i + 1)
                    h = G * (k % HALF) + 2 * pair
                    nc.vector.tensor_reduce(maxes[:, k // HALF, st, h:h + 2], ps_max[:, pair], AX_X, ALU.max).then_inc(max_taken, 1)

            def split_max(b, n, half):
                dve.wait_ge(max_taken, 32 * b + 16 * half + 16)
                if half == 1:
                    dve.wait_ge(job_done["max_a"], b + 1)
                elif n >= 1:
                    dve.wait_ge(job_done["max_b"], b)
                nc.vector.tensor_scalar(max_part[:, :, 0], maxes[:, half], -1.0, None, ALU.mult).then_inc(max_step, 1)
                dve.wait_ge(max_step, 2 * b + half + 1)
                nc.vector.scalar_tensor_tensor(out=max_part[:, :, 1], in0=maxes[:, half], scalar=-1.0, in1=max_part[:, :, 0],
                                               op0=ALU.mult, op1=ALU.subtract).then_inc(max_split, 1)

            def max_to_rows(b, n, half):
                name = "max_" + "ab"[half]
                dve.wait_ge(job_done[name], b + 1)
                if half == 1:
                    dve.wait_ge(max_sent[0], 16 * b + 16)
                elif n >= 1:
                    dve.wait_ge(max_sent[1], 16 * b)
                nc.vector.tensor_copy(max_rows[:], ps_job_bf[0:2 * HALF * G, 0:S]).then_inc(job_read[name], 1)

            def normalize_out(b, n, name):
                half, st = job_index(name)
                i = 4 * b + 2 * half + st
                tile = ps_job[:].rearrange("p (h d) -> p h d", d=32)
                dve.wait_ge(job_done[name], b + 1)
                nc.vector.reciprocal(rden[:], tile[:, :, D]).then_inc(rden_ready, 1)
                dve.wait_ge(rden_ready, i + 1)
                if n >= 1 or half == 1:
                    dve.wait_ge(added, i - 1)
                nc.vector.tensor_tensor(out_norm[:, st].rearrange("p (h d) -> p h d", d=D), tile[:, :, 0:D],
                                        rden[:].unsqueeze(2).to_broadcast([P, HALF * G, D]), ALU.mult).then_inc(normed, 1)

            def job(slot, b, n):
                name, away = job_at(slot, n)
                if name is None:
                    return
                b, n = b + away, n + away
                if name.startswith("query"):
                    query_rest(b, n, int(name[-1]))
                elif name == "key":
                    key_rest(b, n)
                elif name.startswith("max"):
                    max_to_rows(b, n, "ab".index(name[-1]))
                else:
                    normalize_out(b, n, name)

            dve.wait_ge(x_first, 32)
            statistics(0, 2 * ST)
            for b in range(2):
                for st in range(ST):
                    normalize(b, b, st)
                    query_rest(b, b, st)
                key_rest(b, b)
            dve.wait_ge(x_rest, 16 * (B - 2))
            statistics(2 * ST, NT)
            for k in range(KV):
                for st in range(ST):
                    take_max(0, 0, k, st)
                if k == HALF - 1:
                    split_max(0, 0, 0)
                if k == HALF:
                    max_to_rows(0, 0, 0)
            split_max(0, 0, 1)

            def turn(b, n):
                for k in range(KV):
                    if n + 2 < B and k < ST:
                        normalize(b + 2, n + 2, k)
                    for tc in range(ST):
                        if n + 1 < B:
                            take_max(b + 1, n + 1, k, tc)
                        job(2 * k + tc, b, n)
                    if n + 1 < B and k % HALF == HALF - 1:
                        split_max(b + 1, n + 1, k // HALF)

            each_batch(dve, turn)
            for st in range(ST):
                normalize_out(B - 1, B - 1, f"out_b{st}")

        @block.tensor
        def _(pe):
            def bank_free(job, b):
                if job.startswith("out"):
                    half, st = job_index(job)
                    pe.wait_ge(normed, 4 * b + 2 * half + st + 1)
                else:
                    pe.wait_ge(job_read[job], b + 1)

            def do_job(name, b, n):
                if name.startswith("query"):
                    st = int(name[-1])
                    pe.wait_ge(xn_ready[st], b + 1)
                    for c in range(EC):
                        last = nc.tensor.transpose(ps_job[:, c * P:(c + 1) * P], xn[:, st, c * P:(c + 1) * P], ident[:])
                elif name == "key":
                    pe.wait_ge(ctx_loaded[n % 2], 8 * (b - n % 2) + 16)
                    for st in range(ST):
                        last = nc.tensor.transpose(ps_job[:, st * P:(st + 1) * P], ctx_cur[:, n % 2, st], ident[:])
                elif name.startswith("max"):
                    half = "ab".index(name[-1])
                    pe.wait_ge(max_split, 2 * b + half + 1)
                    for st in range(ST):
                        last = nc.tensor.transpose(ps_job_bf[0:2 * HALF * G, st * P:(st + 1) * P],
                                                   max_part[:, st].rearrange("p a h -> p (a h)"), ident_bf[:])
                else:
                    half, st = job_index(name)
                    pe.wait_ge(out_copied, 4 * b + 2 * half + 2)
                    for kv in range(HALF):
                        last = nc.tensor.transpose(ps_job[:, kv * P:(kv + 1) * P], out_t[:, half, kv, st * P:(st + 1) * P], ident[:])
                last.then_inc(job_done[name], 1)

            def job(slot, b, n):
                name, away = job_at(slot, n)
                if name is None:
                    return
                before, b_away = job_before(slot, n)
                bank_free(before, b + b_away)
                do_job(name, b + away, n + away)

            def score_for_max(b, n, k, st, pairs=(0, 1)):
                if st == 0 and k % HALF == 0 and 0 in pairs:
                    pe.wait_ge(stack_ready[k // HALF], 32 * b + 32)
                for pair in pairs:
                    i, ni = 32 * b + 4 * k + 2 * st + pair, 32 * n + 4 * k + 2 * st + pair
                    if ni >= 2:
                        pe.wait_ge(max_taken, i - 1)
                    for j in range(2):
                        last = nc.tensor.matmul(ps_max[:, pair, j], q_stack[0:ROWS, n % 2, G * k + 2 * pair + j, st * P:(st + 1) * P],
                                                k_stack[0:ROWS, n % 2, k, :], start=True, stop=True)
                    last.then_inc(max_scored, 1)

            def score(b, n, k, tc):
                u, nu = 16 * b + 2 * k + tc, 16 * n + 2 * k + tc
                if tc == 0 and k % HALF == 0:
                    pe.wait_ge(max_sent[k // HALF], 16 * b + 16)
                if nu >= 2:
                    pe.wait_ge(exp_done, u - 1)
                for pair in range(2):
                    last = nc.tensor.matmul(ps_score[:, tc, 2 * pair:2 * pair + 2, :], k_stack[:, n % 2, k, tc * P:(tc + 1) * P],
                                            q_stack[:, n % 2, G * k + 2 * pair:G * k + 2 * pair + 2, :], start=True, stop=True)
                last.then_inc(scored, 1)

            def weigh(b, n, k, tc):
                pe.wait_ge(exp_done, 16 * b + 2 * k + tc + 1)
                if k == 0 and tc == 0:
                    pe.wait_ge(v_ready, b + 1)
                if k % 2 == 0 and tc == 0 and 8 * n + k >= 2:
                    pe.wait_ge(out_copied, 4 * b + k // 2)
                for j in range(G):
                    last = nc.tensor.matmul(ps_out[32 * j:32 * j + 32, k % 2, :], v_aug[:, n % 2, tc, k, :], probs[:, k % 2, tc, j, :],
                                            start=(tc == 0), stop=(tc == ST - 1))
                if tc == ST - 1:
                    last.then_inc(weighted, 1)

            pe.wait_ge(ident_set, 4)
            before = None
            for name, b in FIRST_JOBS[:-1]:
                if before:
                    bank_free(*before)
                do_job(name, b, b)
                before = (name, b)
            pe.wait_ge(ones_set, 3)
            for k in range(KV):
                for st in range(ST):
                    score_for_max(0, 0, k, st)
                if k == HALF:
                    bank_free(*before)
                    do_job("max_a", 0, 0)

            def turn(b, n):
                for k in range(KV):
                    for tc in range(ST):
                        score(b, n, k, tc)
                        if n + 1 < B:
                            score_for_max(b + 1, n + 1, k, tc, (0,))
                        if k >= 1:
                            weigh(b, n, k - 1, tc)
                        elif n >= 1:
                            weigh(b - 1, n - 1, KV - 1, tc)
                        if n + 1 < B:
                            score_for_max(b + 1, n + 1, k, tc, (1,))
                        job(2 * k + tc, b, n)

            each_batch(pe, turn)
            for tc in range(ST):
                weigh(B - 1, B - 1, KV - 1, tc)
            for name, b in LAST_JOBS:
                bank_free(*{"out_b0": ("out_a1", B - 1), "out_b1": ("out_b0", B - 1)}[name])
                do_job(name, b, b)

def weight_pieces(gate, up, down):
    return (
        (0, P, EC, HID, gate.rearrange("(c p) j -> p c j", p=P)),
        (UP_AT, P, EC, HID, up.rearrange("(c p) j -> p c j", p=P)),
        (DOWN_AT, P, HC - 1, E, down[0:(HC - 1) * P].rearrange("(c p) j -> p c j", p=P)),
        (DOWN_AT + (HC - 1) * E, HID_TAIL, 1, E, down[(HC - 1) * P:HID].rearrange("(c p) j -> p c j", p=HID_TAIL)),
    )


def split_weights(nc, pool, high, low, stage, pieces, j, high_loaded, stage_loaded, split):
    n = len(pieces)

    def part(buffer, k):
        col, rows, chunks, width, _ = pieces[k]
        return buffer[0:rows, col:col + chunks * width].rearrange("p (c j) -> p c j", j=width)

    def staged(k):
        _, rows, chunks, width, _ = pieces[k]
        return stage[0:rows, k % 2, 0:chunks * width].rearrange("p (c j) -> p c j", j=width)

    for k in range(n):
        pool.dma_start(part(high, k), pieces[k][4]).then_inc(high_loaded, 16)
        if k < 2:
            pool.dma_start(staged(k), pieces[k][4]).then_inc(stage_loaded[k], 16)
    pool.wait_ge(high_loaded, 16 * n * j + 16 * n)
    for k in range(n):
        pool.wait_ge(stage_loaded[k % 2], 8 * n * j + 16 * (k // 2) + 16)
        nc.gpsimd.tensor_tensor(part(low, k), staged(k), part(high, k).bitcast(F32), ALU.subtract).then_inc(split, 1)
        pool.wait_ge(split, n * j + k + 1)
        if k + 2 < n:
            pool.dma_start(staged(k + 2), pieces[k + 2][4]).then_inc(stage_loaded[k % 2], 16)


def gating(nc, x_res, ident, gate_w, ln2, weights_out, slots, plan):
    mean, rstd = ln2
    with ExitStack() as ctx:
        def sb(name, shape, dt=F32):
            return ctx.enter_context(nc.sbuf_tensor(name, shape, dt))

        def psum(name, shape, dt=F32):
            return ctx.enter_context(nc.psum_tensor(name, shape, dt))

        def sem(name):
            return ctx.enter_context(nc.semaphore(name))

        GT = 4
        stats = sb("stats2", [P, NT, 6])
        mv = sb("mv2", [P, NT, 2])
        var = sb("var2", [P, NT])
        n1, n2 = sb("n1_2", [P, NT]), sb("n2_2", [P, NT])
        xn = sb("xn2", [P, 2, E])
        xt = sb("xt2", [P, 2, EC, GT * P])
        gw = sb("gw", [P, EC, NE])
        lt = sb("lt", [NE, 2, GT * P])
        logits = sb("logits", [P, NT, NE])
        best = sb("best", [P, NT, NE])
        index = sb("index", [P, NT, NE], U32)
        index_f = sb("index_f", [P, TOP, NT])
        row_max = sb("row_max", [P, NT])
        row_sum = sb("row_sum", [P, NT])
        expert_no = sb("expert_no", [P, NE])
        chosen = [sb(f"chosen{k}", [P, NT, NE]) for k in range(TOP)]
        mask = sb("mask", [P, NT, NE], BF16)
        before = sb("before", [P, P], BF16)
        ones = sb("ones", [P, P], BF16)
        scan = [sb(f"scan{i}", [P, NT, NE]) for i in range(2)]
        place = sb("place", [P, NT, NE])
        picked = sb("picked", [P, NT, NE])
        tiles_i = sb("tiles_i", [P, NE], I32)
        tiles = sb("tiles", [P, NE])
        ends = [sb(f"ends{i}", [P, NE]) for i in range(2)]
        tile_no = sb("tile_no", [1, SLOT_TILES])
        passed = sb("passed", [1, SLOT_TILES, NE])
        expert_of = sb("expert_of", [1, SLOT_TILES])
        expert_i = sb("expert_i", [1, SLOT_TILES], I32)

        ps_t = psum("ps_t", [P, 2, EC * P])
        ps_l = psum("ps_l", [NE, GT * P])
        ps_r = psum("ps_r", [P, NT, NE])
        ps_c = psum("ps_c", [P, 2, NT * NE])

        gw_loaded, const_set = sem("gw_loaded"), sem("const_set")
        step, xn_ready, turned, copied = sem("g_step"), sem("g_xn"), sem("g_turned"), sem("g_copied")
        projected, lt_ready, back, probs_exp, mask_ready, counted = (sem("g_" + s) for s in ("proj", "lt", "back", "exp", "mask", "count"))
        max_sub = sem("g_maxsub")
        block = ctx.enter_context(nc.Block())

        @block.sync
        def _(sp):
            sp.dma_start(gw[:], gate_w.rearrange("(c p) e -> p c e", p=P)).then_inc(gw_loaded, 16)

        @block.gpsimd
        def _(pool):
            nc.gpsimd.memset(ones[:], 1.0).then_inc(const_set, 1)
            pool.wait_ge(const_set, 1)
            nc.gpsimd.affine_select(out=before[:], in_=ones[:], compare_op=ALU.is_gt, fill=0.0, base=0,
                                    pattern=[[1, P]], channel_multiplier=-1).then_inc(const_set, 1)
            pool.wait_ge(const_set, 2)
            nc.gpsimd.iota(expert_no[:], pattern=[[1, NE]], base=0, channel_multiplier=0, allow_small_or_imprecise_dtypes=True).then_inc(const_set, 1)
            pool.wait_ge(const_set, 3)
            nc.gpsimd.iota(tile_no[:], pattern=[[1, SLOT_TILES]], base=0, channel_multiplier=0, allow_small_or_imprecise_dtypes=True).then_inc(const_set, 1)

        @block.scalar
        def _(act):
            def copy_tile(t, nt):
                act.wait_ge(turned, t + 1)
                nc.scalar.activation(xt[:, (nt // GT) % 2, :, (nt % GT) * P:(nt % GT + 1) * P], ps_t[:, nt % 2].rearrange("p (c s) -> p c s", s=P),
                                     ACT.Copy).then_inc(copied, 1)

            for t in range(NT):
                copy_tile(t, t)
                if t % GT == GT - 1:
                    g = t // GT
                    act.wait_ge(projected, g + 1)
                    nc.scalar.activation(lt[:, g % 2], ps_l[:], ACT.Copy).then_inc(lt_ready, 1)
            act.wait_ge(max_sub, 1)
            nc.scalar.activation(logits[:], logits[:], ACT.Exp).then_inc(probs_exp, 1)

        @block.tensor
        def _(pe):
            pe.wait_ge(gw_loaded, 16)

            def project(g):
                pe.wait_ge(copied, GT * g + GT)
                if g >= 1:
                    pe.wait_ge(lt_ready, g)
                for c in range(EC):
                    last = nc.tensor.matmul(ps_l[:], gw[:, c], xt[:, g % 2, c], start=(c == 0), stop=(c == EC - 1))
                last.then_inc(projected, 1)

            def turn_back(g):
                pe.wait_ge(lt_ready, g + 1)
                for j in range(GT):
                    last = nc.tensor.transpose(ps_r[:, GT * g + j], lt[:, g % 2, j * P:(j + 1) * P], ident[0:NE, 0:NE])
                last.then_inc(back, 1)

            for t in range(NT):
                pe.wait_ge(xn_ready, t + 1)
                if t >= 2:
                    pe.wait_ge(copied, t - 1)
                for c in range(EC):
                    last = nc.tensor.transpose(ps_t[:, t % 2, c * P:(c + 1) * P], xn[:, t % 2, c * P:(c + 1) * P], ident[:])
                last.then_inc(turned, 1)
                if t % GT == 1 and t > GT:
                    turn_back(t // GT - 1)
                if t % GT == 0 and t >= GT:
                    project(t // GT - 1)
            project(NT // GT - 1)
            turn_back(NT // GT - 1)
            pe.wait_ge(mask_ready, 1)
            pe.wait_ge(const_set, 2)
            nc.tensor.matmul(ps_c[:, 0], before[:], mask[:].rearrange("p t e -> p (t e)"), start=True, stop=True)
            nc.tensor.matmul(ps_c[:, 1], ones[:], mask[:].rearrange("p t e -> p (t e)"), start=True, stop=True).then_inc(counted, 1)

        @block.vector
        def _(dve):
            done = [0]

            def chain(ins):
                done[0] += 1
                ins.then_inc(step, 1)
                dve.wait_ge(step, done[0])

            for t in range(NT):
                nc.vector.bn_stats(stats[:, t], x_res[:, t]).then_inc(step, 1)
            done[0] += NT
            dve.wait_ge(step, done[0])
            for t in range(NT):
                nc.vector.bn_aggr(mv[:, t], stats[:, t]).then_inc(step, 1)
            done[0] += NT
            dve.wait_ge(step, done[0])
            nc.vector.tensor_copy(mean[:], mv[:, :, 0]).then_inc(step, 1)
            done[0] += 1
            chain(nc.vector.tensor_copy(var[:], mv[:, :, 1]))
            rsqrt_newton(nc.vector, chain, rstd[:], var[:], n1[:], n2[:])
            for t in range(NT):
                if t >= 2:
                    dve.wait_ge(turned, t - 1)
                nc.vector.tensor_scalar(xn[:, t % 2], x_res[:, t], mean[:, t:t + 1], rstd[:, t:t + 1], ALU.subtract, ALU.mult).then_inc(xn_ready, 1)
            dve.wait_ge(back, NT // GT)
            chain(nc.vector.tensor_reduce(row_max[:], ps_r[:], AX_X, ALU.max))
            nc.vector.tensor_tensor(logits[:], ps_r[:], row_max[:].unsqueeze(2).to_broadcast([P, NT, NE]), ALU.subtract).then_inc(max_sub, 1)
            dve.wait_ge(probs_exp, 1)
            chain(nc.vector.tensor_reduce(row_sum[:], logits[:], AX_X, ALU.add))
            chain(nc.vector.reciprocal(row_sum[:], row_sum[:]))
            chain(nc.vector.tensor_tensor(logits[:], logits[:], row_sum[:].unsqueeze(2).to_broadcast([P, NT, NE]), ALU.mult))
            for t in range(NT):
                nc.vector.max(best[:, t], logits[:, t]).then_inc(step, 1)
            done[0] += NT
            dve.wait_ge(step, done[0])
            for t in range(NT):
                nc.vector.max_index(index[:, t], best[:, t], logits[:, t]).then_inc(step, 1)
            done[0] += NT
            dve.wait_ge(step, done[0])
            nc.vector.tensor_copy(weights_out[:], best[:, :, 0:TOP])
            chain(nc.vector.tensor_copy(index_f[:], index[:, :, 0:TOP].rearrange("p t k -> p k t")))
            dve.wait_ge(const_set, 4)
            for k in range(TOP):
                chain(nc.vector.tensor_tensor(chosen[k][:], expert_no[:].unsqueeze(1).to_broadcast([P, NT, NE]),
                                              index_f[:, k].unsqueeze(2).to_broadcast([P, NT, NE]), ALU.is_equal))
            nc.vector.tensor_tensor(mask[:], chosen[0][:], chosen[1][:], ALU.add).then_inc(mask_ready, 1)
            dve.wait_ge(counted, 1)
            chain(nc.vector.tensor_copy(scan[0][:], ps_c[:, 1].rearrange("p (t e) -> p t e", e=NE)))
            away, src = 1, 0
            while away < NT:
                nc.vector.tensor_copy(scan[1 - src][:, 0:away], scan[src][:, 0:away]).then_inc(step, 1)
                done[0] += 1
                chain(nc.vector.tensor_tensor(scan[1 - src][:, away:NT], scan[src][:, away:NT], scan[src][:, 0:NT - away], ALU.add))
                away, src = 2 * away, 1 - src
            total = scan[src]
            chain(nc.vector.tensor_tensor(place[:], total[:], ps_c[:, 1].rearrange("p (t e) -> p t e", e=NE), ALU.subtract))
            chain(nc.vector.tensor_tensor(place[:], place[:], ps_c[:, 0].rearrange("p (t e) -> p t e", e=NE), ALU.add))
            chain(nc.vector.tensor_scalar(tiles_i[:], total[:, NT - 1], float(P - 1), None, ALU.add))
            chain(nc.vector.tensor_scalar(tiles_i[:], tiles_i[:], P.bit_length() - 1, None, ALU.logical_shift_right))
            chain(nc.vector.tensor_copy(tiles[:], tiles_i[:]))
            chain(nc.vector.tensor_copy(ends[0][:], tiles[:]))
            away, src = 1, 0
            while away < NE:
                nc.vector.tensor_copy(ends[1 - src][:, 0:away], ends[src][:, 0:away]).then_inc(step, 1)
                done[0] += 1
                chain(nc.vector.tensor_tensor(ends[1 - src][:, away:NE], ends[src][:, away:NE], ends[src][:, 0:NE - away], ALU.add))
                away, src = 2 * away, 1 - src
            end = ends[src]
            chain(nc.vector.tensor_tensor(tiles[:], end[:], tiles[:], ALU.subtract))
            chain(nc.vector.tensor_scalar(tiles[:], tiles[:], float(P), None, ALU.mult))
            chain(nc.vector.tensor_tensor(place[:], place[:], tiles[:].unsqueeze(1).to_broadcast([P, NT, NE]), ALU.add))
            for k in range(TOP):
                chain(nc.vector.tensor_tensor(picked[:], place[:], chosen[k][:], ALU.mult))
                chain(nc.vector.tensor_reduce(index_f[:, k], picked[:], AX_X, ALU.add))
            chain(nc.vector.tensor_copy(slots[:], index_f[:]))
            chain(nc.vector.tensor_tensor(passed[:], tile_no[:].unsqueeze(2).to_broadcast([1, SLOT_TILES, NE]),
                                          end[0:1].unsqueeze(1).to_broadcast([1, SLOT_TILES, NE]), ALU.is_ge))
            chain(nc.vector.tensor_reduce(expert_of[:], passed[:], AX_X, ALU.add))
            chain(nc.vector.tensor_scalar(expert_i[:], expert_of[:], float(NE - 1), None, ALU.min))
            chain(nc.vector.tensor_scalar(plan[:, 0, 0:SLOT_TILES], expert_i[:], 1.0, None, ALU.add))
            chain(nc.vector.tensor_scalar(plan[:, 1, 0:SLOT_TILES], expert_i[:], 1, None, ALU.bitwise_and))
            chain(nc.vector.tensor_copy(plan[:, 2, 0:NE], end[0:1]))


def feed_forward(nc, tiles, routed, x_res, ident, ln2, shared_w, slots, plan, xg, y, out, weights_out, expert_w):
    mean, rstd = ln2
    sh, sl = shared_w
    t_first, t_n = tiles
    units = SETS * t_n
    r_n = SLOT_TILES if routed else 0
    tag = "a" if routed else "b"
    with ExitStack() as ctx:
        def sb(name, shape, dt=F32):
            return ctx.enter_context(nc.sbuf_tensor(name + tag, shape, dt))

        def psum(name, shape, dt=F32):
            return ctx.enter_context(nc.psum_tensor(name + tag, shape, dt))

        def sem(name):
            return ctx.enter_context(nc.semaphore(name + tag))

        x_in = sb("x_in", [P, E])
        x_high, x_low = sb("x_high", [P, EC, P], F32R), sb("x_low", [P, EC, P], F32R)
        gated = sb("gated", [P, HID])
        hidden = sb("hidden", [P, HC * P])
        h_high, h_low = sb("h_high", [P, HC, P], F32R), sb("h_low", [P, HC, P], F32R)
        if routed:
            w_high, w_low = sb("w_high", [P, 2, W_COLS], F32R), sb("w_low", [P, 2, W_COLS], F32R)
            stage = sb("stage", [P, 2, UP_AT])
            to_sort = sb("to_sort", [P, 2, E])
            token = sb("token", [P, 1])
            y_out = sb("y_out", [P, E])
        else:
            y_in = sb("y_in", [P, 2, TOP, E])
            result = sb("result", [P, 2, E])

        ps_x, ps_g, ps_u = psum("ps_x", [P, EC, P]), psum("ps_g", [P, 512]), psum("ps_u", [P, 512])
        ps_h, ps_y = psum("ps_h", [P, HC, P]), psum("ps_y", [P, E])

        x_normed, x_loaded = sem("x_normed"), sem("x_loaded")
        x_turned, x_high_ready, x_split = sem("x_turned"), sem("x_high_ready"), sem("x_split")
        up_done, silu_done, hidden_ready = sem("up_done"), sem("silu_done"), sem("hidden_ready")
        h_turned, h_high_ready, h_split = sem("h_turned"), sem("h_high_ready"), sem("h_split")
        down_done, y_read = sem("down_done"), sem("y_read")
        pad_set = sem("pad_set")
        if routed:
            sort_ready, sorted_ = sem("sort_ready"), [sem(f"sorted{i}") for i in range(2)]
            high_loaded, stage_loaded, weights_split = sem("high_loaded"), [sem(f"stage_loaded{i}") for i in range(2)], sem("weights_split")
            y_stored, buffer_free = sem("y_stored"), sem("buffer_free")
        else:
            y_loaded = [sem(f"y_loaded{i}") for i in range(2)]
            part_ready, result_ready, stored = sem("part_ready"), sem("result_ready"), [sem(f"stored{i}") for i in range(2)]
        block = ctx.enter_context(nc.Block())

        @block.sync
        def _(sp):
            if routed:
                for par in range(2):
                    sp.wait_ge(sorted_[par], 16 * TOP * NT // 2)

                def load(i):
                    sp.wait_ge(x_turned, t_n + i)
                    sp.dma_start(x_in[:], xg[bass.ds(i * P, P), :]).then_inc(x_loaded, 16)

                def store(i):
                    sp.wait_ge(y_read, t_n + i + 1)
                    sp.dma_start(y[bass.ds(i * P, P), :], y_out[:]).then_inc(y_stored, 16)

                load(0)
                load(1)
                with sp.Fori(0, r_n - 2) as i:
                    load(i + 2)
                    store(i)
                store(r_n - 2)
                store(r_n - 1)
                sp.wait_ge(y_stored, 16 * r_n)
            else:
                def store(k, par, t):
                    sp.wait_ge(result_ready, k + 1)
                    sp.dma_start(out[bass.ds(t * P, P), :], result[:, par]).then_inc(stored[par], 16)

                with sp.Fori(0, t_n) as m:
                    store(2 * m, 0, m)
                    store(2 * m + 1, 1, m + t_first)
                for par in range(2):
                    sp.wait_ge(stored[par], 16 * t_n)

        @block.gpsimd
        def _(pool):
            nc.gpsimd.memset(hidden[:, HID:], 0.0).then_inc(pad_set, 1)
            if routed:
                pool.wait_ge(pad_set, 1)
                nc.gpsimd.memset(token[:], 0.0).then_inc(pad_set, 1)
                pool.wait_ge(pad_set, 2)

                def scatter(t, par):
                    pool.wait_ge(sort_ready, t + 1)
                    for k in range(TOP):
                        pool.indirect_dma_start(out=xg[:, :], out_offset=bass.IndirectOffsetOnAxis(ap=slots[:, k, t:t + 1], axis=0),
                                                in_=to_sort[:, par], in_offset=None).then_inc(sorted_[par], 16)

                for t in range(NT):
                    scatter(t, t % 2)

                g, u, d = expert_w
                for e in range(NE):
                    if e >= 2:
                        end = pool.value_load(plan[0:1, 2, e - 2:e - 1], min_val=0, max_val=SLOT_TILES)
                        pool.wait_ge(down_done, end + units)
                        nc.gpsimd.tensor_tensor(token[:], token[:], token[:], ALU.add).then_inc(buffer_free, 1)
                        pool.wait_ge(buffer_free, e - 1)
                    split_weights(nc, pool, w_high[:, e % 2], w_low[:, e % 2], stage, weight_pieces(g[e], u[e], d[e]), e,
                                  high_loaded, stage_loaded, weights_split)

            else:
                def gather(k, nk, par, t):
                    if nk >= 2:
                        pool.wait_ge(result_ready, k - 1)
                    for j in range(TOP):
                        pool.indirect_dma_start(out=y_in[:, par, j], out_offset=None, in_=y[:, :],
                                                in_offset=bass.IndirectOffsetOnAxis(ap=slots[:, j, t:t + 1], axis=0)).then_inc(y_loaded[par], 16)

                gather(0, 0, 0, 0)
                gather(1, 1, 1, t_first)
                for m in range(1, t_n):
                    gather(2 * m, 2, 0, m)
                    gather(2 * m + 1, 3, 1, m + t_first)

        @block.scalar
        def _(act):
            def x_part(a):
                act.wait_ge(x_turned, a + 1)
                nc.scalar.activation(x_high[:], ps_x[:], ACT.Copy).then_inc(x_high_ready, 1)

            def silu(q):
                act.wait_ge(up_done, q + 1)
                nc.scalar.activation(gated[:], ps_g[:, 0:HID], ACT.Silu).then_inc(silu_done, 1)

            def h_part(q):
                act.wait_ge(h_turned, q + 1)
                nc.scalar.activation(h_high[:], ps_h[:], ACT.Copy).then_inc(h_high_ready, 1)

            def shared_tile(m, last):
                silu(2 * m)
                h_part(2 * m)
                silu(2 * m + 1)
                if not last:
                    x_part(m + 1)
                h_part(2 * m + 1)

            x_part(0)
            with act.Fori(0, t_n - 1) as m:
                shared_tile(m, False)
            shared_tile(t_n - 1, not routed)
            if routed:
                with act.Fori(0, r_n - 1) as i:
                    silu(units + i)
                    x_part(t_n + i + 1)
                    h_part(units + i)
                silu(units + r_n - 1)
                h_part(units + r_n - 1)

        @block.vector
        def _(dve):
            def normalize(out_ap, t):
                return nc.vector.tensor_scalar(out_ap, x_res[:, bass.ds(t, 1), :].rearrange("p o c -> p (o c)"), mean[:, bass.ds(t, 1)],
                                               rstd[:, bass.ds(t, 1)], ALU.subtract, ALU.mult)

            def x_norm(m, nm):
                if nm >= 1:
                    dve.wait_ge(x_turned, m)
                normalize(x_in[:], m + t_first).then_inc(x_normed, 1)

            def x_part(a):
                dve.wait_ge(x_high_ready, a + 1)
                nc.vector.tensor_tensor(x_low[:], ps_x[:], x_high[:].bitcast(F32), ALU.subtract).then_inc(x_split, 1)

            def hide(q):
                dve.wait_ge(silu_done, q + 1)
                nc.vector.tensor_tensor(hidden[:, 0:HID], ps_u[:, 0:HID], gated[:], ALU.mult).then_inc(hidden_ready, 1)

            def h_part(q):
                dve.wait_ge(h_high_ready, q + 1)
                nc.vector.tensor_tensor(h_low[:], ps_h[:], h_high[:].bitcast(F32), ALU.subtract).then_inc(h_split, 1)

            def to_scatter(m, nm, k):
                if not routed or nm >= NT // 4:
                    return
                t, nt, par = 4 * m + k, 4 * nm + k, k % 2
                if nt >= 2:
                    dve.wait_ge(sorted_[par], 16 * (t - par))
                normalize(to_sort[:, par], t).then_inc(sort_ready, 1)

            def add_shared(m):
                dve.wait_ge(down_done, 2 * m + 2)
                row = x_res[:, bass.ds(m + t_first, 1), :].rearrange("p o c -> p (o c)")
                nc.vector.tensor_tensor(row, row, ps_y[:], ALU.add).then_inc(y_read, 1)

            def combine(k, nk, par, m, t):
                if routed:
                    return
                dve.wait_ge(y_loaded[par], 32 * m + 32)
                if nk >= 2:
                    dve.wait_ge(stored[par], 16 * m)
                row = x_res[:, bass.ds(t, 1), :].rearrange("p o c -> p (o c)")
                nc.vector.scalar_tensor_tensor(out=result[:, par], in0=y_in[:, par, 0], scalar=weights_out[:, bass.ds(t, 1), 0], in1=row,
                                               op0=ALU.mult, op1=ALU.add).then_inc(part_ready, 1)
                dve.wait_ge(part_ready, k + 1)
                nc.vector.scalar_tensor_tensor(out=result[:, par], in0=y_in[:, par, 1], scalar=weights_out[:, bass.ds(t, 1), 1], in1=result[:, par],
                                               op0=ALU.mult, op1=ALU.add).then_inc(result_ready, 1)

            def shared_tile(m, nm):
                last = nm == t_n - 1
                hide(2 * m)
                to_scatter(m, nm, 0)
                if not last:
                    x_norm(m + 1, 1)
                if nm >= 1:
                    add_shared(m - 1)
                h_part(2 * m)
                to_scatter(m, nm, 1)
                if nm >= 1 and not routed:
                    dve.wait_ge(y_read, m)
                    combine(2 * m - 1, nm, 1, m - 1, m - 1 + t_first)
                hide(2 * m + 1)
                to_scatter(m, nm, 2)
                if routed or not last:
                    x_part(m + 1)
                h_part(2 * m + 1)
                to_scatter(m, nm, 3)
                combine(2 * m, 2 * nm, 0, m, m)

            x_norm(0, 0)
            x_part(0)
            shared_tile(0, 0)
            if routed:
                with dve.Fori(1, NT // 4) as m:
                    shared_tile(m, 1)
                with dve.Fori(NT // 4, t_n - 1) as m:
                    shared_tile(m, NT // 4)
            else:
                shared_tile(1, 1)
                with dve.Fori(2, t_n - 1) as m:
                    shared_tile(m, 2)
            shared_tile(t_n - 1, t_n - 1)
            if routed:
                def copy_y(i, ni):
                    dve.wait_ge(down_done, units + i + 1)
                    if ni >= 1:
                        dve.wait_ge(y_stored, 16 * i)
                    nc.vector.tensor_copy(y_out[:], ps_y[:]).then_inc(y_read, 1)

                hide(units)
                x_part(t_n + 1)
                add_shared(t_n - 1)
                h_part(units)
                hide(units + 1)
                x_part(t_n + 2)
                copy_y(0, 0)
                h_part(units + 1)
                with dve.Fori(2, r_n - 1) as i:
                    hide(units + i)
                    x_part(t_n + i + 1)
                    copy_y(i - 1, 1)
                    h_part(units + i)
                hide(units + r_n - 1)
                copy_y(r_n - 2, 1)
                h_part(units + r_n - 1)
                copy_y(r_n - 1, 1)
            else:
                add_shared(t_n - 1)
                dve.wait_ge(y_read, t_n)
                combine(2 * t_n - 1, 2, 1, t_n - 1, t_n - 1 + t_first)

        @block.tensor
        def _(pe):
            def turn_x(a, na):
                if na >= 1:
                    pe.wait_ge(x_split, a)
                for c in range(EC):
                    last = nc.tensor.transpose(ps_x[:, c], x_in[:, c * P:(c + 1) * P], ident[:])
                last.then_inc(x_turned, 1)

            def up(q, nq, a, high, low):
                pe.wait_ge(x_split, a + 1)
                if nq >= 1:
                    pe.wait_ge(hidden_ready, q)
                for bank, at in ((ps_g, 0), (ps_u, UP_AT)):
                    for c in range(EC):
                        cols = slice(at + c * HID, at + (c + 1) * HID)
                        for k, (x_part, w_part) in enumerate(((x_high, high), (x_high, low), (x_low, high))):
                            last = nc.tensor.matmul(bank[:, 0:HID], x_part[:, c], w_part(P, cols), start=(c == 0 and k == 0),
                                                    stop=(c == EC - 1 and k == 2))
                last.then_inc(up_done, 1)

            def turn_h(q, nq):
                pe.wait_ge(hidden_ready, q + 1)
                if nq >= 1:
                    pe.wait_ge(h_split, q)
                for c in range(HC):
                    last = nc.tensor.transpose(ps_h[:, c], hidden[:, c * P:(c + 1) * P], ident[:])
                last.then_inc(h_turned, 1)

            def down(q, high, low, first, final):
                pe.wait_ge(h_split, q + 1)
                for c in range(HC):
                    rows = P if c < HC - 1 else HID_TAIL
                    cols = slice(DOWN_AT + c * E, DOWN_AT + (c + 1) * E)
                    for k, (h_part, w_part) in enumerate(((h_high, high), (h_high, low), (h_low, high))):
                        last = nc.tensor.matmul(ps_y[:], h_part[0:rows, c], w_part(rows, cols), start=(first and c == 0 and k == 0),
                                                stop=(final and c == HC - 1 and k == 2))
                last.then_inc(down_done, 1)

            def shared(s):
                return (lambda rows, cols: sh[0:rows, s, cols]), (lambda rows, cols: sl[0:rows, s, cols])

            def turn_routed(i):
                pe.wait_ge(x_loaded, 16 * i + 16)
                turn_x(t_n + i, 1)

            def shared_tile(m, nm, last):
                up(2 * m, nm, m, *shared(0))
                if nm >= 1:
                    down(2 * m - 1, *shared(1), False, True)
                turn_h(2 * m, nm)
                up(2 * m + 1, 1, m, *shared(1))
                if not last:
                    pe.wait_ge(x_normed, m + 2)
                    turn_x(m + 1, 1)
                elif routed:
                    turn_routed(0)
                if nm >= 1:
                    pe.wait_ge(y_read, m)
                down(2 * m, *shared(0), True, False)
                turn_h(2 * m + 1, 1)

            pe.wait_ge(pad_set, 1)
            pe.wait_ge(x_normed, 1)
            turn_x(0, 0)
            shared_tile(0, 0, False)
            with pe.Fori(1, t_n - 1) as m:
                shared_tile(m, 1, False)
            shared_tile(t_n - 1, 1, True)
            if not routed:
                down(units - 1, *shared(1), False, True)
                return

            def weights_of(i):
                slot = pe.value_load(plan[0:1, 1, bass.ds(i, 1)], min_val=0, max_val=1)

                def of(w):
                    return lambda rows, cols: w[0:rows, bass.ds(slot, 1), cols].rearrange("p o c -> p (o c)")

                return of(w_high), of(w_low)

            def routed_up(i):
                need = pe.value_load(plan[0:1, 0, bass.ds(i, 1)], min_val=1, max_val=NE)
                high, low = weights_of(i)
                pe.wait_ge(weights_split, need * 4)
                up(units + i, 1, t_n + i, high, low)

            def routed_down(i):
                high, low = weights_of(i)
                pe.wait_ge(y_read, t_n + i)
                down(units + i, high, low, True, True)

            routed_up(0)
            turn_routed(1)
            down(units - 1, *shared(1), False, True)
            turn_h(units, 1)
            with pe.Fori(1, r_n - 1) as i:
                routed_up(i)
                turn_routed(i + 1)
                routed_down(i - 1)
                turn_h(units + i, 1)
            routed_up(r_n - 1)
            routed_down(r_n - 2)
            turn_h(units + r_n - 1, 1)
            routed_down(r_n - 1)


def build(nc, x, ctx512, gate_w, w_gate, w_up, w_down, sw_gate, sw_up, sw_down, out):
    q_scr = nc.dram_tensor("q_scr", (B, E, TERMS, S), BF16, kind="Internal").ap()
    k_scr = nc.dram_tensor("k_scr", (B, KV * D, TERMS, S), BF16, kind="Internal").ap()
    xg = nc.dram_tensor("x_sorted", (SLOT_ROWS, E), F32, kind="Internal").ap()
    y = nc.dram_tensor("y_sorted", (SLOT_TILES * P, E), F32, kind="Internal").ap()
    with ExitStack() as ctx:
        def sb(name, shape, dt=F32):
            return ctx.enter_context(nc.sbuf_tensor(name, shape, dt))

        x_res = sb("x_res", [P, NT, E])
        ident = sb("ident", [P, P])
        ident_bf = sb("ident_bf", [P, P], BF16)
        mean2, rstd2 = sb("mean2", [P, NT]), sb("rstd2", [P, NT])
        top_w = sb("top_w", [P, NT, TOP])
        slots = sb("slots", [P, TOP, NT], U32)
        plan = sb("plan", [1, 3, SLOT_TILES], I32)
        sh, sl = sb("shared_high", [P, SETS, W_COLS], F32R), sb("shared_low", [P, SETS, W_COLS], F32R)

        attention(nc, x_res, ident, ident_bf, x, ctx512, q_scr, k_scr, xg, sh, sl, (sw_gate, sw_up, sw_down))
        gating(nc, x_res, ident, gate_w, (mean2, rstd2), top_w, slots, plan)
        feed_forward(nc, (0, NA), True, x_res, ident, (mean2, rstd2), (sh, sl), slots, plan, xg, y, None, top_w, (w_gate, w_up, w_down))
        feed_forward(nc, (NA, NT - NA), False, x_res, ident, (mean2, rstd2), (sh, sl), slots, plan, xg, y,
                     out.rearrange("b s e -> (b s) e"), top_w, None)


_INS = ["x", "ctx_512", "L0_ffn_gate_w", "L0_ffn_w_gate", "L0_ffn_w_up", "L0_ffn_w_down", "L0_ffn_sw_gate", "L0_ffn_sw_up", "L0_ffn_sw_down"]


def kernel(**inputs):
    import numpy as _np
    import concourse.bacc as _bacc
    from concourse import mybir as _mybir
    from concourse.bass_utils import run_bass_kernel_spmd as _run

    nc = _bacc.Bacc("TRN2", target_bir_lowering=False, num_devices=1)
    arrays, args = {}, []
    for name in _INS:
        a = _np.ascontiguousarray(inputs[name])
        arrays[f"in_{name}_dram"] = a
        args.append(nc.dram_tensor(f"in_{name}_dram", a.shape, _mybir.dt.from_np(a.dtype), kind="ExternalInput").ap())
    out = nc.dram_tensor("out_dram", (B, S, E), _mybir.dt.float32, kind="ExternalOutput").ap()
    build(nc, *args, out)
    r = _run(nc, [arrays], core_ids=[0])
    return r.results[0]["out_dram"]
```

```python
from contextlib import ExitStack

import concourse.bass as bass
from concourse import mybir

P = 128
F32 = mybir.dt.float32
F32R = mybir.dt.float32r
BF16 = mybir.dt.bfloat16
I32 = mybir.dt.int32
U32 = mybir.dt.uint32
ALU = mybir.AluOpType
ACT = mybir.ActivationFunctionType
AX_X = mybir.AxisListType.X

B, S, E = 8, 256, 512
KV, G, D = 8, 4, 16
H = KV * G
T = B * S
NT = T // P
ST = S // P
EC = E // P
HALF = KV // 2
SCALE = 1.0 / D ** 0.5
EPS = 1e-5
RSQRT_SEED = float(0x5F3759DF)
NEWTON = 4

NE, TOP, HID = 8, 2, 352
SETS = 2
HC = 3
HID_TAIL = HID - (HC - 1) * P
UP_AT, DOWN_AT = EC * HID, 2 * EC * HID
W_COLS = DOWN_AT + HC * E
PIECES = 4
SLOT_TILES = (TOP * T) // P + NE - 1
LOOP_TILES = 4
ZERO_TILES = -(-SLOT_TILES // B)
SLOT_ROWS = ZERO_TILES * B * P
NA = NT // 2
UNITS_A = SETS * NA

Q_PART = (0, 1, 2, 0, 1, 0)
K_PART = (0, 0, 0, 1, 1, 2)
TERMS = len(Q_PART)
Q_RUNS = ((0, 3, 0, 1), (0, 2, 3, 1), (0, 1, 5, 1))
K_RUNS = ((0, 1, 0, 3), (1, 1, 3, 2), (2, 1, 5, 1))
ROWS = TERMS * D
ROWS_MAX = ROWS + 2


def rsqrt_newton(eng, chain, out, var, t1, t2):
    chain(eng.tensor_scalar(var, var, EPS, None, ALU.add))
    chain(eng.tensor_scalar(out.bitcast(I32), var.bitcast(I32), -0.5, RSQRT_SEED, ALU.mult, ALU.add))
    for _ in range(NEWTON):
        chain(eng.tensor_tensor(t1, out, out, ALU.mult))
        chain(eng.tensor_tensor(t2, t1, var, ALU.mult))
        chain(eng.tensor_scalar(t1, t2, -0.5, 1.5, ALU.mult, ALU.add))
        chain(eng.tensor_tensor(out, out, t1, ALU.mult))


def each_batch(eng, body):
    body(0, 0)
    with eng.Fori(1, 4, 2) as i:
        body(i, 1)
        body(i + 1, 2)
    for b in (5, 6, 7):
        body(b, b)


SPLIT_TURNS = (0, 5, 6, 7)


JOBS = (
    (0, "max_b", 0),
    (1, "query_0", 2),
    (2, "key", 2),
    (3, "query_1", 2),
    (4, "out_b0", -1),
    (5, "out_b1", -1),
    (8, "max_a", 1),
    (12, "out_a0", 0),
    (13, "out_a1", 0),
)
FIRST_JOBS = (("query_0", 0), ("query_1", 0), ("key", 0), ("query_0", 1), ("query_1", 1), ("key", 1), ("max_a", 0))
LAST_JOBS = (("out_b0", B - 1), ("out_b1", B - 1))


def job_at(slot, n):
    for s, job, away in JOBS:
        if s == slot and 0 <= n + away < B:
            return job, away
    return None, 0


def job_before(slot, n):
    here = [(job, away) for s, job, away in JOBS if s < slot and 0 <= n + away < B]
    if here:
        return here[-1]
    if n == 0:
        job, b = FIRST_JOBS[-1]
        return job, b
    there = [(job, away - 1) for _, job, away in JOBS if 0 <= n - 1 + away < B]
    return there[-1]


def attention(nc, x_res, ident, ident_bf, x, ctx512, q_scr, k_scr, xg, sh, sl, shared_src):
    x_dram = x.rearrange("b (t p) e -> b p t e", p=P)
    ctx_dram = ctx512.rearrange("b (t p) e -> b p t e", p=P)

    with ExitStack() as ctx:
        def sb(name, shape, dt=F32):
            return ctx.enter_context(nc.sbuf_tensor(name, shape, dt))

        def psum(name, shape, dt=F32):
            return ctx.enter_context(nc.psum_tensor(name, shape, dt))

        def sem(name):
            return ctx.enter_context(nc.semaphore(name))

        stats = sb("stats", [P, NT, 6])
        mean_var = sb("mean_var", [P, NT, 2])
        rstd = sb("rstd", [P, NT])
        var = sb("var", [P, NT])
        newton_1 = sb("newton_1", [P, NT])
        newton_2 = sb("newton_2", [P, NT])
        xn = sb("xn", [P, ST, E])
        q_part = sb("q_part", [P, 2, EC, 3, S], BF16)
        q_rest = sb("q_rest", [P, EC, P])
        k_part = sb("k_part", [P, 3, S], BF16)
        k_rest = sb("k_rest", [P, S])
        ctx_cur = sb("ctx_cur", [P, 2, ST, KV * D])
        q_stack = sb("q_stack", [ROWS_MAX, 2, H, S], BF16)
        k_stack = sb("k_stack", [ROWS_MAX, 2, KV, S], BF16)
        v_aug = sb("v_aug", [P, 2, ST, KV, 32])
        maxes = sb("maxes", [P, 2, ST, HALF * G])
        max_part = sb("max_part", [P, ST, 2, HALF * G], BF16)
        max_rows = sb("max_rows", [2 * HALF * G, S], BF16)
        probs = sb("probs", [P, 2, ST, G, S])
        out_t = sb("out_t", [P, 2, HALF, S])
        rden = sb("rden", [P, HALF * G])
        out_norm = sb("out_norm", [P, 2, HALF * G * D])

        stage = sb("sh_stage", [P, 2, UP_AT])
        zero = sb("zero", [P, E // 2])

        ps_score = psum("ps_score", [P, 2, G, S])
        ps_max = psum("ps_max", [P, 2, 2, S])
        ps_out = psum("ps_out", [P, 2, S])
        ps_job = psum("ps_job", [P, 4 * P])
        ps_job_bf = ps_job[:].bitcast(BF16)

        x_first, x_rest = sem("x_first"), sem("x_rest")
        ctx_loaded = [sem(f"ctx_loaded{i}") for i in range(2)]
        ln_step = sem("ln_step")
        ones_set = sem("ones_set")
        zero_set, cleared, ident_set = sem("zero_set"), sem("cleared"), sem("ident_set")
        high_loaded, stage_loaded, weights_split = [sem(f"sh_high_loaded{i}") for i in range(PIECES)], [sem(f"sh_stage_loaded{i}") for i in range(2)], sem("sh_split")
        xn_ready = [sem(f"xn_ready{i}") for i in range(ST)]
        names = [job for _, job, _ in JOBS]
        job_done = {j: sem("done_" + j) for j in names}
        job_read = {j: sem("read_" + j) for j in names if not j.startswith("out")}
        q_high = [sem(f"q_high{i}") for i in range(ST)]
        k_high = sem("k_high")
        q_split = sem("q_split")
        k_split = sem("k_split")
        pool_step = sem("pool_step")
        parts_written = sem("parts_written")
        stack_ready = [sem(f"stack_ready{i}") for i in range(2)]
        v_ready = sem("v_ready")
        max_scored = sem("max_scored")
        max_taken = sem("max_taken")
        max_split = sem("max_split")
        max_sent = [sem(f"max_sent{i}") for i in range(2)]
        max_step = sem("max_step")
        scored = sem("scored")
        exp_done = sem("exp_done")
        weighted = sem("weighted")
        out_copied = sem("out_copied")
        rden_ready = sem("rden_ready")
        normed = sem("normed")
        added = sem("added")

        block = ctx.enter_context(nc.Block())

        def job_index(job):
            return (0 if job[4] == "a" else 1), int(job[5])

        @block.sync
        def _(sp):
            for b in range(2):
                sp.dma_start(x_res[:, ST * b:ST * b + ST, :], x_dram[b]).then_inc(x_first, 16)
                sp.dma_start(ctx_cur[:, b], ctx_dram[b]).then_inc(ctx_loaded[b], 16)
            for b in range(2, B):
                sp.dma_start(x_res[:, ST * b:ST * b + ST, :], x_dram[b]).then_inc(x_rest, 16)

            def write_parts(b, n):
                sp.wait_ge(q_split, 2 * b + 2)
                for part, n_parts, term, _ in Q_RUNS:
                    sp.dma_start(q_scr[bass.ds(b, 1)].rearrange("o (c p) t s -> p (o c) t s", p=P)[:, :, term:term + n_parts],
                                 q_part[:, n % 2, :, part:part + n_parts]).then_inc(parts_written, 16)
                sp.wait_ge(k_split, b + 1)
                for part, _, term, times in K_RUNS:
                    sp.dma_start(k_scr[bass.ds(b, 1)].rearrange("o p t s -> p (o t) s")[:, term:term + times],
                                 k_part[:, part:part + 1].to_broadcast([P, times, S])).then_inc(parts_written, 16)

            def read_stack(b, n, half):
                free = 16 * (b - 2) + 8 * half + 8
                if n >= 2 and not isinstance(b, int):
                    free = sp.snap(free)
                if half == 0:
                    sp.wait_ge(parts_written, 96 * b + 96)
                if n >= 2:
                    sp.wait_ge(scored, free)
                heads = slice(half * HALF * G, (half + 1) * HALF * G)
                kvs = slice(half * HALF, (half + 1) * HALF)
                sp.dma_start(q_stack[0:ROWS, n % 2, heads, :],
                             q_scr[bass.ds(b, 1)].rearrange("o (h d) t s -> (d t) (o h) s", d=D)[:, heads]).then_inc(stack_ready[half], 16)
                sp.dma_start(k_stack[0:ROWS, n % 2, kvs, :],
                             k_scr[bass.ds(b, 1)].rearrange("o (h d) t s -> (d t) (o h) s", d=D)[:, kvs]).then_inc(stack_ready[half], 16)

            def send_max(b, n, half):
                sp.wait_ge(job_read["max_a" if half == 0 else "max_b"], b + 1)
                sp.dma_start(q_stack[ROWS:ROWS_MAX, n % 2, half * HALF * G:(half + 1) * HALF * G, :],
                             max_rows[:]).then_inc(max_sent[half], 16)

            for b in range(2):
                write_parts(b, b)
                for half in range(2):
                    read_stack(b, b, half)
            send_max(0, 0, 0)

            def turn(b, n):
                send_max(b, n, 1)
                if n + 2 < B:
                    sp.wait_ge(job_done["key"], b + 1)
                    sp.wait_ge(v_ready, b + 1)
                    sp.dma_start(ctx_cur[:, n % 2], ctx_dram[bass.ds(b + 2, 1)].rearrange("o p t e -> p (o t) e")).then_inc(ctx_loaded[n % 2], 16)
                    write_parts(b + 2, n + 2)
                    read_stack(b + 2, n + 2, 0)
                if n + 1 < B:
                    send_max(b + 1, n + 1, 0)
                if n + 2 < B:
                    read_stack(b + 2, n + 2, 1)
                sp.dma_start(xg[bass.ds(b * ZERO_TILES * P, ZERO_TILES * P), :].rearrange("(p t) (f e) -> p (t f) e", p=P, f=2),
                             zero[:].unsqueeze(1).to_broadcast([P, 2 * ZERO_TILES, E // 2])).then_inc(cleared, 16)

            sp.wait_ge(zero_set, 1)
            each_batch(sp, turn)
            sp.wait_ge(cleared, 16 * B)

        @block.gpsimd
        def _(pool):
            for m in (ident, ident_bf):
                nc.gpsimd.memset(m[:], 0.0).then_inc(ident_set, 1)
            pool.wait_ge(ident_set, 2)
            for m in (ident, ident_bf):
                nc.gpsimd.affine_select(out=m[:], in_=m[:], compare_op=ALU.not_equal, fill=1.0, base=0, pattern=[[-1, P]],
                                        channel_multiplier=1).then_inc(ident_set, 1)
            nc.gpsimd.memset(zero[:], 0.0).then_inc(zero_set, 1)
            nc.gpsimd.memset(v_aug[:], 0.0).then_inc(ones_set, 1)
            pool.wait_ge(ones_set, 1)
            nc.gpsimd.memset(v_aug[:, :, :, :, D:D + 1], 1.0).then_inc(ones_set, 1)
            pool.wait_ge(ones_set, 2)
            nc.gpsimd.memset(k_stack[ROWS:ROWS_MAX], 1.0).then_inc(ones_set, 1)

            def split_queries(b, n, st):
                tokens = slice(st * P, (st + 1) * P)
                pool.wait_ge(job_read[f"query_{st}"], b + 1)
                if n >= 2:
                    pool.wait_ge(parts_written, 96 * b - 96)
                nc.gpsimd.tensor_tensor(q_part[:, n % 2, :, 1, tokens], q_rest[:], zero[:, 0:1].unsqueeze(2).to_broadcast([P, EC, P]), ALU.add).then_inc(pool_step, 1)
                pool.wait_ge(pool_step, 3 * b + (1, 3)[st])
                nc.gpsimd.tensor_tensor(q_part[:, n % 2, :, 2, tokens], q_rest[:], q_part[:, n % 2, :, 1, tokens], ALU.subtract).then_inc(q_split, 1)

            def split_keys(b, n):
                pool.wait_ge(job_read["key"], b + 1)
                if n >= 1:
                    pool.wait_ge(parts_written, 96 * b)
                nc.gpsimd.tensor_tensor(k_part[:, 1], k_rest[:], zero[:, 0:1].to_broadcast([P, S]), ALU.add).then_inc(pool_step, 1)
                pool.wait_ge(pool_step, 3 * b + 2)
                nc.gpsimd.tensor_tensor(k_part[:, 2], k_rest[:], k_part[:, 1], ALU.subtract).then_inc(k_split, 1)

            def values(b, n):
                pool.wait_ge(ctx_loaded[n % 2], 8 * (b - n % 2) + 16)
                if n >= 2:
                    pool.wait_ge(weighted, 8 * (b - 1))
                for tc in range(ST):
                    now = ctx_cur[:, n % 2, tc].rearrange("p (k d) -> p k d", d=D)
                    last = nc.gpsimd.tensor_tensor(v_aug[:, n % 2, tc, :, 0:D], now, zero[:, 0:1].unsqueeze(2).to_broadcast([P, KV, D]), ALU.add)
                last.then_inc(v_ready, 1)

            def add_out(b, n, half, st):
                k = 2 * half + st
                pool.wait_ge(normed, 4 * b + k + 1)
                cols = slice(half * HALF * G * D, (half + 1) * HALF * G * D)
                row = x_res[:, bass.ds(ST * b + st, 1), cols].rearrange("p o c -> p (o c)")
                nc.gpsimd.tensor_tensor(row, row, out_norm[:, st], ALU.add).then_inc(added, 1)

            pool.wait_ge(ones_set, 3)
            splitter = Splitter(nc, pool, stage, high_loaded, stage_loaded, weights_split)
            g, u, d = shared_src
            pieces = []
            for s in range(SETS):
                cols = slice(s * HID, (s + 1) * HID)
                pieces += weight_pieces(g[:, cols], u[:, cols], d[cols, :])

            def shared_weights(n):
                if n not in SPLIT_TURNS:
                    return
                first = 2 * SPLIT_TURNS.index(n)
                for k in (first, first + 1):
                    splitter.subtract(k, pieces[k], sh[:, k // PIECES], sl[:, k // PIECES])
                    if k + 2 < SETS * PIECES:
                        splitter.load_high(k + 2, pieces[k + 2], sh[:, (k + 2) // PIECES])
                        splitter.load_stage(k + 2, pieces[k + 2])

            for b in range(2):
                split_queries(b, b, 0)
                split_keys(b, b)
                split_queries(b, b, 1)
            values(0, 0)

            def turn(b, n):
                if n + 2 < B:
                    split_queries(b + 2, n + 2, 0)
                    split_keys(b + 2, n + 2)
                    split_queries(b + 2, n + 2, 1)
                if n + 1 < B:
                    values(b + 1, n + 1)
                if n == 0:
                    for k in range(2):
                        splitter.load_high(k, pieces[k], sh[:, 0])
                        splitter.load_stage(k, pieces[k])
                if n >= 1:
                    for st in range(ST):
                        add_out(b - 1, n - 1, 1, st)
                shared_weights(n)
                for st in range(ST):
                    add_out(b, n, 0, st)
            each_batch(pool, turn)
            for st in range(ST):
                add_out(B - 1, B - 1, 1, st)

        @block.scalar
        def _(act):
            def query_high(b, n, st):
                act.wait_ge(job_done[f"query_{st}"], b + 1)
                if n >= 2:
                    act.wait_ge(parts_written, 96 * b - 96)
                nc.scalar.activation(q_part[:, n % 2, :, 0, st * P:(st + 1) * P], ps_job[:].rearrange("p (c s) -> p c s", s=P), ACT.Copy).then_inc(q_high[st], 1)

            def key_high(b, n):
                act.wait_ge(job_done["key"], b + 1)
                if n >= 1:
                    act.wait_ge(parts_written, 96 * b)
                nc.scalar.activation(k_part[:, 0], ps_job[:, 0:S], ACT.Copy).then_inc(k_high, 1)

            def job(slot, b, n):
                name, away = job_at(slot, n)
                if name in ("query_0", "query_1"):
                    query_high(b + away, n + away, int(name[-1]))
                if name == "key":
                    key_high(b + away, n + away)

            for b in range(2):
                query_high(b, b, 0)
                query_high(b, b, 1)
                key_high(b, b)

            def turn(b, n):
                for k in range(KV):
                    g, ng = 8 * b + k, 8 * n + k
                    if k % 2 == 1 and ng >= 3:
                        i = (k - 3) // 2
                        act.wait_ge(weighted, 8 * b + 2 * i + 2)
                        half, nb_away = ((i % 4) // 2, -1 if i < 0 else 0)
                        if n + nb_away >= 1:
                            act.wait_ge(job_done[f"out_{'ab'[half]}1"], b + nb_away)
                        nc.scalar.activation(out_t[:, half, 2 * (i % 2):2 * (i % 2) + 2, :], ps_out[:], ACT.Copy).then_inc(out_copied, 1)
                    for tc in range(ST):
                        u = 2 * g + tc
                        act.wait_ge(scored, u + 1)
                        if ng >= 2:
                            act.wait_ge(weighted, g - 1)
                        nc.scalar.activation(probs[:, k % 2, tc], ps_score[:, tc], ACT.Exp, scale=SCALE).then_inc(exp_done, 1)
                        job(2 * k + tc, b, n)

            each_batch(act, turn)
            act.wait_ge(weighted, KV * B)
            act.wait_ge(job_done["out_b1"], B - 1)
            nc.scalar.activation(out_t[:, 1, 2:4, :], ps_out[:], ACT.Copy).then_inc(out_copied, 1)

        @block.vector
        def _(dve):
            done = [0]

            def chain(ins):
                done[0] += 1
                ins.then_inc(ln_step, 1)
                dve.wait_ge(ln_step, done[0])

            def statistics(t0, t1):
                for t in range(t0, t1):
                    nc.vector.bn_stats(stats[:, t], x_res[:, t]).then_inc(ln_step, 1)
                    done[0] += 1
                dve.wait_ge(ln_step, done[0])
                for t in range(t0, t1):
                    nc.vector.bn_aggr(mean_var[:, t], stats[:, t]).then_inc(ln_step, 1)
                    done[0] += 1
                dve.wait_ge(ln_step, done[0])
                some = slice(t0, t1)
                chain(nc.vector.tensor_copy(var[:, some], mean_var[:, some, 1]))
                rsqrt_newton(nc.vector, chain, rstd[:, some], var[:, some], newton_1[:, some], newton_2[:, some])

            def normalize(b, n, st):
                if n >= 1:
                    dve.wait_ge(job_done[f"query_{st}"], b)
                t = ST * b + st
                nc.vector.tensor_scalar(xn[:, st], x_res[:, bass.ds(t, 1), :].rearrange("p o c -> p (o c)"), mean_var[:, bass.ds(t, 1), 0],
                                        rstd[:, bass.ds(t, 1)], ALU.subtract, ALU.mult).then_inc(xn_ready[st], 1)

            def query_rest(b, n, st):
                dve.wait_ge(q_high[st], b + 1)
                if n >= 1 or st == 1:
                    dve.wait_ge(q_split, 2 * b + st)
                nc.vector.tensor_tensor(q_rest[:], ps_job[:].rearrange("p (c s) -> p c s", s=P), q_part[:, n % 2, :, 0, st * P:(st + 1) * P],
                                        ALU.subtract).then_inc(job_read[f"query_{st}"], 1)

            def key_rest(b, n):
                dve.wait_ge(k_high, b + 1)
                if n >= 1:
                    dve.wait_ge(k_split, b)
                nc.vector.tensor_tensor(k_rest[:], ps_job[:, 0:S], k_part[:, 0], ALU.subtract).then_inc(job_read["key"], 1)

            def take_max(b, n, k, st):
                for pair in range(2):
                    i = 32 * b + 4 * k + 2 * st + pair
                    dve.wait_ge(max_scored, i + 1)
                    h = G * (k % HALF) + 2 * pair
                    nc.vector.tensor_reduce(maxes[:, k // HALF, st, h:h + 2], ps_max[:, pair], AX_X, ALU.max).then_inc(max_taken, 1)

            def split_max(b, n, half):
                dve.wait_ge(max_taken, 32 * b + 16 * half + 16)
                if half == 1:
                    dve.wait_ge(job_done["max_a"], b + 1)
                elif n >= 1:
                    dve.wait_ge(job_done["max_b"], b)
                nc.vector.tensor_scalar(max_part[:, :, 0], maxes[:, half], -1.0, None, ALU.mult).then_inc(max_step, 1)
                dve.wait_ge(max_step, 2 * b + half + 1)
                nc.vector.scalar_tensor_tensor(out=max_part[:, :, 1], in0=maxes[:, half], scalar=-1.0, in1=max_part[:, :, 0],
                                               op0=ALU.mult, op1=ALU.subtract).then_inc(max_split, 1)

            def max_to_rows(b, n, half):
                name = "max_" + "ab"[half]
                dve.wait_ge(job_done[name], b + 1)
                if half == 1:
                    dve.wait_ge(max_sent[0], 16 * b + 16)
                elif n >= 1:
                    dve.wait_ge(max_sent[1], 16 * b)
                nc.vector.tensor_copy(max_rows[:], ps_job_bf[0:2 * HALF * G, 0:S]).then_inc(job_read[name], 1)

            def normalize_out(b, n, name):
                half, st = job_index(name)
                i = 4 * b + 2 * half + st
                tile = ps_job[:].rearrange("p (h d) -> p h d", d=32)
                dve.wait_ge(job_done[name], b + 1)
                nc.vector.reciprocal(rden[:], tile[:, :, D]).then_inc(rden_ready, 1)
                dve.wait_ge(rden_ready, i + 1)
                if n >= 1 or half == 1:
                    dve.wait_ge(added, i - 1)
                nc.vector.tensor_tensor(out_norm[:, st].rearrange("p (h d) -> p h d", d=D), tile[:, :, 0:D],
                                        rden[:].unsqueeze(2).to_broadcast([P, HALF * G, D]), ALU.mult).then_inc(normed, 1)

            def job(slot, b, n):
                name, away = job_at(slot, n)
                if name is None:
                    return
                b, n = b + away, n + away
                if name.startswith("query"):
                    query_rest(b, n, int(name[-1]))
                elif name == "key":
                    key_rest(b, n)
                elif name.startswith("max"):
                    max_to_rows(b, n, "ab".index(name[-1]))
                else:
                    normalize_out(b, n, name)

            dve.wait_ge(x_first, 32)
            statistics(0, 2 * ST)
            for b in range(2):
                for st in range(ST):
                    normalize(b, b, st)
                    query_rest(b, b, st)
                key_rest(b, b)
            dve.wait_ge(x_rest, 16 * (B - 2))
            statistics(2 * ST, NT)
            for k in range(KV):
                for st in range(ST):
                    take_max(0, 0, k, st)
                if k == HALF - 1:
                    split_max(0, 0, 0)
                if k == HALF:
                    max_to_rows(0, 0, 0)
            split_max(0, 0, 1)

            def turn(b, n):
                for k in range(KV):
                    if n + 2 < B and k < ST:
                        normalize(b + 2, n + 2, k)
                    for tc in range(ST):
                        if n + 1 < B:
                            take_max(b + 1, n + 1, k, tc)
                        job(2 * k + tc, b, n)
                    if n + 1 < B and k % HALF == HALF - 1:
                        split_max(b + 1, n + 1, k // HALF)

            each_batch(dve, turn)
            for st in range(ST):
                normalize_out(B - 1, B - 1, f"out_b{st}")

        @block.tensor
        def _(pe):
            def bank_free(job, b):
                if job.startswith("out"):
                    half, st = job_index(job)
                    pe.wait_ge(normed, 4 * b + 2 * half + st + 1)
                else:
                    pe.wait_ge(job_read[job], b + 1)

            def do_job(name, b, n):
                if name.startswith("query"):
                    st = int(name[-1])
                    pe.wait_ge(xn_ready[st], b + 1)
                    for c in range(EC):
                        last = nc.tensor.transpose(ps_job[:, c * P:(c + 1) * P], xn[:, st, c * P:(c + 1) * P], ident[:])
                elif name == "key":
                    pe.wait_ge(ctx_loaded[n % 2], 8 * (b - n % 2) + 16)
                    for st in range(ST):
                        last = nc.tensor.transpose(ps_job[:, st * P:(st + 1) * P], ctx_cur[:, n % 2, st], ident[:])
                elif name.startswith("max"):
                    half = "ab".index(name[-1])
                    pe.wait_ge(max_split, 2 * b + half + 1)
                    for st in range(ST):
                        last = nc.tensor.transpose(ps_job_bf[0:2 * HALF * G, st * P:(st + 1) * P],
                                                   max_part[:, st].rearrange("p a h -> p (a h)"), ident_bf[:])
                else:
                    half, st = job_index(name)
                    pe.wait_ge(out_copied, 4 * b + 2 * half + 2)
                    for kv in range(HALF):
                        last = nc.tensor.transpose(ps_job[:, kv * P:(kv + 1) * P], out_t[:, half, kv, st * P:(st + 1) * P], ident[:])
                last.then_inc(job_done[name], 1)

            def job(slot, b, n):
                name, away = job_at(slot, n)
                if name is None:
                    return
                before, b_away = job_before(slot, n)
                bank_free(before, b + b_away)
                do_job(name, b + away, n + away)

            def score_for_max(b, n, k, st, pairs=(0, 1)):
                if st == 0 and k % HALF == 0 and 0 in pairs:
                    pe.wait_ge(stack_ready[k // HALF], 32 * b + 32)
                for pair in pairs:
                    i, ni = 32 * b + 4 * k + 2 * st + pair, 32 * n + 4 * k + 2 * st + pair
                    if ni >= 2:
                        pe.wait_ge(max_taken, i - 1)
                    for j in range(2):
                        last = nc.tensor.matmul(ps_max[:, pair, j], q_stack[0:ROWS, n % 2, G * k + 2 * pair + j, st * P:(st + 1) * P],
                                                k_stack[0:ROWS, n % 2, k, :], start=True, stop=True)
                    last.then_inc(max_scored, 1)

            def score(b, n, k, tc):
                u, nu = 16 * b + 2 * k + tc, 16 * n + 2 * k + tc
                if tc == 0 and k % HALF == 0:
                    pe.wait_ge(max_sent[k // HALF], 16 * b + 16)
                if nu >= 2:
                    pe.wait_ge(exp_done, u - 1)
                for pair in range(2):
                    last = nc.tensor.matmul(ps_score[:, tc, 2 * pair:2 * pair + 2, :], k_stack[:, n % 2, k, tc * P:(tc + 1) * P],
                                            q_stack[:, n % 2, G * k + 2 * pair:G * k + 2 * pair + 2, :], start=True, stop=True)
                last.then_inc(scored, 1)

            def weigh(b, n, k, tc):
                pe.wait_ge(exp_done, 16 * b + 2 * k + tc + 1)
                if k == 0 and tc == 0:
                    pe.wait_ge(v_ready, b + 1)
                if k % 2 == 0 and tc == 0 and 8 * n + k >= 2:
                    pe.wait_ge(out_copied, 4 * b + k // 2)
                for j in range(G):
                    last = nc.tensor.matmul(ps_out[32 * j:32 * j + 32, k % 2, :], v_aug[:, n % 2, tc, k, :], probs[:, k % 2, tc, j, :],
                                            start=(tc == 0), stop=(tc == ST - 1))
                if tc == ST - 1:
                    last.then_inc(weighted, 1)

            pe.wait_ge(ident_set, 4)
            before = None
            for name, b in FIRST_JOBS[:-1]:
                if before:
                    bank_free(*before)
                do_job(name, b, b)
                before = (name, b)
            pe.wait_ge(ones_set, 3)
            for k in range(KV):
                for st in range(ST):
                    score_for_max(0, 0, k, st)
                if k == HALF:
                    bank_free(*before)
                    do_job("max_a", 0, 0)

            def turn(b, n):
                for k in range(KV):
                    for tc in range(ST):
                        score(b, n, k, tc)
                        if n + 1 < B:
                            score_for_max(b + 1, n + 1, k, tc, (0,))
                        if k >= 1:
                            weigh(b, n, k - 1, tc)
                        elif n >= 1:
                            weigh(b - 1, n - 1, KV - 1, tc)
                        if n + 1 < B:
                            score_for_max(b + 1, n + 1, k, tc, (1,))
                        job(2 * k + tc, b, n)

            each_batch(pe, turn)
            for tc in range(ST):
                weigh(B - 1, B - 1, KV - 1, tc)
            for name, b in LAST_JOBS:
                bank_free(*{"out_b0": ("out_a1", B - 1), "out_b1": ("out_b0", B - 1)}[name])
                do_job(name, b, b)

def weight_pieces(gate, up, down):
    return (
        (0, P, EC, HID, gate.rearrange("(c p) j -> p c j", p=P)),
        (UP_AT, P, EC, HID, up.rearrange("(c p) j -> p c j", p=P)),
        (DOWN_AT, P, HC - 1, E, down[0:(HC - 1) * P].rearrange("(c p) j -> p c j", p=P)),
        (DOWN_AT + (HC - 1) * E, HID_TAIL, 1, E, down[(HC - 1) * P:HID].rearrange("(c p) j -> p c j", p=HID_TAIL)),
    )


class Splitter:

    def __init__(self, nc, pool, stage, high_loaded, stage_loaded, split):
        self.nc, self.pool, self.stage = nc, pool, stage
        self.high_loaded, self.stage_loaded, self.split = high_loaded, stage_loaded, split

    @staticmethod
    def part(buffer, piece):
        col, rows, chunks, width, _ = piece
        return buffer[0:rows, col:col + chunks * width].rearrange("p (c j) -> p c j", j=width)

    def staged(self, k, piece):
        _, rows, chunks, width, _ = piece
        return self.stage[0:rows, k % 2, 0:chunks * width].rearrange("p (c j) -> p c j", j=width)

    def load_high(self, k, piece, high):
        self.pool.dma_start(self.part(high, piece), piece[4]).then_inc(self.high_loaded[k % PIECES], 16)

    def load_stage(self, k, piece):
        self.pool.dma_start(self.staged(k, piece), piece[4]).then_inc(self.stage_loaded[k % 2], 16)

    def subtract(self, k, piece, high, low):
        self.pool.wait_ge(self.high_loaded[k % PIECES], 16 * (k // PIECES) + 16)
        self.pool.wait_ge(self.stage_loaded[k % 2], 16 * (k // 2) + 16)
        self.nc.gpsimd.tensor_tensor(self.part(low, piece), self.staged(k, piece), self.part(high, piece).bitcast(F32),
                                     ALU.subtract).then_inc(self.split, 1)
        self.pool.wait_ge(self.split, k + 1)


def gating(nc, x_res, ident, gate_w, ln2, weights_out, slots, plan, ends):
    mean, rstd = ln2
    with ExitStack() as ctx:
        def sb(name, shape, dt=F32):
            return ctx.enter_context(nc.sbuf_tensor(name, shape, dt))

        def psum(name, shape, dt=F32):
            return ctx.enter_context(nc.psum_tensor(name, shape, dt))

        def sem(name):
            return ctx.enter_context(nc.semaphore(name))

        GT = 4
        stats = sb("stats2", [P, NT, 6])
        mv = sb("mv2", [P, NT, 2])
        var = sb("var2", [P, NT])
        n1, n2 = sb("n1_2", [P, NT]), sb("n2_2", [P, NT])
        xn = sb("xn2", [P, 2, E])
        xt = sb("xt2", [P, 2, EC, GT * P])
        gw = sb("gw", [P, EC, NE])
        lt = sb("lt", [NE, 2, GT * P])
        logits = sb("logits", [P, NT, NE])
        best = sb("best", [P, NT, NE])
        index = sb("index", [P, NT, NE], U32)
        index_f = sb("index_f", [P, TOP, NT])
        row_max = sb("row_max", [P, NT])
        row_sum = sb("row_sum", [P, NT])
        expert_no = sb("expert_no", [P, NE])
        chosen = [sb(f"chosen{k}", [P, NT, NE]) for k in range(TOP)]
        mask = sb("mask", [P, NT, NE], BF16)
        before = sb("before", [P, P], BF16)
        ones = sb("ones", [P, P], BF16)
        scan = [sb(f"scan{i}", [P, NT, NE]) for i in range(2)]
        place = sb("place", [P, NT, NE])
        picked = sb("picked", [P, NT, NE])
        tiles_i = sb("tiles_i", [P, NE], I32)
        tiles = sb("tiles", [P, NE])
        end_sum = [sb(f"end_sum{i}", [P, NE]) for i in range(2)]
        tile_no = sb("tile_no", [1, SLOT_TILES])
        passed = sb("passed", [1, SLOT_TILES, NE])
        expert_of = sb("expert_of", [1, SLOT_TILES])
        expert_i = sb("expert_i", [1, SLOT_TILES], I32)

        ps_t = psum("ps_t", [P, 2, EC * P])
        ps_l = psum("ps_l", [NE, GT * P])
        ps_r = psum("ps_r", [P, NT, NE])
        ps_c = psum("ps_c", [P, 2, NT * NE])

        gw_loaded, const_set = sem("gw_loaded"), sem("const_set")
        step, xn_ready, turned, copied = sem("g_step"), sem("g_xn"), sem("g_turned"), sem("g_copied")
        projected, lt_ready, back, probs_exp, mask_ready, counted = (sem("g_" + s) for s in ("proj", "lt", "back", "exp", "mask", "count"))
        max_sub = sem("g_maxsub")
        block = ctx.enter_context(nc.Block())

        @block.sync
        def _(sp):
            sp.dma_start(gw[:], gate_w.rearrange("(c p) e -> p c e", p=P)).then_inc(gw_loaded, 16)

        @block.gpsimd
        def _(pool):
            nc.gpsimd.memset(ones[:], 1.0).then_inc(const_set, 1)
            pool.wait_ge(const_set, 1)
            nc.gpsimd.affine_select(out=before[:], in_=ones[:], compare_op=ALU.is_gt, fill=0.0, base=0,
                                    pattern=[[1, P]], channel_multiplier=-1).then_inc(const_set, 1)
            pool.wait_ge(const_set, 2)
            nc.gpsimd.iota(expert_no[:], pattern=[[1, NE]], base=0, channel_multiplier=0, allow_small_or_imprecise_dtypes=True).then_inc(const_set, 1)
            pool.wait_ge(const_set, 3)
            nc.gpsimd.iota(tile_no[:], pattern=[[1, SLOT_TILES]], base=0, channel_multiplier=0, allow_small_or_imprecise_dtypes=True).then_inc(const_set, 1)

        @block.scalar
        def _(act):
            def copy_tile(t, nt):
                act.wait_ge(turned, t + 1)
                nc.scalar.activation(xt[:, (nt // GT) % 2, :, (nt % GT) * P:(nt % GT + 1) * P], ps_t[:, nt % 2].rearrange("p (c s) -> p c s", s=P),
                                     ACT.Copy).then_inc(copied, 1)

            for t in range(NT):
                copy_tile(t, t)
                if t % GT == GT - 1:
                    g = t // GT
                    act.wait_ge(projected, g + 1)
                    nc.scalar.activation(lt[:, g % 2], ps_l[:], ACT.Copy).then_inc(lt_ready, 1)
            act.wait_ge(max_sub, 1)
            nc.scalar.activation(logits[:], logits[:], ACT.Exp).then_inc(probs_exp, 1)

        @block.tensor
        def _(pe):
            pe.wait_ge(gw_loaded, 16)

            def project(g):
                pe.wait_ge(copied, GT * g + GT)
                if g >= 1:
                    pe.wait_ge(lt_ready, g)
                for c in range(EC):
                    last = nc.tensor.matmul(ps_l[:], gw[:, c], xt[:, g % 2, c], start=(c == 0), stop=(c == EC - 1))
                last.then_inc(projected, 1)

            def turn_back(g):
                pe.wait_ge(lt_ready, g + 1)
                for j in range(GT):
                    last = nc.tensor.transpose(ps_r[:, GT * g + j], lt[:, g % 2, j * P:(j + 1) * P], ident[0:NE, 0:NE])
                last.then_inc(back, 1)

            for t in range(NT):
                pe.wait_ge(xn_ready, t + 1)
                if t >= 2:
                    pe.wait_ge(copied, t - 1)
                for c in range(EC):
                    last = nc.tensor.transpose(ps_t[:, t % 2, c * P:(c + 1) * P], xn[:, t % 2, c * P:(c + 1) * P], ident[:])
                last.then_inc(turned, 1)
                if t % GT == 1 and t > GT:
                    turn_back(t // GT - 1)
                if t % GT == 0 and t >= GT:
                    project(t // GT - 1)
            project(NT // GT - 1)
            turn_back(NT // GT - 1)
            pe.wait_ge(mask_ready, 1)
            pe.wait_ge(const_set, 2)
            nc.tensor.matmul(ps_c[:, 0], before[:], mask[:].rearrange("p t e -> p (t e)"), start=True, stop=True)
            nc.tensor.matmul(ps_c[:, 1], ones[:], mask[:].rearrange("p t e -> p (t e)"), start=True, stop=True).then_inc(counted, 1)

        @block.vector
        def _(dve):
            done = [0]

            def chain(ins):
                done[0] += 1
                ins.then_inc(step, 1)
                dve.wait_ge(step, done[0])

            for t in range(NT):
                nc.vector.bn_stats(stats[:, t], x_res[:, t]).then_inc(step, 1)
            done[0] += NT
            dve.wait_ge(step, done[0])
            for t in range(NT):
                nc.vector.bn_aggr(mv[:, t], stats[:, t]).then_inc(step, 1)
            done[0] += NT
            dve.wait_ge(step, done[0])
            nc.vector.tensor_copy(mean[:], mv[:, :, 0]).then_inc(step, 1)
            done[0] += 1
            chain(nc.vector.tensor_copy(var[:], mv[:, :, 1]))
            rsqrt_newton(nc.vector, chain, rstd[:], var[:], n1[:], n2[:])
            for t in range(NT):
                if t >= 2:
                    dve.wait_ge(turned, t - 1)
                nc.vector.tensor_scalar(xn[:, t % 2], x_res[:, t], mean[:, t:t + 1], rstd[:, t:t + 1], ALU.subtract, ALU.mult).then_inc(xn_ready, 1)
            dve.wait_ge(back, NT // GT)
            chain(nc.vector.tensor_reduce(row_max[:], ps_r[:], AX_X, ALU.max))
            nc.vector.tensor_tensor(logits[:], ps_r[:], row_max[:].unsqueeze(2).to_broadcast([P, NT, NE]), ALU.subtract).then_inc(max_sub, 1)
            dve.wait_ge(probs_exp, 1)
            chain(nc.vector.tensor_reduce(row_sum[:], logits[:], AX_X, ALU.add))
            chain(nc.vector.reciprocal(row_sum[:], row_sum[:]))
            chain(nc.vector.tensor_tensor(logits[:], logits[:], row_sum[:].unsqueeze(2).to_broadcast([P, NT, NE]), ALU.mult))
            for t in range(NT):
                nc.vector.max(best[:, t], logits[:, t]).then_inc(step, 1)
            done[0] += NT
            dve.wait_ge(step, done[0])
            for t in range(NT):
                nc.vector.max_index(index[:, t], best[:, t], logits[:, t]).then_inc(step, 1)
            done[0] += NT
            dve.wait_ge(step, done[0])
            nc.vector.tensor_copy(weights_out[:], best[:, :, 0:TOP])
            chain(nc.vector.tensor_copy(index_f[:], index[:, :, 0:TOP].rearrange("p t k -> p k t")))
            dve.wait_ge(const_set, 4)
            for k in range(TOP):
                chain(nc.vector.tensor_tensor(chosen[k][:], expert_no[:].unsqueeze(1).to_broadcast([P, NT, NE]),
                                              index_f[:, k].unsqueeze(2).to_broadcast([P, NT, NE]), ALU.is_equal))
            nc.vector.tensor_tensor(mask[:], chosen[0][:], chosen[1][:], ALU.add).then_inc(mask_ready, 1)
            dve.wait_ge(counted, 1)
            chain(nc.vector.tensor_copy(scan[0][:], ps_c[:, 1].rearrange("p (t e) -> p t e", e=NE)))
            away, src = 1, 0
            while away < NT:
                nc.vector.tensor_copy(scan[1 - src][:, 0:away], scan[src][:, 0:away]).then_inc(step, 1)
                done[0] += 1
                chain(nc.vector.tensor_tensor(scan[1 - src][:, away:NT], scan[src][:, away:NT], scan[src][:, 0:NT - away], ALU.add))
                away, src = 2 * away, 1 - src
            total = scan[src]
            chain(nc.vector.tensor_tensor(place[:], total[:], ps_c[:, 1].rearrange("p (t e) -> p t e", e=NE), ALU.subtract))
            chain(nc.vector.tensor_tensor(place[:], place[:], ps_c[:, 0].rearrange("p (t e) -> p t e", e=NE), ALU.add))
            chain(nc.vector.tensor_scalar(tiles_i[:], total[:, NT - 1], float(P - 1), None, ALU.add))
            chain(nc.vector.tensor_scalar(tiles_i[:], tiles_i[:], P.bit_length() - 1, None, ALU.logical_shift_right))
            chain(nc.vector.tensor_copy(tiles[:], tiles_i[:]))
            chain(nc.vector.tensor_copy(end_sum[0][:], tiles[:]))
            away, src = 1, 0
            while away < NE:
                nc.vector.tensor_copy(end_sum[1 - src][:, 0:away], end_sum[src][:, 0:away]).then_inc(step, 1)
                done[0] += 1
                chain(nc.vector.tensor_tensor(end_sum[1 - src][:, away:NE], end_sum[src][:, away:NE], end_sum[src][:, 0:NE - away], ALU.add))
                away, src = 2 * away, 1 - src
            end = end_sum[src]
            chain(nc.vector.tensor_tensor(tiles[:], end[:], tiles[:], ALU.subtract))
            chain(nc.vector.tensor_scalar(tiles[:], tiles[:], float(P), None, ALU.mult))
            chain(nc.vector.tensor_tensor(place[:], place[:], tiles[:].unsqueeze(1).to_broadcast([P, NT, NE]), ALU.add))
            for k in range(TOP):
                chain(nc.vector.tensor_tensor(picked[:], place[:], chosen[k][:], ALU.mult))
                chain(nc.vector.tensor_reduce(index_f[:, k], picked[:], AX_X, ALU.add))
            chain(nc.vector.tensor_copy(slots[:], index_f[:]))
            chain(nc.vector.tensor_tensor(passed[:], tile_no[:].unsqueeze(2).to_broadcast([1, SLOT_TILES, NE]),
                                          end[0:1].unsqueeze(1).to_broadcast([1, SLOT_TILES, NE]), ALU.is_ge))
            chain(nc.vector.tensor_reduce(expert_of[:], passed[:], AX_X, ALU.add))
            chain(nc.vector.tensor_scalar(expert_i[:], expert_of[:], float(NE - 1), None, ALU.min))
            chain(nc.vector.tensor_copy(plan[:, 0:SLOT_TILES, 0], expert_i[:]))
            chain(nc.vector.tensor_scalar(plan[:, 0:SLOT_TILES, 1], expert_i[:], 1, None, ALU.bitwise_and))
            chain(nc.vector.tensor_copy(ends[:], end[0:1]))


def feed_forward(nc, tiles, routed, x_res, ident, ln2, shared_w, slots, plan, ends, xg, y, out, weights_out, expert_w):
    mean, rstd = ln2
    sh, sl = shared_w
    t_first, t_n = tiles
    units = SETS * t_n
    r_n = SLOT_TILES if routed else 0
    tag = "a" if routed else "b"
    with ExitStack() as ctx:
        def sb(name, shape, dt=F32):
            return ctx.enter_context(nc.sbuf_tensor(name + tag, shape, dt))

        def psum(name, shape, dt=F32):
            return ctx.enter_context(nc.psum_tensor(name + tag, shape, dt))

        def sem(name):
            return ctx.enter_context(nc.semaphore(name + tag))

        x_in = sb("x_in", [P, 2 if routed else 1, E])
        x_high, x_low = sb("x_high", [P, EC, P], F32R), sb("x_low", [P, EC, P], F32R)
        gated = sb("gated", [P, HID])
        hidden = sb("hidden", [P, HC * P])
        h_high, h_low = sb("h_high", [P, HC, P], F32R), sb("h_low", [P, HC, P], F32R)
        if routed:
            w_high, w_low = sb("w_high", [P, 2, W_COLS], F32R), sb("w_low", [P, 2, W_COLS], F32R)
            stage = sb("stage", [P, 2, UP_AT])
            to_sort = sb("to_sort", [P, 2, E])
            token = sb("token", [P, 1])
            y_out = to_sort
        else:
            y_in = sb("y_in", [P, 2, TOP, E])
            result = sb("result", [P, 2, E])

        ps_x, ps_g, ps_u = psum("ps_x", [P, EC, P]), psum("ps_g", [P, 512]), psum("ps_u", [P, 512])
        ps_h, ps_y = psum("ps_h", [P, HC, P]), psum("ps_y", [P, E])

        x_normed, x_loaded = sem("x_normed"), [sem(f"x_loaded{i}") for i in range(2)]
        x_turned, x_high_ready, x_split = sem("x_turned"), sem("x_high_ready"), sem("x_split")
        up_done, silu_done, hidden_ready = sem("up_done"), sem("silu_done"), sem("hidden_ready")
        h_turned, h_high_ready, h_split = sem("h_turned"), sem("h_high_ready"), sem("h_split")
        down_done, y_read = sem("down_done"), sem("y_read")
        pad_set = sem("pad_set")
        if routed:
            sort_ready, sorted_ = sem("sort_ready"), [sem(f"sorted{i}") for i in range(2)]
            high_loaded, stage_loaded, weights_split = [sem(f"high_loaded{i}") for i in range(PIECES)], [sem(f"stage_loaded{i}") for i in range(2)], sem("weights_split")
            y_stored, buffer_free = [sem(f"y_stored{i}") for i in range(2)], sem("buffer_free")
        else:
            y_loaded = [sem(f"y_loaded{i}") for i in range(2)]
            part_ready, result_ready, stored = sem("part_ready"), sem("result_ready"), [sem(f"stored{i}") for i in range(2)]
        block = ctx.enter_context(nc.Block())

        @block.sync
        def _(sp):
            if routed:
                for par in range(2):
                    sp.wait_ge(sorted_[par], 16 * TOP * NT // 2)

                def load(i, ni):
                    sp.wait_ge(x_turned, t_n + i - 1)
                    sp.dma_start(x_in[:, 1 - ni % 2], xg[bass.ds(i * P, P), :]).then_inc(x_loaded[ni % 2], 16)

                def store(i, ni):
                    sp.wait_ge(y_read, t_n + i + 1)
                    sp.dma_start(y[bass.ds(i * P, P), :], y_out[:, ni % 2]).then_inc(y_stored[ni % 2], 16)

                for i in range(4):
                    load(i, i)
                loops = (r_n - 4) // 2 * 2
                with sp.Fori(0, loops, 2) as i:
                    for par in range(2):
                        load(i + par + 4, par)
                        store(i + par, par)
                for i in range(loops, r_n):
                    if i + 4 < r_n:
                        load(i + 4, i)
                    store(i, i)
                for par in range(2):
                    sp.wait_ge(y_stored[par], 16 * ((r_n + 1 - par) // 2))
            else:
                def store(k, par, t):
                    sp.wait_ge(result_ready, k + 1)
                    sp.dma_start(out[bass.ds(t * P, P), :], result[:, par]).then_inc(stored[par], 16)

                with sp.Fori(0, t_n) as m:
                    store(2 * m, 0, m)
                    store(2 * m + 1, 1, m + t_first)
                for par in range(2):
                    sp.wait_ge(stored[par], 16 * t_n)

        @block.gpsimd
        def _(pool):
            nc.gpsimd.memset(hidden[:, HID:], 0.0).then_inc(pad_set, 1)
            if routed:
                pool.wait_ge(pad_set, 1)
                nc.gpsimd.memset(token[:], 0.0).then_inc(pad_set, 1)
                pool.wait_ge(pad_set, 2)

                def scatter(t, par):
                    pool.wait_ge(sort_ready, t + 1)
                    for k in range(TOP):
                        pool.indirect_dma_start(out=xg[:, :], out_offset=bass.IndirectOffsetOnAxis(ap=slots[:, k, t:t + 1], axis=0),
                                                in_=to_sort[:, par], in_offset=None).then_inc(sorted_[par], 16)

                for t in range(NT):
                    scatter(t, t % 2)

                g, u, d = expert_w
                splitter = Splitter(nc, pool, stage, high_loaded, stage_loaded, weights_split)
                pieces = [piece for e in range(NE) for piece in weight_pieces(g[e], u[e], d[e])]
                for k in range(2):
                    splitter.load_stage(k, pieces[k])
                for e in range(NE):
                    if e >= 2:
                        end = pool.value_load(ends[0:1, e - 2:e - 1], min_val=0, max_val=SLOT_TILES)
                        pool.wait_ge(down_done, end + units)
                        nc.gpsimd.tensor_tensor(token[:], token[:], token[:], ALU.add).then_inc(buffer_free, 1)
                        pool.wait_ge(buffer_free, e - 1)
                    some = range(PIECES * e, PIECES * e + PIECES)
                    for k in some:
                        splitter.load_high(k, pieces[k], w_high[:, e % 2])
                    for k in some:
                        splitter.subtract(k, pieces[k], w_high[:, e % 2], w_low[:, e % 2])
                        if k + 2 < NE * PIECES:
                            splitter.load_stage(k + 2, pieces[k + 2])

            else:
                def gather(k, nk, par, t):
                    if nk >= 2:
                        pool.wait_ge(result_ready, k - 1)
                    for j in range(TOP):
                        pool.indirect_dma_start(out=y_in[:, par, j], out_offset=None, in_=y[:, :],
                                                in_offset=bass.IndirectOffsetOnAxis(ap=slots[:, j, t:t + 1], axis=0)).then_inc(y_loaded[par], 16)

                gather(0, 0, 0, 0)
                gather(1, 1, 1, t_first)
                for m in range(1, t_n):
                    gather(2 * m, 2, 0, m)
                    gather(2 * m + 1, 3, 1, m + t_first)

        @block.scalar
        def _(act):
            def x_part(a):
                act.wait_ge(x_turned, a + 1)
                nc.scalar.activation(x_high[:], ps_x[:], ACT.Copy).then_inc(x_high_ready, 1)

            def silu(q):
                act.wait_ge(up_done, q + 1)
                nc.scalar.activation(gated[:], ps_g[:, 0:HID], ACT.Silu).then_inc(silu_done, 1)

            def h_part(q):
                act.wait_ge(h_turned, q + 1)
                nc.scalar.activation(h_high[:], ps_h[:], ACT.Copy).then_inc(h_high_ready, 1)

            def shared_tile(m, last):
                silu(2 * m)
                h_part(2 * m)
                silu(2 * m + 1)
                if not last:
                    x_part(m + 1)
                h_part(2 * m + 1)

            x_part(0)
            with act.Fori(0, t_n - 1) as m:
                shared_tile(m, False)
            shared_tile(t_n - 1, not routed)
            if routed:
                with act.Fori(0, r_n - 1) as i:
                    silu(units + i)
                    x_part(t_n + i + 1)
                    h_part(units + i)
                silu(units + r_n - 1)
                h_part(units + r_n - 1)

        @block.vector
        def _(dve):
            def normalize(out_ap, t):
                return nc.vector.tensor_scalar(out_ap, x_res[:, bass.ds(t, 1), :].rearrange("p o c -> p (o c)"), mean[:, bass.ds(t, 1)],
                                               rstd[:, bass.ds(t, 1)], ALU.subtract, ALU.mult)

            def x_norm(m, nm):
                if nm >= 1:
                    dve.wait_ge(x_turned, m)
                normalize(x_in[:, 0], m + t_first).then_inc(x_normed, 1)

            def x_part(a):
                dve.wait_ge(x_high_ready, a + 1)
                nc.vector.tensor_tensor(x_low[:], ps_x[:], x_high[:].bitcast(F32), ALU.subtract).then_inc(x_split, 1)

            def hide(q):
                dve.wait_ge(silu_done, q + 1)
                nc.vector.tensor_tensor(hidden[:, 0:HID], ps_u[:, 0:HID], gated[:], ALU.mult).then_inc(hidden_ready, 1)

            def h_part(q):
                dve.wait_ge(h_high_ready, q + 1)
                nc.vector.tensor_tensor(h_low[:], ps_h[:], h_high[:].bitcast(F32), ALU.subtract).then_inc(h_split, 1)

            def to_scatter(m, nm, k):
                if not routed or nm >= NT // 4:
                    return
                t, nt, par = 4 * m + k, 4 * nm + k, k % 2
                if nt >= 2:
                    dve.wait_ge(sorted_[par], 16 * (t - par))
                normalize(to_sort[:, par], t).then_inc(sort_ready, 1)

            def add_shared(m):
                dve.wait_ge(down_done, 2 * m + 2)
                row = x_res[:, bass.ds(m + t_first, 1), :].rearrange("p o c -> p (o c)")
                nc.vector.tensor_tensor(row, row, ps_y[:], ALU.add).then_inc(y_read, 1)

            def combine(k, nk, par, m, t):
                if routed:
                    return
                dve.wait_ge(y_loaded[par], 32 * m + 32)
                if nk >= 2:
                    dve.wait_ge(stored[par], 16 * m)
                row = x_res[:, bass.ds(t, 1), :].rearrange("p o c -> p (o c)")
                nc.vector.scalar_tensor_tensor(out=result[:, par], in0=y_in[:, par, 0], scalar=weights_out[:, bass.ds(t, 1), 0], in1=row,
                                               op0=ALU.mult, op1=ALU.add).then_inc(part_ready, 1)
                dve.wait_ge(part_ready, k + 1)
                nc.vector.scalar_tensor_tensor(out=result[:, par], in0=y_in[:, par, 1], scalar=weights_out[:, bass.ds(t, 1), 1], in1=result[:, par],
                                               op0=ALU.mult, op1=ALU.add).then_inc(result_ready, 1)

            def shared_tile(m, nm):
                last = nm == t_n - 1
                hide(2 * m)
                to_scatter(m, nm, 0)
                if not last:
                    x_norm(m + 1, 1)
                if nm >= 1:
                    add_shared(m - 1)
                h_part(2 * m)
                to_scatter(m, nm, 1)
                if nm >= 1 and not routed:
                    dve.wait_ge(y_read, m)
                    combine(2 * m - 1, nm, 1, m - 1, m - 1 + t_first)
                hide(2 * m + 1)
                to_scatter(m, nm, 2)
                if routed or not last:
                    x_part(m + 1)
                h_part(2 * m + 1)
                to_scatter(m, nm, 3)
                combine(2 * m, 2 * nm, 0, m, m)

            x_norm(0, 0)
            x_part(0)
            shared_tile(0, 0)
            if routed:
                with dve.Fori(1, NT // 4) as m:
                    shared_tile(m, 1)
                with dve.Fori(NT // 4, t_n - 1) as m:
                    shared_tile(m, NT // 4)
            else:
                shared_tile(1, 1)
                with dve.Fori(2, t_n - 1) as m:
                    shared_tile(m, 2)
            shared_tile(t_n - 1, t_n - 1)
            if routed:
                def copy_y(i, ni):
                    dve.wait_ge(down_done, units + i + 1)
                    if ni >= 2:
                        dve.wait_ge(y_stored[ni % 2], 8 * (i - ni % 2))
                    else:
                        dve.wait_ge(sorted_[ni], 16 * TOP * NT // 2)
                    nc.vector.tensor_copy(y_out[:, ni % 2], ps_y[:]).then_inc(y_read, 1)

                def routed_tile(i, ni):
                    hide(units + i)
                    if ni < r_n - 1:
                        x_part(t_n + i + 1)
                    if ni == 0:
                        add_shared(t_n - 1)
                    else:
                        copy_y(i - 1, ni - 1)
                    h_part(units + i)

                for i in range(3):
                    routed_tile(i, i)
                loops = (r_n - 4) // 2 * 2
                with dve.Fori(3, 3 + loops, 2) as i:
                    routed_tile(i, 3)
                    routed_tile(i + 1, 4)
                for i in range(3 + loops, r_n):
                    routed_tile(i, i)
                copy_y(r_n - 1, r_n - 1)
            else:
                add_shared(t_n - 1)
                dve.wait_ge(y_read, t_n)
                combine(2 * t_n - 1, 2, 1, t_n - 1, t_n - 1 + t_first)

        @block.tensor
        def _(pe):
            def turn_x(a, na, buffer=0):
                if na >= 1:
                    pe.wait_ge(x_split, a)
                for c in range(EC):
                    last = nc.tensor.transpose(ps_x[:, c], x_in[:, buffer, c * P:(c + 1) * P], ident[:])
                last.then_inc(x_turned, 1)

            def up(q, nq, a, high, low):
                pe.wait_ge(x_split, a + 1)
                if nq >= 1:
                    pe.wait_ge(hidden_ready, q)
                for bank, at in ((ps_g, 0), (ps_u, UP_AT)):
                    for c in range(EC):
                        cols = slice(at + c * HID, at + (c + 1) * HID)
                        for k, (x_part, w_part) in enumerate(((x_high, high), (x_high, low), (x_low, high))):
                            last = nc.tensor.matmul(bank[:, 0:HID], x_part[:, c], w_part(P, cols), start=(c == 0 and k == 0),
                                                    stop=(c == EC - 1 and k == 2))
                last.then_inc(up_done, 1)

            def turn_h(q, nq):
                pe.wait_ge(hidden_ready, q + 1)
                if nq >= 1:
                    pe.wait_ge(h_split, q)
                for c in range(HC):
                    last = nc.tensor.transpose(ps_h[:, c], hidden[:, c * P:(c + 1) * P], ident[:])
                last.then_inc(h_turned, 1)

            def down(q, high, low, first, final):
                pe.wait_ge(h_split, q + 1)
                for c in range(HC):
                    rows = P if c < HC - 1 else HID_TAIL
                    cols = slice(DOWN_AT + c * E, DOWN_AT + (c + 1) * E)
                    for k, (h_part, w_part) in enumerate(((h_high, high), (h_high, low), (h_low, high))):
                        last = nc.tensor.matmul(ps_y[:], h_part[0:rows, c], w_part(rows, cols), start=(first and c == 0 and k == 0),
                                                stop=(final and c == HC - 1 and k == 2))
                last.then_inc(down_done, 1)

            def shared(s):
                return (lambda rows, cols: sh[0:rows, s, cols]), (lambda rows, cols: sl[0:rows, s, cols])

            def turn_routed(i, ni):
                pe.wait_ge(x_loaded[ni % 2], 8 * (i - ni % 2) + 16)
                turn_x(t_n + i, 1, 1 - ni % 2)

            def shared_tile(m, nm, last):
                up(2 * m, nm, m, *shared(0))
                if nm >= 1:
                    down(2 * m - 1, *shared(1), False, True)
                turn_h(2 * m, nm)
                up(2 * m + 1, 1, m, *shared(1))
                if not last:
                    pe.wait_ge(x_normed, m + 2)
                    turn_x(m + 1, 1)
                elif routed:
                    turn_routed(0, 0)
                if nm >= 1:
                    pe.wait_ge(y_read, m)
                down(2 * m, *shared(0), True, False)
                turn_h(2 * m + 1, 1)

            pe.wait_ge(pad_set, 1)
            pe.wait_ge(x_normed, 1)
            turn_x(0, 0)
            shared_tile(0, 0, False)
            with pe.Fori(1, t_n - 1) as m:
                shared_tile(m, 1, False)
            shared_tile(t_n - 1, 1, True)
            if not routed:
                down(units - 1, *shared(1), False, True)
                return

            def planned(i):
                _, (expert, slot) = nc.values_load_multi_w_load_instructions(plan[0:1, bass.ds(i, 1), :].rearrange("p o k -> p (o k)"),
                                                                           engines=[mybir.EngineType.PE], min_val=0, max_val=NE)
                slot = nc.s_assert_within(slot, 0, 1, skip_runtime_bounds_check_because="the table holds the lowest bit of the expert's number")

                def of(w):
                    return lambda rows, cols: w[0:rows, bass.ds(slot, 1), cols].rearrange("p o c -> p (o c)")

                return expert, of(w_high), of(w_low)

            def routed_up(i, tile):
                expert, high, low = tile
                pe.wait_ge(weights_split, expert * PIECES + 2)
                up(units + i, 1, t_n + i, high, low)

            def routed_down(i, tile):
                expert, high, low = tile
                pe.wait_ge(y_read, t_n + i)
                pe.wait_ge(weights_split, expert * PIECES + PIECES)
                down(units + i, high, low, True, True)

            def routed_step(i, ni):
                if ni >= 1:
                    last_tile = planned(i - 1)
                turn_routed(i + 1, ni + 1)
                if ni >= 1:
                    routed_down(i - 1, last_tile)
                else:
                    down(units - 1, *shared(1), False, True)
                next_tile = planned(i + 1)
                turn_h(units + i, 1)
                routed_up(i + 1, next_tile)

            routed_up(0, planned(0))
            routed_step(0, 0)
            loops = (r_n - 2) // LOOP_TILES * LOOP_TILES
            with pe.Fori(1, 1 + loops, LOOP_TILES) as i:
                for k in range(LOOP_TILES):
                    routed_step(i + k, 1 + k)
            for i in range(1 + loops, r_n - 1):
                routed_step(i, i)
            last_tiles = planned(r_n - 2), planned(r_n - 1)
            routed_down(r_n - 2, last_tiles[0])
            turn_h(units + r_n - 1, 1)
            routed_down(r_n - 1, last_tiles[1])


def build(nc, x, ctx512, gate_w, w_gate, w_up, w_down, sw_gate, sw_up, sw_down, out):
    q_scr = nc.dram_tensor("q_scr", (B, E, TERMS, S), BF16, kind="Internal").ap()
    k_scr = nc.dram_tensor("k_scr", (B, KV * D, TERMS, S), BF16, kind="Internal").ap()
    xg = nc.dram_tensor("x_sorted", (SLOT_ROWS, E), F32, kind="Internal").ap()
    y = nc.dram_tensor("y_sorted", (SLOT_TILES * P, E), F32, kind="Internal").ap()
    with ExitStack() as ctx:
        def sb(name, shape, dt=F32):
            return ctx.enter_context(nc.sbuf_tensor(name, shape, dt))

        x_res = sb("x_res", [P, NT, E])
        ident = sb("ident", [P, P])
        ident_bf = sb("ident_bf", [P, P], BF16)
        mean2, rstd2 = sb("mean2", [P, NT]), sb("rstd2", [P, NT])
        top_w = sb("top_w", [P, NT, TOP])
        slots = sb("slots", [P, TOP, NT], U32)
        plan, ends = sb("plan", [1, SLOT_TILES + LOOP_TILES, 2], I32), sb("ends", [1, NE], I32)
        sh, sl = sb("shared_high", [P, SETS, W_COLS], F32R), sb("shared_low", [P, SETS, W_COLS], F32R)

        attention(nc, x_res, ident, ident_bf, x, ctx512, q_scr, k_scr, xg, sh, sl, (sw_gate, sw_up, sw_down))
        gating(nc, x_res, ident, gate_w, (mean2, rstd2), top_w, slots, plan, ends)
        feed_forward(nc, (0, NA), True, x_res, ident, (mean2, rstd2), (sh, sl), slots, plan, ends, xg, y, None, top_w, (w_gate, w_up, w_down))
        feed_forward(nc, (NA, NT - NA), False, x_res, ident, (mean2, rstd2), (sh, sl), slots, plan, ends, xg, y,
                     out.rearrange("b s e -> (b s) e"), top_w, None)


_INS = ["x", "ctx_512", "L0_ffn_gate_w", "L0_ffn_w_gate", "L0_ffn_w_up", "L0_ffn_w_down", "L0_ffn_sw_gate", "L0_ffn_sw_up", "L0_ffn_sw_down"]


def kernel(**inputs):
    import numpy as _np
    import concourse.bacc as _bacc
    from concourse import mybir as _mybir
    from concourse.bass_utils import run_bass_kernel_spmd as _run

    nc = _bacc.Bacc("TRN2", target_bir_lowering=False, num_devices=1)
    arrays, args = {}, []
    for name in _INS:
        a = _np.ascontiguousarray(inputs[name])
        arrays[f"in_{name}_dram"] = a
        args.append(nc.dram_tensor(f"in_{name}_dram", a.shape, _mybir.dt.from_np(a.dtype), kind="ExternalInput").ap())
    out = nc.dram_tensor("out_dram", (B, S, E), _mybir.dt.float32, kind="ExternalOutput").ap()
    build(nc, *args, out)
    r = _run(nc, [arrays], core_ids=[0])
    return r.results[0]["out_dram"]
```

```python
from contextlib import ExitStack

import concourse.bass as bass
from concourse import mybir

P = 128
F32 = mybir.dt.float32
F32R = mybir.dt.float32r
BF16 = mybir.dt.bfloat16
I32 = mybir.dt.int32
U32 = mybir.dt.uint32
ALU = mybir.AluOpType
ACT = mybir.ActivationFunctionType
AX_X = mybir.AxisListType.X

B, S, E = 8, 256, 512
KV, G, D = 8, 4, 16
H = KV * G
T = B * S
NT = T // P
ST = S // P
EC = E // P
HALF = KV // 2
SCALE = 1.0 / D ** 0.5
EPS = 1e-5
RSQRT_SEED = float(0x5F3759DF)
NEWTON = 3

NE, TOP, HID = 8, 2, 352
SETS = 2
HC = 3
HID_TAIL = HID - (HC - 1) * P
UP_AT, DOWN_AT = EC * HID, 2 * EC * HID
W_COLS = DOWN_AT + HC * E
PIECES = 4
SLOT_TILES = (TOP * T) // P + NE - 1
LOOP_TILES = 4
ZERO_TILES = -(-SLOT_TILES // B)
SLOT_ROWS = ZERO_TILES * B * P
NA = NT // 2
SORT_AT = 3
SORT_TILES = NT // 4

Q_PART = (0, 1, 2, 0, 1, 0)
K_PART = (0, 0, 0, 1, 1, 2)
TERMS = len(Q_PART)
Q_RUNS = ((0, 3, 0, 1), (0, 2, 3, 1), (0, 1, 5, 1))
K_RUNS = ((0, 1, 0, 3), (1, 1, 3, 2), (2, 1, 5, 1))
ROWS = TERMS * D
ROWS_MAX = ROWS + 2

RSQRT_STEPS = 3 + 3 * NEWTON


def rsqrt_step(eng, i, out, variance, v, t):
    if i == 0:
        return eng.tensor_scalar(v, variance, EPS, None, ALU.add)
    if i == 1:
        return eng.tensor_scalar(out.bitcast(I32), v.bitcast(I32), -0.5, RSQRT_SEED, ALU.mult, ALU.add)
    if i == 2:
        return eng.tensor_scalar(v, v, -0.5, None, ALU.mult)
    if i % 3 == 0:
        return eng.tensor_tensor(t, out, out, ALU.mult)
    if i % 3 == 1:
        return eng.tensor_tensor(t, t, v, ALU.mult)
    return eng.scalar_tensor_tensor(out=out, in0=t, scalar=1.5, in1=out, op0=ALU.add, op1=ALU.mult)


def each_batch(eng, body):
    body(0, 0)
    with eng.Fori(1, 4, 2) as i:
        body(i, 1)
        body(i + 1, 2)
    for b in (5, 6, 7):
        body(b, b)


GROUP = 4
ROUTED_IN_TURN = 2 * GROUP
STATS_BEFORE = 6
SPLIT_TURNS = (5, 6, 7)


JOBS = (
    (0, "max_b", 0),
    (1, "query_0", 2),
    (3, "query_1", 2),
    (4, "key", 2),
    (6, "out_b0", -1),
    (7, "out_b1", -1),
    (8, "max_a", 1),
    (12, "out_a0", 0),
    (13, "out_a1", 0),
)
FIRST_JOBS = (("key", 0), ("query_0", 0), ("query_1", 0), ("query_0", 1), ("query_1", 1), ("key", 1))
LAST_JOBS = (("out_b0", B - 1), ("out_b1", B - 1))


def job_at(slot, n):
    for s, job, away in JOBS:
        if s == slot and 0 <= n + away < B:
            return job, away
    return None, 0


def job_before(slot, n):
    here = [(job, away) for s, job, away in JOBS if s < slot and 0 <= n + away < B]
    if here:
        return here[-1]
    if n == 0:
        return "max_a", 0
    there = [(job, away - 1) for _, job, away in JOBS if 0 <= n - 1 + away < B]
    return there[-1]


def attention(nc, x_res, ident, ident_bf, ln2, x, ctx512, q_scr, k_scr, xg, sh, sl, shared_src, gate_w, exps):
    mean2, rstd2 = ln2
    x_dram = x.rearrange("b (t p) e -> b p t e", p=P)
    ctx_dram = ctx512.rearrange("b (t p) e -> b p t e", p=P)

    with ExitStack() as ctx:
        def sb(name, shape, dt=F32):
            return ctx.enter_context(nc.sbuf_tensor(name, shape, dt))

        def psum(name, shape, dt=F32):
            return ctx.enter_context(nc.psum_tensor(name, shape, dt))

        def sem(name):
            return ctx.enter_context(nc.semaphore(name))

        stats = sb("stats", [P, NT, 6])
        mean_var = sb("mean_var", [P, NT, 2])
        rstd = sb("rstd", [P, NT])
        var = sb("var", [P, NT])
        newton = sb("newton", [P, NT])
        xn = sb("xn", [P, ST, E])
        q_part = sb("q_part", [P, 2, EC, 3, S], BF16)
        q_rest = sb("q_rest", [P, EC, P])
        k_part = sb("k_part", [P, 3, S], BF16)
        k_rest = sb("k_rest", [P, S])
        ctx_cur = sb("ctx_cur", [P, 2, ST, KV * D])
        q_stack = sb("q_stack", [ROWS_MAX, 2, H, S], BF16)
        k_stack = sb("k_stack", [ROWS_MAX, 2, KV, S], BF16)
        v_aug = sb("v_aug", [P, 2, ST, KV, 32])
        maxes = sb("maxes", [P, 2, ST, HALF * G])
        max_part = sb("max_part", [P, ST, 2, HALF * G], BF16)
        max_rows = sb("max_rows", [2 * HALF * G, S], BF16)
        probs = sb("probs", [P, 2, ST, G, S])
        out_t = sb("out_t", [P, 2, HALF, S])
        rden = sb("rden", [P, HALF * G])
        out_norm = sb("out_norm", [P, 2, HALF * G * D])

        stage = sb("sh_stage", [P, 2, UP_AT])
        zero = sb("zero", [P, E // 4])

        router_w = k_part[:].rearrange("p t s -> p (t s)").bitcast(F32)[:, 0:EC * 32].rearrange("p (c e) -> p c e", e=32)
        x_turned = [buffer[:, 0:EC * GROUP * P].rearrange("p (c s) -> p c s", c=EC) for buffer in
                    (q_part[:].rearrange("p a c t s -> p (a c t s)").bitcast(F32), stage[:].rearrange("p a c -> p (a c)"))]
        logits_t = ctx_cur[:].rearrange("p a t e -> p (a t e)")

        ps_score = psum("ps_score", [P, 2, G, S])
        ps_max = psum("ps_max", [P, 2, 2, S])
        ps_out = psum("ps_out", [P, 2, S])
        ps_job = psum("ps_job", [P, 4 * P])
        ps_job_bf = ps_job[:].bitcast(BF16)

        def job_bank(job, n):
            if n >= 2:
                return ps_job[:]
            if job == "key":
                return (ps_job[:], ps_out[:].rearrange("p a s -> p (a s)"))[n]
            st = int(job[-1])
            return ps_score[:, n, 2 * st:2 * st + 2, :].rearrange("p a s -> p (a s)")

        x_first, x_rest = [sem(f"x_first{b}") for b in range(2)], sem("x_rest")
        ctx_loaded = [sem(f"ctx_loaded{i}") for i in range(2)]
        ln_step = sem("ln_step")
        late_rstd, centred = sem("late_rstd"), sem("centred")
        ones_set = sem("ones_set")
        zero_set, cleared, ident_set = sem("zero_set"), sem("cleared"), sem("ident_set")
        high_loaded, stage_loaded, weights_split = [sem(f"sh_high_loaded{i}") for i in range(PIECES)], [sem(f"sh_stage_loaded{i}") for i in range(2)], sem("sh_split")
        xn_ready = [sem(f"xn_ready{i}") for i in range(ST)]
        names = [job for _, job, _ in JOBS]
        job_done = {j: sem("done_" + j) for j in names}
        job_read = {j: sem("read_" + j) for j in names if not j.startswith("out")}
        q_high = [sem(f"q_high{i}") for i in range(ST)]
        k_high = sem("k_high")
        q_split = sem("q_split")
        k_split = sem("k_split")
        q_middle, k_middle = sem("q_middle"), sem("k_middle")
        parts_written = sem("parts_written")
        stack_ready = [sem(f"stack_ready{i}") for i in range(2)]
        v_ready = sem("v_ready")
        max_scored = sem("max_scored")
        max_taken = sem("max_taken")
        first_scored, first_taken = sem("first_scored"), sem("first_taken")
        max_split = sem("max_split")
        max_sent = [sem(f"max_sent{i}") for i in range(2)]
        max_step = sem("max_step")
        scored = sem("scored")
        exp_done = sem("exp_done")
        weighted = sem("weighted")
        out_copied = sem("out_copied")
        rden_ready = sem("rden_ready")
        normed = sem("normed")
        added = sem("added")
        weights_cleared, router_loaded, token_normed, token_turned = (sem("router_" + s) for s in ("cleared", "loaded", "normed", "turned"))
        turned_copied, late_copied, projected, logits_copied = (sem("router_" + s) for s in ("copied", "late_copied", "projected", "logits"))
        turned_back, logits_ready, max_subtracted, exps_ready = (sem("router_" + s) for s in ("back", "ready", "max", "exps"))

        def router_bank(t):
            bank = ps_score[:, 0, 0:2, :] if t > ROUTED_IN_TURN and t % 2 else ps_max[:, 0]
            return bank.rearrange("p a s -> p (a s)")

        logits_bank = ps_max[:, 1].rearrange("p a s -> p (a s)")

        def turned_tile(t):
            return x_turned[t // GROUP % 2][:, :, t % GROUP * P:(t % GROUP + 1) * P]

        block = ctx.enter_context(nc.Block())

        def job_index(job):
            return (0 if job[4] == "a" else 1), int(job[5])

        @block.sync
        def _(sp):
            for b in range(2):
                sp.dma_start(x_res[:, ST * b:ST * b + ST, :], x_dram[b]).then_inc(x_first[b], 16)
                sp.dma_start(ctx_cur[:, b], ctx_dram[b]).then_inc(ctx_loaded[b], 16)
            for b in range(2, B):
                sp.dma_start(x_res[:, ST * b:ST * b + ST, :], x_dram[b]).then_inc(x_rest, 16)

            def write_parts(b, n):
                if n >= 1:
                    write_queries(b, n)
                sp.wait_ge(k_split, b + 1)
                for part, _, term, times in K_RUNS:
                    sp.dma_start(k_scr[bass.ds(b, 1)].rearrange("o p t s -> p (o t) s")[:, term:term + times],
                                 k_part[:, part:part + 1].to_broadcast([P, times, S])).then_inc(parts_written, 16)
                if n == 0:
                    write_queries(b, n)

            def write_queries(b, n):
                sp.wait_ge(q_split, 2 * b + 2)
                for part, n_parts, term, _ in Q_RUNS:
                    sp.dma_start(q_scr[bass.ds(b, 1)].rearrange("o (c p) t s -> p (o c) t s", p=P)[:, :, term:term + n_parts],
                                 q_part[:, n % 2, :, part:part + n_parts]).then_inc(parts_written, 16)

            def read_stack(b, n, half):
                free = 16 * (b - 2) + 8 * half + 8
                if n >= 2 and not isinstance(b, int):
                    free = sp.snap(free)
                if half == 0:
                    sp.wait_ge(parts_written, 96 * b + 96)
                if n >= 2:
                    sp.wait_ge(scored, free)
                heads = slice(half * HALF * G, (half + 1) * HALF * G)
                kvs = slice(half * HALF, (half + 1) * HALF)
                sp.dma_start(q_stack[0:ROWS, n % 2, heads, :],
                             q_scr[bass.ds(b, 1)].rearrange("o (h d) t s -> (d t) (o h) s", d=D)[:, heads]).then_inc(stack_ready[half], 16)
                sp.dma_start(k_stack[0:ROWS, n % 2, kvs, :],
                             k_scr[bass.ds(b, 1)].rearrange("o (h d) t s -> (d t) (o h) s", d=D)[:, kvs]).then_inc(stack_ready[half], 16)

            def send_max(b, n, half):
                sp.wait_ge(job_read["max_a" if half == 0 else "max_b"], b + 1)
                sp.dma_start(q_stack[ROWS:ROWS_MAX, n % 2, half * HALF * G:(half + 1) * HALF * G, :],
                             max_rows[:]).then_inc(max_sent[half], 16)

            for b in range(2):
                write_parts(b, b)
                if b == 1:
                    send_max(0, 0, 0)
                for half in range(2):
                    read_stack(b, b, half)

            def turn(b, n):
                send_max(b, n, 1)
                if n + 2 < B:
                    sp.wait_ge(job_done["key"], b + 1)
                    sp.wait_ge(v_ready, b + 1)
                    sp.dma_start(ctx_cur[:, n % 2], ctx_dram[bass.ds(b + 2, 1)].rearrange("o p t e -> p (o t) e")).then_inc(ctx_loaded[n % 2], 16)
                    write_parts(b + 2, n + 2)
                    read_stack(b + 2, n + 2, 0)
                if n + 1 < B:
                    send_max(b + 1, n + 1, 0)
                if n + 2 < B:
                    read_stack(b + 2, n + 2, 1)
                sp.dma_start(xg[bass.ds(b * ZERO_TILES * P, ZERO_TILES * P), :].rearrange("(p t) (f e) -> p (t f) e", p=P, f=4),
                             zero[:].unsqueeze(1).to_broadcast([P, 4 * ZERO_TILES, E // 4])).then_inc(cleared, 16)

            sp.wait_ge(zero_set, 1)
            each_batch(sp, turn)
            sp.wait_ge(weights_cleared, 1)
            sp.dma_start(router_w[:, :, 0:NE], gate_w.rearrange("(c p) e -> p c e", p=P)).then_inc(router_loaded, 16)
            sp.wait_ge(cleared, 16 * B)

        @block.gpsimd
        def _(pool):
            for m in (ident, ident_bf):
                nc.gpsimd.memset(m[:], 0.0).then_inc(ident_set, 1)
            pool.wait_ge(ident_set, 2)
            for m in (ident, ident_bf):
                nc.gpsimd.affine_select(out=m[:], in_=m[:], compare_op=ALU.not_equal, fill=1.0, base=0, pattern=[[-1, P]],
                                        channel_multiplier=1).then_inc(ident_set, 1)
            nc.gpsimd.memset(zero[:], 0.0).then_inc(zero_set, 1)
            nc.gpsimd.memset(v_aug[:], 0.0).then_inc(ones_set, 1)
            pool.wait_ge(ones_set, 1)
            nc.gpsimd.memset(v_aug[:, :, :, :, D:D + 1], 1.0).then_inc(ones_set, 1)
            pool.wait_ge(ones_set, 2)
            nc.gpsimd.memset(k_stack[ROWS:ROWS_MAX], 1.0).then_inc(ones_set, 1)

            def split_queries(b, n, st):
                tokens = slice(st * P, (st + 1) * P)
                pool.wait_ge(job_read[f"query_{st}"], b + 1)
                if n >= 2:
                    pool.wait_ge(parts_written, 96 * b - 96)
                nc.gpsimd.tensor_tensor(q_part[:, n % 2, :, 1, tokens], q_rest[:], zero[:, 0:1].unsqueeze(2).to_broadcast([P, EC, P]), ALU.add).then_inc(q_middle, 1)
                pool.wait_ge(q_middle, 2 * b + st + 1)
                nc.gpsimd.tensor_tensor(q_part[:, n % 2, :, 2, tokens], q_rest[:], q_part[:, n % 2, :, 1, tokens], ALU.subtract).then_inc(q_split, 1)

            def normalize(b, n, st):
                pool.wait_ge(job_done[f"query_{st}"], b)
                if n >= 2 * ST:
                    pool.wait_ge(late_rstd, 1)
                t = ST * b + st
                nc.gpsimd.tensor_tensor(xn[:, st], x_res[:, bass.ds(t, 1), :].rearrange("p o c -> p (o c)"),
                                        mean_var[:, bass.ds(t, 1), 0].to_broadcast([P, E]), ALU.subtract).then_inc(centred, 1)
                pool.wait_ge(centred, t - 3 * ST + 1)
                nc.gpsimd.tensor_tensor(xn[:, st], xn[:, st], rstd[:, bass.ds(t, 1)].to_broadcast([P, E]), ALU.mult).then_inc(xn_ready[st], 1)

            def split_keys(b, n):
                pool.wait_ge(job_read["key"], b + 1)
                if n >= 1:
                    pool.wait_ge(parts_written, 96 * b)
                nc.gpsimd.tensor_tensor(k_part[:, 1], k_rest[:], zero[:, 0:1].to_broadcast([P, S]), ALU.add).then_inc(k_middle, 1)
                pool.wait_ge(k_middle, b + 1)
                nc.gpsimd.tensor_tensor(k_part[:, 2], k_rest[:], k_part[:, 1], ALU.subtract).then_inc(k_split, 1)

            def values(b, n):
                pool.wait_ge(ctx_loaded[n % 2], 8 * (b - n % 2) + 16)
                if n >= 2:
                    pool.wait_ge(weighted, 8 * (b - 1))
                for tc in range(ST):
                    now = ctx_cur[:, n % 2, tc].rearrange("p (k d) -> p k d", d=D)
                    last = nc.gpsimd.tensor_tensor(v_aug[:, n % 2, tc, :, 0:D], now, zero[:, 0:1].unsqueeze(2).to_broadcast([P, KV, D]), ALU.add)
                last.then_inc(v_ready, 1)

            def add_out(b, n, half, st):
                k = 2 * half + st
                pool.wait_ge(normed, 4 * b + k + 1)
                cols = slice(half * HALF * G * D, (half + 1) * HALF * G * D)
                row = x_res[:, bass.ds(ST * b + st, 1), cols].rearrange("p o c -> p (o c)")
                nc.gpsimd.tensor_tensor(row, row, out_norm[:, st], ALU.add).then_inc(added, 1)

            pool.wait_ge(ones_set, 3)
            splitter = Splitter(nc, pool, stage, high_loaded, stage_loaded, weights_split)
            g, u, d = shared_src
            pieces = []
            for s in range(SETS):
                cols = slice(s * HID, (s + 1) * HID)
                pieces += weight_pieces(g[:, cols], u[:, cols], d[cols, :])

            def shared_weights(n):
                first = 2 * SPLIT_TURNS.index(n) + 2 if n else 0
                for k in (first, first + 1):
                    splitter.subtract(k, pieces[k], sh[:, k // PIECES], sl[:, k // PIECES])
                    if k + 2 < SETS * PIECES:
                        splitter.load_high(k + 2, pieces[k + 2], sh[:, (k + 2) // PIECES])
                        splitter.load_stage(k + 2, pieces[k + 2])

            split_keys(0, 0)
            values(0, 0)
            for st in range(ST):
                split_queries(1, 1, st)
            split_keys(1, 1)
            pool.wait_ge(parts_written, 96 * 2)
            for k in range(2):
                splitter.load_high(k, pieces[k], sh[:, 0])
                splitter.load_stage(k, pieces[k])
            shared_weights(0)

            def turn(b, n):
                if n + 2 < B:
                    split_queries(b + 2, n + 2, 0)
                    split_queries(b + 2, n + 2, 1)
                    split_keys(b + 2, n + 2)
                if n + 3 < B:
                    for st in range(ST):
                        normalize(b + 3, n + 3, st)
                if n + 1 < B:
                    values(b + 1, n + 1)
                if n == B - 1:
                    shared_weights(n)
                if n >= 1:
                    for st in range(ST):
                        add_out(b - 1, n - 1, 1, st)
                if n in SPLIT_TURNS[:-1]:
                    shared_weights(n)
                for st in range(ST):
                    add_out(b, n, 0, st)
            each_batch(pool, turn)
            for st in range(ST):
                add_out(B - 1, B - 1, 1, st)

        @block.scalar
        def _(act):
            def query_high(b, n, st):
                act.wait_ge(job_done[f"query_{st}"], b + 1)
                if n >= 2:
                    act.wait_ge(parts_written, 96 * b - 96)
                nc.scalar.activation(q_part[:, n % 2, :, 0, st * P:(st + 1) * P], job_bank(f"query_{st}", n).rearrange("p (c s) -> p c s", s=P), ACT.Copy).then_inc(q_high[st], 1)

            def key_high(b, n):
                act.wait_ge(job_done["key"], b + 1)
                if n >= 1:
                    act.wait_ge(parts_written, 96 * b)
                nc.scalar.activation(k_part[:, 0], job_bank("key", n)[:, 0:S], ACT.Copy).then_inc(k_high, 1)

            def job(slot, b, n):
                name, away = job_at(slot, n)
                if name in ("query_0", "query_1"):
                    query_high(b + away, n + away, int(name[-1]))
                if name == "key":
                    key_high(b + away, n + away)

            for name, b in FIRST_JOBS:
                if name == "key":
                    key_high(b, b)
                else:
                    query_high(b, b, int(name[-1]))

            def turn(b, n):
                for k in range(KV):
                    g, ng = 8 * b + k, 8 * n + k
                    if k % 2 == 1 and ng >= 3:
                        i = (k - 3) // 2
                        act.wait_ge(weighted, 8 * b + 2 * i + 2)
                        half, nb_away = ((i % 4) // 2, -1 if i < 0 else 0)
                        if n + nb_away >= 1:
                            act.wait_ge(job_done[f"out_{'ab'[half]}1"], b + nb_away)
                        nc.scalar.activation(out_t[:, half, 2 * (i % 2):2 * (i % 2) + 2, :], ps_out[:], ACT.Copy).then_inc(out_copied, 1)
                    for tc in range(ST):
                        u = 2 * g + tc
                        act.wait_ge(scored, u + 1)
                        if ng >= 2:
                            act.wait_ge(weighted, g - 1)
                        nc.scalar.activation(probs[:, k % 2, tc], ps_score[:, tc], ACT.Exp, scale=SCALE).then_inc(exp_done, 1)
                        job(2 * k + tc, b, n)

            each_batch(act, turn)
            act.wait_ge(weighted, KV * B)
            act.wait_ge(job_done["out_b1"], B - 1)
            nc.scalar.activation(out_t[:, 1, 2:4, :], ps_out[:], ACT.Copy).then_inc(out_copied, 1)
            for t in range(ROUTED_IN_TURN, NT):
                act.wait_ge(token_turned, t + 1)
                if t % GROUP == 0:
                    act.wait_ge(projected, t // GROUP - 1)
                nc.scalar.activation(turned_tile(t), router_bank(t).rearrange("p (c s) -> p c s", s=P), ACT.Copy).then_inc(late_copied, 1)
            act.wait_ge(max_subtracted, 1)
            nc.scalar.activation(exps[:], exps[:], ACT.Exp).then_inc(exps_ready, 1)

        @block.vector
        def _(dve):
            done = [0]

            def chain(ins):
                done[0] += 1
                ins.then_inc(ln_step, 1)
                dve.wait_ge(ln_step, done[0])

            def statistics(t0, t1):
                for t in range(t0, t1):
                    nc.vector.bn_stats(stats[:, t], x_res[:, t]).then_inc(ln_step, 1)
                    done[0] += 1
                deviations(t0, t1)

            def deviations(t0, t1, mean_out=None, rstd_out=rstd, beside=None):
                dve.wait_ge(ln_step, done[0])
                for t in range(t0, t1):
                    nc.vector.bn_aggr(mean_var[:, t], stats[:, t]).then_inc(ln_step, 1)
                    done[0] += 1
                dve.wait_ge(ln_step, done[0])
                some = slice(t0, t1)
                if mean_out is not None:
                    chain(nc.vector.tensor_copy(mean_out[:, some], mean_var[:, some, 0]))
                for i in range(RSQRT_STEPS):
                    if beside:
                        beside(i)
                    chain(rsqrt_step(nc.vector, i, rstd_out[:, some], mean_var[:, some, 1], var[:, some], newton[:, some]))

            def normalize(b, n, st):
                if n >= 1:
                    dve.wait_ge(job_done[f"query_{st}"], b)
                t = ST * b + st
                nc.vector.tensor_scalar(xn[:, st], x_res[:, bass.ds(t, 1), :].rearrange("p o c -> p (o c)"), mean_var[:, bass.ds(t, 1), 0],
                                        rstd[:, bass.ds(t, 1)], ALU.subtract, ALU.mult).then_inc(xn_ready[st], 1)

            def query_rest(b, n, st):
                dve.wait_ge(q_high[st], b + 1)
                if n >= 1 or st == 1:
                    dve.wait_ge(q_split, 2 * b + st)
                nc.vector.tensor_tensor(q_rest[:], job_bank(f"query_{st}", n).rearrange("p (c s) -> p c s", s=P), q_part[:, n % 2, :, 0, st * P:(st + 1) * P],
                                        ALU.subtract).then_inc(job_read[f"query_{st}"], 1)

            def key_rest(b, n):
                dve.wait_ge(k_high, b + 1)
                if n >= 1:
                    dve.wait_ge(k_split, b)
                nc.vector.tensor_tensor(k_rest[:], job_bank("key", n)[:, 0:S], k_part[:, 0], ALU.subtract).then_inc(job_read["key"], 1)

            def take_max(b, n, k, st, pairs=(0, 1)):
                for pair in pairs:
                    i = 32 * (b - 1) + 4 * k + 2 * st + pair
                    dve.wait_ge(max_scored, i + 1)
                    h = G * (k % HALF) + 2 * pair
                    nc.vector.tensor_reduce(maxes[:, k // HALF, st, h:h + 2], ps_max[:, pair], AX_X, ALU.max).then_inc(max_taken, 1)

            def take_first_max(k, st):
                dve.wait_ge(first_scored, ST * k + st + 1)
                h = G * (k % HALF)
                nc.vector.tensor_reduce(maxes[:, k // HALF, st, h:h + G], ps_score[:, st], AX_X, ALU.max).then_inc(first_taken, 1)

            def split_max(b, n, half):
                if n == 0:
                    dve.wait_ge(first_taken, ST * HALF * (half + 1))
                else:
                    dve.wait_ge(max_taken, 32 * (b - 1) + 16 * half + 16)
                if half == 1:
                    dve.wait_ge(job_done["max_a"], b + 1)
                elif n >= 1:
                    dve.wait_ge(job_done["max_b"], b)
                nc.vector.tensor_scalar(max_part[:, :, 0], maxes[:, half], -1.0, None, ALU.mult).then_inc(max_step, 1)
                dve.wait_ge(max_step, 2 * b + half + 1)
                nc.vector.scalar_tensor_tensor(out=max_part[:, :, 1], in0=maxes[:, half], scalar=-1.0, in1=max_part[:, :, 0],
                                               op0=ALU.mult, op1=ALU.subtract).then_inc(max_split, 1)

            def max_to_rows(b, n, half):
                name = "max_" + "ab"[half]
                dve.wait_ge(job_done[name], b + 1)
                if half == 1:
                    dve.wait_ge(max_sent[0], 16 * b + 16)
                elif n >= 1:
                    dve.wait_ge(max_sent[1], 16 * b)
                nc.vector.tensor_copy(max_rows[:], ps_job_bf[0:2 * HALF * G, 0:S]).then_inc(job_read[name], 1)

            def normalize_out(b, n, name):
                half, st = job_index(name)
                i = 4 * b + 2 * half + st
                tile = ps_job[:].rearrange("p (h d) -> p h d", d=32)
                dve.wait_ge(job_done[name], b + 1)
                nc.vector.reciprocal(rden[:], tile[:, :, D]).then_inc(rden_ready, 1)
                dve.wait_ge(rden_ready, i + 1)
                if n >= 1 or half == 1:
                    dve.wait_ge(added, i - 1)
                nc.vector.tensor_tensor(out_norm[:, st].rearrange("p (h d) -> p h d", d=D), tile[:, :, 0:D],
                                        rden[:].unsqueeze(2).to_broadcast([P, HALF * G, D]), ALU.mult).then_inc(normed, 1)

            def job(slot, b, n):
                name, away = job_at(slot, n)
                if name is None:
                    return
                b, n = b + away, n + away
                if name.startswith("query"):
                    query_rest(b, n, int(name[-1]))
                elif name == "key":
                    key_rest(b, n)
                elif name.startswith("max"):
                    max_to_rows(b, n, "ab".index(name[-1]))
                else:
                    normalize_out(b, n, name)

            for b in range(2):
                dve.wait_ge(x_first[b], 16)
                statistics(ST * b, ST * b + ST)
                for st in range(ST):
                    normalize(b, b, st)
                if b == 0:
                    key_rest(b, b)
                for st in range(ST):
                    if b == 1 and st == 1:
                        dve.wait_ge(x_rest, 16 * (B - 2))
                        statistics(2 * ST, 4 * ST)
                    query_rest(b, b, st)
                    if b == 0:
                        dve.wait_ge(job_read[f"query_{st}"], 1)
                        middle, low = (q_part[:, 0, :, part, st * P:(st + 1) * P] for part in (1, 2))
                        nc.vector.tensor_copy(middle, q_rest[:]).then_inc(q_middle, 1)
                        dve.wait_ge(q_middle, st + 1)
                        nc.vector.tensor_tensor(low, q_rest[:], middle, ALU.subtract).then_inc(q_split, 1)
            key_rest(1, 1)
            for st in range(ST):
                normalize(2, 2, st)
            for k in range(KV):
                for st in range(ST):
                    take_first_max(k, st)
                if k == HALF - 1:
                    split_max(0, 0, 0)
                if k == HALF:
                    max_to_rows(0, 0, 0)
            split_max(0, 0, 1)

            def bn_stats_2(t):
                dve.wait_ge(added, 4 * (t // ST) + 2 + t % ST + 1)
                nc.vector.bn_stats(stats[:, t], x_res[:, t]).then_inc(ln_step, 1)
                done[0] += 1

            def late_step(i):
                late = slice(4 * ST, NT)
                dve.wait_ge(ln_step, done[0])
                return rsqrt_step(nc.vector, i - 1, rstd[:, late], mean_var[:, late, 1], var[:, late], newton[:, late])

            for t in range(4 * ST, NT):
                nc.vector.bn_stats(stats[:, t], x_res[:, t]).then_inc(ln_step, 1)
                done[0] += 1

            def late_statistics(slot):
                i = slot - (2 * KV - RSQRT_STEPS)
                if i == 0:
                    dve.wait_ge(ln_step, done[0])
                    for t in range(4 * ST, NT):
                        nc.vector.bn_aggr(mean_var[:, t], stats[:, t]).then_inc(ln_step, 1)
                        done[0] += 1
                elif i > 0:
                    late_step(i).then_inc(ln_step, 1)
                    done[0] += 1

            def router_normalize(t):
                if t >= 2:
                    dve.wait_ge(token_turned, t - 1)
                else:
                    dve.wait_ge(job_done[f"query_{t}"], B)
                nc.vector.tensor_scalar(xn[:, t % 2], x_res[:, t], mean2[:, t:t + 1], rstd2[:, t:t + 1], ALU.subtract, ALU.mult).then_inc(token_normed, 1)

            def router_copy(t):
                dve.wait_ge(token_turned, t + 1)
                if t == 0:
                    dve.wait_ge(parts_written, 96 * B)
                if t == GROUP:
                    dve.wait_ge(weights_split, SETS * PIECES)
                nc.vector.tensor_copy(turned_tile(t), router_bank(t).rearrange("p (c s) -> p c s", s=P)).then_inc(turned_copied, 1)

            def router_logits_t(g):
                dve.wait_ge(projected, g + 1)
                if g == 0:
                    dve.wait_ge(job_done["key"], B)
                    dve.wait_ge(v_ready, B)
                else:
                    dve.wait_ge(turned_back, g)
                nc.vector.tensor_copy(logits_t, logits_bank).then_inc(logits_copied, 1)

            def router_logits(g):
                dve.wait_ge(turned_back, g + 1)
                nc.vector.tensor_reduce(exps[:, GROUP * g:GROUP * g + GROUP, :], logits_bank.rearrange("p (j c e) -> p j e c", c=EC, e=32)[:, :, 0:NE],
                                        AX_X, ALU.add).then_inc(logits_ready, 1)

            def router_beside(slot):
                early = NT - 2 * ST
                if slot == 0:
                    dve.wait_ge(parts_written, 96 * B)
                    nc.vector.memset(router_w, 0.0).then_inc(weights_cleared, 1)
                first = STATS_BEFORE + 2 * slot
                if first < early:
                    bn_stats_2(first)
                    bn_stats_2(first + 1)
                if first == early:
                    deviations(0, early, mean2, rstd2)
                first = 2 * KV - ROUTED_IN_TURN
                if slot > first:
                    router_copy(slot - first - 1)
                if slot >= first - 1:
                    router_normalize(slot - first + 1)
                if slot == first + GROUP + 2:
                    router_logits_t(0)
                if slot >= 2 * KV - ST:
                    bn_stats_2(early + slot - (2 * KV - ST))

            def turn(b, n):
                for k in range(KV):
                    for tc in range(ST):
                        slot = 2 * k + tc
                        if n + 1 < B:
                            take_max(b + 1, n + 1, k, tc)
                            job(slot, b, n)
                        else:
                            router_beside(slot)
                            job(slot - 1, b, n)
                        if n == 0:
                            late_statistics(2 * k + tc)
                        if n == B - 2 and 1 <= 2 * k + tc <= STATS_BEFORE:
                            bn_stats_2(2 * k + tc - 1)
                    if n + 1 < B and k % HALF == HALF - 1:
                        split_max(b + 1, n + 1, k // HALF)
                if n == 0:
                    late_step(RSQRT_STEPS).then_inc(late_rstd, 1)

            each_batch(dve, turn)
            router_copy(ROUTED_IN_TURN - 1)
            router_logits(0)
            router_normalize(ROUTED_IN_TURN + 1)
            for st in range(ST):
                normalize_out(B - 1, B - 1, f"out_b{st}")
            router_normalize(ROUTED_IN_TURN + 2)
            router_logits_t(1)
            for t in range(NT - ST, NT):
                bn_stats_2(t)

            def router_meanwhile(i):
                if i == 0:
                    router_normalize(ROUTED_IN_TURN + 3)
                if i == 2 * RSQRT_STEPS // 3:
                    router_logits(1)

            deviations(NT - 2 * ST, NT, mean2, rstd2, beside=router_meanwhile)
            for t in (NT - 4, NT - 3):
                router_normalize(t)
            router_logits_t(2)
            for t in (NT - 2, NT - 1):
                router_normalize(t)
            router_logits(2)
            router_logits_t(3)
            router_logits(3)
            dve.wait_ge(logits_ready, NT // GROUP)
            chain(nc.vector.tensor_reduce(newton[:], exps[:], AX_X, ALU.max))
            nc.vector.tensor_tensor(exps[:], exps[:], newton[:].unsqueeze(2).to_broadcast([P, NT, NE]), ALU.subtract).then_inc(max_subtracted, 1)

        @block.tensor
        def _(pe):
            def bank_free(job, b):
                if job.startswith("out"):
                    half, st = job_index(job)
                    pe.wait_ge(normed, 4 * b + 2 * half + st + 1)
                else:
                    pe.wait_ge(job_read[job], b + 1)

            def do_job(name, b, n):
                if not name.startswith(("max", "out")):
                    bank = job_bank(name, n)
                if name.startswith("query"):
                    st = int(name[-1])
                    pe.wait_ge(xn_ready[st], b + 1)
                    for c in range(EC):
                        last = nc.tensor.transpose(bank[:, c * P:(c + 1) * P], xn[:, st, c * P:(c + 1) * P], ident[:])
                elif name == "key":
                    pe.wait_ge(ctx_loaded[n % 2], 8 * (b - n % 2) + 16)
                    for st in range(ST):
                        last = nc.tensor.transpose(bank[:, st * P:(st + 1) * P], ctx_cur[:, n % 2, st], ident[:])
                elif name.startswith("max"):
                    half = "ab".index(name[-1])
                    pe.wait_ge(max_split, 2 * b + half + 1)
                    for st in range(ST):
                        last = nc.tensor.transpose(ps_job_bf[0:2 * HALF * G, st * P:(st + 1) * P],
                                                   max_part[:, st].rearrange("p a h -> p (a h)"), ident_bf[:])
                else:
                    half, st = job_index(name)
                    pe.wait_ge(out_copied, 4 * b + 2 * half + 2)
                    for kv in range(HALF):
                        last = nc.tensor.transpose(ps_job[:, kv * P:(kv + 1) * P], out_t[:, half, kv, st * P:(st + 1) * P], ident[:])
                last.then_inc(job_done[name], 1)

            def job(slot, b, n):
                name, away = job_at(slot, n)
                if name is None:
                    return
                before, b_away = job_before(slot, n)
                bank_free(before, b + b_away)
                do_job(name, b + away, n + away)

            def score_for_max(b, n, k, st, pairs=(0, 1)):
                if st == 0 and k % HALF == 0 and 0 in pairs:
                    pe.wait_ge(stack_ready[k // HALF], 32 * b + 32)
                for pair in pairs:
                    i, ni = 32 * (b - 1) + 4 * k + 2 * st + pair, 32 * (n - 1) + 4 * k + 2 * st + pair
                    if ni >= 2:
                        pe.wait_ge(max_taken, i - 1)
                    for j in range(2):
                        last = nc.tensor.matmul(ps_max[:, pair, j], q_stack[0:ROWS, n % 2, G * k + 2 * pair + j, st * P:(st + 1) * P],
                                                k_stack[0:ROWS, n % 2, k, :], start=True, stop=True)
                    last.then_inc(max_scored, 1)

            def score(b, n, k, tc):
                u, nu = 16 * b + 2 * k + tc, 16 * n + 2 * k + tc
                if tc == 0 and k % HALF == 0:
                    pe.wait_ge(max_sent[k // HALF], 16 * b + 16)
                if nu >= 2:
                    pe.wait_ge(exp_done, u - 1)
                for pair in range(2):
                    last = nc.tensor.matmul(ps_score[:, tc, 2 * pair:2 * pair + 2, :], k_stack[:, n % 2, k, tc * P:(tc + 1) * P],
                                            q_stack[:, n % 2, G * k + 2 * pair:G * k + 2 * pair + 2, :], start=True, stop=True)
                last.then_inc(scored, 1)

            def weigh(b, n, k, tc):
                pe.wait_ge(exp_done, 16 * b + 2 * k + tc + 1)
                if k == 0 and tc == 0:
                    pe.wait_ge(v_ready, b + 1)
                if k % 2 == 0 and tc == 0 and 8 * n + k >= 2:
                    pe.wait_ge(out_copied, 4 * b + k // 2)
                for j in range(G):
                    last = nc.tensor.matmul(ps_out[32 * j:32 * j + 32, k % 2, :], v_aug[:, n % 2, tc, k, :], probs[:, k % 2, tc, j, :],
                                            start=(tc == 0), stop=(tc == ST - 1))
                if tc == ST - 1:
                    last.then_inc(weighted, 1)

            pe.wait_ge(ident_set, 4)
            for name, b in FIRST_JOBS:
                do_job(name, b, b)
            pe.wait_ge(ones_set, 3)
            for k in range(KV):
                if k % HALF == 0:
                    pe.wait_ge(stack_ready[k // HALF], 32)
                for st in range(ST):
                    if k == 0:
                        for name in ("query_0", "query_1"):
                            bank_free(name, st)
                    else:
                        pe.wait_ge(first_taken, ST * (k - 1) + st + 1)
                    for j in range(G):
                        last = nc.tensor.matmul(ps_score[:, st, j], q_stack[0:ROWS, 0, G * k + j, st * P:(st + 1) * P],
                                                k_stack[0:ROWS, 0, k, :], start=True, stop=True)
                    last.then_inc(first_scored, 1)
                if k == HALF:
                    bank_free("key", 0)
                    do_job("max_a", 0, 0)
            pe.wait_ge(first_taken, ST * KV)
            bank_free("key", 1)

            def router_turn(t):
                pe.wait_ge(token_normed, t + 1)
                if t >= ROUTED_IN_TURN + 2:
                    pe.wait_ge(late_copied, t - ROUTED_IN_TURN - 1)
                elif 1 <= t <= ROUTED_IN_TURN:
                    pe.wait_ge(turned_copied, t)
                bank = router_bank(t)
                for c in range(EC):
                    last = nc.tensor.transpose(bank[:, c * P:(c + 1) * P], xn[:, t % 2, c * P:(c + 1) * P], ident[:])
                last.then_inc(token_turned, 1)

            def project(g):
                if g == 0:
                    pe.wait_ge(router_loaded, 16)
                else:
                    pe.wait_ge(logits_ready, g)
                if GROUP * g < ROUTED_IN_TURN:
                    pe.wait_ge(turned_copied, GROUP * g + GROUP)
                else:
                    pe.wait_ge(late_copied, GROUP * g + GROUP - ROUTED_IN_TURN)
                for c in range(EC):
                    last = nc.tensor.matmul(logits_bank[32 * c:32 * c + 32, :], router_w[:, c], x_turned[g % 2][:, c], start=True, stop=True)
                last.then_inc(projected, 1)

            def turn_back(g):
                pe.wait_ge(logits_copied, g + 1)
                for j in range(GROUP):
                    last = nc.tensor.transpose(logits_bank[:, j * P:(j + 1) * P], logits_t[:, j * P:(j + 1) * P], ident[:])
                last.then_inc(turned_back, 1)

            def router_beside(slot):
                first = 2 * KV - ROUTED_IN_TURN
                if slot >= first:
                    router_turn(slot - first)
                if slot == first + GROUP + 1:
                    project(0)
                if slot == 2 * KV - 1:
                    turn_back(0)

            def turn(b, n):
                for k in range(KV):
                    for tc in range(ST):
                        score(b, n, k, tc)
                        if n + 1 < B:
                            score_for_max(b + 1, n + 1, k, tc, (0,))
                        else:
                            router_beside(2 * k + tc)
                        if k >= 1:
                            weigh(b, n, k - 1, tc)
                        elif n >= 1:
                            weigh(b - 1, n - 1, KV - 1, tc)
                        if n + 1 < B:
                            score_for_max(b + 1, n + 1, k, tc, (1,))
                        job(2 * k + tc, b, n)

            each_batch(pe, turn)
            for tc in range(ST):
                weigh(B - 1, B - 1, KV - 1, tc)
            router_turn(ROUTED_IN_TURN)
            router_turn(ROUTED_IN_TURN + 1)
            for name, b in LAST_JOBS:
                bank_free(*{"out_b0": ("out_a1", B - 1), "out_b1": ("out_b0", B - 1)}[name])
                do_job(name, b, b)
            project(1)
            router_turn(ROUTED_IN_TURN + 2)
            router_turn(ROUTED_IN_TURN + 3)
            turn_back(1)
            project(2)
            router_turn(NT - 4)
            router_turn(NT - 3)
            turn_back(2)
            router_turn(NT - 2)
            router_turn(NT - 1)
            project(3)
            turn_back(3)


def weight_pieces(gate, up, down):
    return (
        (0, P, EC, HID, gate.rearrange("(c p) j -> p c j", p=P)),
        (UP_AT, P, EC, HID, up.rearrange("(c p) j -> p c j", p=P)),
        (DOWN_AT, P, HC - 1, E, down[0:(HC - 1) * P].rearrange("(c p) j -> p c j", p=P)),
        (DOWN_AT + (HC - 1) * E, HID_TAIL, 1, E, down[(HC - 1) * P:HID].rearrange("(c p) j -> p c j", p=HID_TAIL)),
    )


class Splitter:

    def __init__(self, nc, pool, stage, high_loaded, stage_loaded, split):
        self.nc, self.pool, self.stage = nc, pool, stage
        self.high_loaded, self.stage_loaded, self.split = high_loaded, stage_loaded, split

    @staticmethod
    def part(buffer, piece):
        col, rows, chunks, width, _ = piece
        return buffer[0:rows, col:col + chunks * width].rearrange("p (c j) -> p c j", j=width)

    def staged(self, k, piece):
        _, rows, chunks, width, _ = piece
        return self.stage[0:rows, k % 2, 0:chunks * width].rearrange("p (c j) -> p c j", j=width)

    def load_high(self, k, piece, high):
        self.pool.dma_start(self.part(high, piece), piece[4]).then_inc(self.high_loaded[k % PIECES], 16)

    def load_stage(self, k, piece):
        self.pool.dma_start(self.staged(k, piece), piece[4]).then_inc(self.stage_loaded[k % 2], 16)

    def subtract(self, k, piece, high, low):
        self.pool.wait_ge(self.high_loaded[k % PIECES], 16 * (k // PIECES) + 16)
        self.pool.wait_ge(self.stage_loaded[k % 2], 16 * (k // 2) + 16)
        self.nc.gpsimd.tensor_tensor(self.part(low, piece), self.staged(k, piece), self.part(high, piece).bitcast(F32),
                                     ALU.subtract).then_inc(self.split, 1)
        self.pool.wait_ge(self.split, k + 1)


class Routing:

    STEPS = 12

    def __init__(self, nc, region, exps, weights_out, slots, plan, ends, ps_count, count_operands, sems):
        self.nc, self.exps, self.weights_out, self.slots, self.plan, self.ends = nc, exps, weights_out, slots, plan, ends
        self.step, self.const_set, self.mask_ready, self.counted, self.slots_ready, self.plan_ready = sems
        self.before_tile, self.of_tile = (ps_count[:, k].rearrange("p (t e) -> p t e", e=NE) for k in range(2))
        self.ps_count = ps_count
        self.done = 0
        at = 0

        def scratch(shape, dt=F32):
            nonlocal at
            n = 1
            for size in shape:
                n *= size
            words = n if dt != BF16 else n // 2
            view = region[:, at:at + words].bitcast(dt)
            at += words
            if len(shape) == 1:
                return view
            return view.rearrange("p (a b) -> p a b", b=shape[1])

        self.row_sum = scratch([NT])
        self.best = scratch([NT, NE])
        self.index = scratch([NT, NE], U32)
        self.index_f = scratch([TOP, NT])
        self.chosen = [scratch([NT, NE]) for _ in range(TOP)]
        self.mask, self.before, self.ones = count_operands
        self.scan = [scratch([NT, NE]) for _ in range(2)]
        self.place = scratch([NT, NE])
        self.picked = scratch([NT, NE])
        self.tiles_i = scratch([NE], I32)
        self.tiles = scratch([NE])
        self.end_sum = [scratch([NE]) for _ in range(2)]
        self.expert_no = scratch([NE])
        self.tile_no = scratch([SLOT_TILES])
        self.passed = scratch([SLOT_TILES, NE])
        self.expert_of = scratch([SLOT_TILES])
        self.expert_i = scratch([SLOT_TILES], I32)
        self.kept = [scratch([E]) for _ in range(SORT_AT)]

    def constants(self, pool):
        nc, set_ = self.nc, self.const_set
        nc.gpsimd.memset(self.ones, 1.0).then_inc(set_, 1)
        pool.wait_ge(set_, 1)
        nc.gpsimd.affine_select(out=self.before, in_=self.ones, compare_op=ALU.is_gt, fill=0.0, base=0,
                                pattern=[[1, P]], channel_multiplier=-1).then_inc(set_, 1)
        pool.wait_ge(set_, 2)
        nc.gpsimd.iota(self.expert_no, pattern=[[1, NE]], base=0, channel_multiplier=0, allow_small_or_imprecise_dtypes=True).then_inc(set_, 1)
        pool.wait_ge(set_, 3)
        nc.gpsimd.iota(self.tile_no[0:1], pattern=[[1, SLOT_TILES]], base=0, channel_multiplier=0, allow_small_or_imprecise_dtypes=True).then_inc(set_, 1)
        pool.wait_ge(set_, 4)

    def count(self, pe):
        pe.wait_ge(self.mask_ready, 1)
        pe.wait_ge(self.const_set, 2)
        mask = self.mask.rearrange("p t e -> p (t e)")
        self.nc.tensor.matmul(self.ps_count[:, 0], self.before, mask, start=True, stop=True)
        self.nc.tensor.matmul(self.ps_count[:, 1], self.ones, mask, start=True, stop=True).then_inc(self.counted, 1)

    def running_sum(self, dve, buffers, n, doublings):
        for d in doublings:
            away, src, dst = 1 << d, buffers[d % 2], buffers[1 - d % 2]
            self.note(dve, self.nc.vector.tensor_copy(dst[:, 0:away], src[:, 0:away]))
            self.chain(dve, self.nc.vector.tensor_tensor(dst[:, away:n], src[:, away:n], src[:, 0:n - away], ALU.add))

    def note(self, dve, ins):
        self.done += 1
        ins.then_inc(self.step, 1)

    def chain(self, dve, ins):
        self.note(dve, ins)
        dve.wait_ge(self.step, self.done)

    def vector_step(self, dve, k):
        nc = self.nc
        exps, best, index, index_f, chosen, scan, place, tiles = (self.exps, self.best, self.index, self.index_f, self.chosen,
                                                                  self.scan, self.place, self.tiles)
        total, end = scan[(NT.bit_length() - 1) % 2], self.end_sum[(NE.bit_length() - 1) % 2]
        if k == 0:
            self.chain(dve, nc.vector.tensor_reduce(self.row_sum, exps[:], AX_X, ALU.add))
            self.chain(dve, nc.vector.reciprocal(self.row_sum, self.row_sum))
            self.chain(dve, nc.vector.tensor_tensor(exps[:], exps[:], self.row_sum.unsqueeze(2).to_broadcast([P, NT, NE]), ALU.mult))
        elif k == 1:
            for t in range(NT):
                self.note(dve, nc.vector.max(best[:, t], exps[:, t]))
            dve.wait_ge(self.step, self.done)
        elif k == 2:
            for t in range(NT):
                self.note(dve, nc.vector.max_index(index[:, t], best[:, t], exps[:, t]))
            dve.wait_ge(self.step, self.done)
        elif k == 3:
            self.note(dve, nc.vector.tensor_copy(self.weights_out[:], best[:, :, 0:TOP]))
            self.chain(dve, nc.vector.tensor_copy(index_f, index[:, :, 0:TOP].rearrange("p t k -> p k t")))
            dve.wait_ge(self.const_set, 4)
            for c in range(TOP):
                self.chain(dve, nc.vector.tensor_tensor(chosen[c], self.expert_no.unsqueeze(1).to_broadcast([P, NT, NE]),
                                                        index_f[:, c].unsqueeze(2).to_broadcast([P, NT, NE]), ALU.is_equal))
            nc.vector.tensor_tensor(self.mask, chosen[0], chosen[1], ALU.add).then_inc(self.mask_ready, 1)
        elif k == 4:
            dve.wait_ge(self.counted, 1)
            self.chain(dve, nc.vector.tensor_copy(scan[0], self.of_tile))
            self.running_sum(dve, scan, NT, (0, 1))
        elif k == 5:
            self.running_sum(dve, scan, NT, range(2, NT.bit_length() - 1))
        elif k == 6:
            self.chain(dve, nc.vector.tensor_tensor(place, total, self.of_tile, ALU.subtract))
            self.chain(dve, nc.vector.tensor_tensor(place, place, self.before_tile, ALU.add))
            self.chain(dve, nc.vector.tensor_scalar(self.tiles_i, total[:, NT - 1], float(P - 1), None, ALU.add))
            self.chain(dve, nc.vector.tensor_scalar(self.tiles_i, self.tiles_i, P.bit_length() - 1, None, ALU.logical_shift_right))
            self.chain(dve, nc.vector.tensor_scalar(tiles, self.tiles_i, 1.0, None, ALU.max))
        elif k == 7:
            self.chain(dve, nc.vector.tensor_copy(self.end_sum[0], tiles))
            self.running_sum(dve, self.end_sum, NE, range(NE.bit_length() - 1))
        elif k == 8:
            self.chain(dve, nc.vector.tensor_tensor(tiles, end, tiles, ALU.subtract))
            self.chain(dve, nc.vector.tensor_scalar(tiles, tiles, float(P), None, ALU.mult))
            self.chain(dve, nc.vector.tensor_tensor(place, place, tiles.unsqueeze(1).to_broadcast([P, NT, NE]), ALU.add))
        elif k == 9:
            for c in range(TOP):
                self.chain(dve, nc.vector.tensor_tensor(self.picked, place, chosen[c], ALU.mult))
                self.chain(dve, nc.vector.tensor_reduce(index_f[:, c], self.picked, AX_X, ALU.add))
            nc.vector.tensor_copy(self.slots[:], index_f).then_inc(self.slots_ready, 1)
        elif k == 10:
            passed, expert_of, expert_i = (a[0:1] for a in (self.passed, self.expert_of, self.expert_i))
            self.chain(dve, nc.vector.tensor_tensor(passed, self.tile_no[0:1].unsqueeze(2).to_broadcast([1, SLOT_TILES, NE]),
                                                    end[0:1].unsqueeze(1).to_broadcast([1, SLOT_TILES, NE]), ALU.is_ge))
            self.chain(dve, nc.vector.tensor_reduce(expert_of, passed, AX_X, ALU.add))
            self.chain(dve, nc.vector.tensor_scalar(expert_i, expert_of, float(NE - 1), None, ALU.min))
        else:
            plan, expert_i = self.plan, self.expert_i[0:1]
            nc.vector.tensor_copy(plan[:, 0:SLOT_TILES, 0], expert_i).then_inc(self.plan_ready, 1)
            nc.vector.tensor_scalar(plan[:, 0:SLOT_TILES, 1], expert_i, 1, None, ALU.bitwise_and).then_inc(self.plan_ready, 1)
            nc.vector.tensor_copy(self.ends[:], end[0:1]).then_inc(self.plan_ready, 1)


def feed_forward(nc, tiles, routed, exps, x_res, ident, ln2, shared_w, slots, plan, ends, xg, y, y_stored, out, weights_out, expert_w):
    mean, rstd = ln2
    sh, sl = shared_w
    t_first, t_n = tiles
    units = SETS * t_n
    r_n = SLOT_TILES if routed else 0
    tag = "a" if routed else "b"
    with ExitStack() as ctx:
        def sb(name, shape, dt=F32):
            return ctx.enter_context(nc.sbuf_tensor(name + tag, shape, dt))

        def psum(name, shape, dt=F32):
            return ctx.enter_context(nc.psum_tensor(name + tag, shape, dt))

        def sem(name):
            return ctx.enter_context(nc.semaphore(name + tag))

        x_in = sb("x_in", [P, 2 if routed else 1, E])
        x_high, x_low = sb("x_high", [P, EC, P], F32R), sb("x_low", [P, EC, P], F32R)
        gated = sb("gated", [P, HID])
        hidden = sb("hidden", [P, HC * P])
        h_high, h_low = sb("h_high", [P, HC, P], F32R), sb("h_low", [P, HC, P], F32R)
        if routed:
            w_high, w_low = sb("w_high", [P, 2, W_COLS], F32R), sb("w_low", [P, 2, W_COLS], F32R)
            stage = sb("stage", [P, 2, UP_AT])
            to_sort = sb("to_sort", [P, 2, E])
            token = sb("token", [P, 1])
            y_out = to_sort
        else:
            y_in = sb("y_in", [P, 2, TOP, E])
            result = sb("result", [P, 2, E])
            arrived = sb("arrived", [P, 1])

        def tokens(nm):
            return routing.kept[nm] if routed and nm < SORT_AT else x_in[:, 0]

        ps_x, ps_g, ps_u = psum("ps_x", [P, EC, P]), psum("ps_g", [P, 512]), psum("ps_u", [P, 512])
        ps_h, ps_y = psum("ps_h", [P, HC, P]), psum("ps_y", [P, E])

        x_normed, x_loaded = sem("x_normed"), [sem(f"x_loaded{i}") for i in range(2)]
        x_turned, x_high_ready, x_split = sem("x_turned"), sem("x_high_ready"), sem("x_split")
        up_done, silu_done, hidden_ready = sem("up_done"), sem("silu_done"), sem("hidden_ready")
        h_turned, h_high_ready, h_split = sem("h_turned"), sem("h_high_ready"), sem("h_split")
        down_done, y_read = sem("down_done"), sem("y_read")
        pad_set = sem("pad_set")
        if routed:
            ps_count = psum("ps_count", [P, 2, NT * NE])
            slots_ready, plan_ready = sem("slots_ready"), sem("plan_ready")
            count_operands = [sb(name, shape, BF16)[:] for name, shape in (("mask", [P, NT, NE]), ("before", [P, P]), ("ones", [P, P]))]
            sems = tuple(sem(name) for name in ("routing_step", "const_set", "mask_ready", "counted")) + (slots_ready, plan_ready)
            routing = Routing(nc, w_low[:, 1].bitcast(F32), exps, weights_out, slots, plan, ends, ps_count, count_operands, sems)
            sort_ready, sorted_ = sem("sort_ready"), [sem(f"sorted{i}") for i in range(2)]
            high_loaded, stage_loaded, weights_split = [sem(f"high_loaded{i}") for i in range(PIECES)], [sem(f"stage_loaded{i}") for i in range(2)], sem("weights_split")
            buffer_free = sem("buffer_free")
        else:
            y_loaded = [sem(f"y_loaded{i}") for i in range(2)]
            part_ready, result_ready, stored = sem("part_ready"), sem("result_ready"), [sem(f"stored{i}") for i in range(2)]
        block = ctx.enter_context(nc.Block())

        @block.sync
        def _(sp):
            if routed:
                for par in range(2):
                    sp.wait_ge(sorted_[par], 16 * TOP * NT // 2)

                def load(i, ni):
                    sp.wait_ge(x_turned, t_n + i - 1)
                    sp.dma_start(x_in[:, 1 - ni % 2], xg[bass.ds(i * P, P), :]).then_inc(x_loaded[ni % 2], 16)

                def store(i, ni):
                    sp.wait_ge(y_read, t_n + i + 1)
                    sp.dma_start(y[bass.ds(i * P, P), :], y_out[:, ni % 2]).then_inc(y_stored[ni % 2], 16)

                for i in range(4):
                    load(i, i)
                loops = (r_n - 4) // 2 * 2
                with sp.Fori(0, loops, 2) as i:
                    for par in range(2):
                        load(i + par + 4, par)
                        store(i + par, par)
                for i in range(loops, r_n):
                    if i + 4 < r_n:
                        load(i + 4, i)
                    store(i, i)
            else:
                def store(k, par, t):
                    sp.wait_ge(result_ready, k + 1)
                    sp.dma_start(out[bass.ds(t * P, P), :], result[:, par]).then_inc(stored[par], 16)

                with sp.Fori(0, t_n) as m:
                    store(2 * m, 0, m)
                    store(2 * m + 1, 1, m + t_first)
                for par in range(2):
                    sp.wait_ge(stored[par], 16 * t_n)

        @block.gpsimd
        def _(pool):
            nc.gpsimd.memset(hidden[:, HID:], 0.0).then_inc(pad_set, 1)
            if routed:
                pool.wait_ge(pad_set, 1)
                nc.gpsimd.memset(token[:], 0.0).then_inc(pad_set, 1)
                pool.wait_ge(pad_set, 2)
                routing.constants(pool)

                def scatter(t, par):
                    if t < SORT_AT:
                        pool.wait_ge(x_normed, t + 1)
                    else:
                        pool.wait_ge(sort_ready, t - SORT_AT + 1)
                    tile = routing.kept[t] if t < SORT_AT else to_sort[:, par]
                    for k in range(TOP):
                        pool.indirect_dma_start(out=xg[:, :], out_offset=bass.IndirectOffsetOnAxis(ap=slots[:, k, t:t + 1], axis=0),
                                                in_=tile, in_offset=None).then_inc(sorted_[par], 16)

                splitter = Splitter(nc, pool, stage, high_loaded, stage_loaded, weights_split)
                g, u, d = expert_w
                pieces = [piece for e in range(NE) for piece in weight_pieces(g[e], u[e], d[e])]

                def load_high(e):
                    for k in range(PIECES * e, PIECES * e + PIECES):
                        splitter.load_high(k, pieces[k], w_high[:, e % 2])

                def subtract(e):
                    for k in range(PIECES * e, PIECES * e + PIECES):
                        splitter.subtract(k, pieces[k], w_high[:, e % 2], w_low[:, e % 2])
                        if k + 2 < NE * PIECES:
                            splitter.load_stage(k + 2, pieces[k + 2])

                for k in range(2):
                    splitter.load_stage(k, pieces[k])
                load_high(0)
                subtract(0)
                load_high(1)

                pool.wait_ge(slots_ready, 1)
                for t in range(NT):
                    scatter(t, t % 2)

                for par in range(2):
                    pool.wait_ge(sorted_[par], 16 * TOP * NT // 2)
                pool.wait_ge(plan_ready, 3)
                nc.gpsimd.tensor_tensor(token[:], token[:], token[:], ALU.add).then_inc(buffer_free, 1)
                pool.wait_ge(buffer_free, 1)
                subtract(1)
                for e in range(2, NE):
                    end = pool.value_load(ends[0:1, e - 2:e - 1], min_val=0, max_val=SLOT_TILES)
                    pool.wait_ge(down_done, end + units)
                    nc.gpsimd.tensor_tensor(token[:], token[:], token[:], ALU.add).then_inc(buffer_free, 1)
                    pool.wait_ge(buffer_free, e)
                    load_high(e)
                    subtract(e)

            else:
                def gather(k, nk, par, t):
                    if nk >= 2:
                        pool.wait_ge(result_ready, k - 1)
                    for j in range(TOP):
                        pool.indirect_dma_start(out=y_in[:, par, j], out_offset=None, in_=y[:, :],
                                                in_offset=bass.IndirectOffsetOnAxis(ap=slots[:, j, t:t + 1], axis=0)).then_inc(y_loaded[par], 16)

                for par in range(2):
                    pool.wait_ge(y_stored[par], 16 * ((SLOT_TILES + 1 - par) // 2))
                nc.gpsimd.memset(arrived[:], 0.0).then_inc(pad_set, 1)
                pool.wait_ge(pad_set, 2)
                gather(0, 0, 0, 0)
                gather(1, 1, 1, t_first)
                for m in range(1, t_n):
                    gather(2 * m, 2, 0, m)
                    gather(2 * m + 1, 3, 1, m + t_first)

        @block.scalar
        def _(act):
            def x_part(a):
                act.wait_ge(x_turned, a + 1)
                nc.scalar.activation(x_high[:], ps_x[:], ACT.Copy).then_inc(x_high_ready, 1)

            def silu(q):
                act.wait_ge(up_done, q + 1)
                nc.scalar.activation(gated[:], ps_g[:, 0:HID], ACT.Silu).then_inc(silu_done, 1)

            def h_part(q):
                act.wait_ge(h_turned, q + 1)
                nc.scalar.activation(h_high[:], ps_h[:], ACT.Copy).then_inc(h_high_ready, 1)

            def shared_tile(m, last):
                silu(2 * m)
                h_part(2 * m)
                silu(2 * m + 1)
                if not last:
                    x_part(m + 1)
                h_part(2 * m + 1)

            x_part(0)
            with act.Fori(0, t_n - 1) as m:
                shared_tile(m, False)
            shared_tile(t_n - 1, not routed)
            if routed:
                with act.Fori(0, r_n - 1) as i:
                    silu(units + i)
                    x_part(t_n + i + 1)
                    h_part(units + i)
                silu(units + r_n - 1)
                h_part(units + r_n - 1)

        @block.vector
        def _(dve):
            def normalize(out_ap, t):
                return nc.vector.tensor_scalar(out_ap, x_res[:, bass.ds(t, 1), :].rearrange("p o c -> p (o c)"), mean[:, bass.ds(t, 1)],
                                               rstd[:, bass.ds(t, 1)], ALU.subtract, ALU.mult)

            def x_norm(m, nm):
                if nm > (SORT_AT if routed else 0):
                    dve.wait_ge(x_turned, m)
                normalize(tokens(nm), m + t_first).then_inc(x_normed, 1)

            def x_part(a):
                dve.wait_ge(x_high_ready, a + 1)
                nc.vector.tensor_tensor(x_low[:], ps_x[:], x_high[:].bitcast(F32), ALU.subtract).then_inc(x_split, 1)

            def hide(q):
                dve.wait_ge(silu_done, q + 1)
                nc.vector.tensor_tensor(hidden[:, 0:HID], ps_u[:, 0:HID], gated[:], ALU.mult).then_inc(hidden_ready, 1)

            def h_part(q):
                dve.wait_ge(h_high_ready, q + 1)
                nc.vector.tensor_tensor(h_low[:], ps_h[:], h_high[:].bitcast(F32), ALU.subtract).then_inc(h_split, 1)

            def beside(m, nm, k):
                if not routed or nm >= SORT_AT + SORT_TILES:
                    return
                if nm < SORT_AT:
                    routing.vector_step(dve, 4 * nm + k)
                    return
                t, nt, par = 4 * (m - SORT_AT) + k, 4 * (nm - SORT_AT) + k, k % 2
                if nt < SORT_AT:
                    return
                if nt >= SORT_AT + 1:
                    dve.wait_ge(sorted_[par], 16 * (t - par))
                normalize(to_sort[:, par], t).then_inc(sort_ready, 1)

            def add_shared(m):
                dve.wait_ge(down_done, 2 * m + 2)
                row = x_res[:, bass.ds(m + t_first, 1), :].rearrange("p o c -> p (o c)")
                nc.vector.tensor_tensor(row, row, ps_y[:], ALU.add).then_inc(y_read, 1)

            def combine(k, nk, par, m, t):
                if routed:
                    return
                dve.wait_ge(y_loaded[par], 32 * m + 32)
                if nk >= 2:
                    dve.wait_ge(stored[par], 16 * m)
                row = x_res[:, bass.ds(t, 1), :].rearrange("p o c -> p (o c)")
                nc.vector.scalar_tensor_tensor(out=result[:, par], in0=y_in[:, par, 0], scalar=weights_out[:, bass.ds(t, 1), 0], in1=row,
                                               op0=ALU.mult, op1=ALU.add).then_inc(part_ready, 1)
                dve.wait_ge(part_ready, k + 1)
                nc.vector.scalar_tensor_tensor(out=result[:, par], in0=y_in[:, par, 1], scalar=weights_out[:, bass.ds(t, 1), 1], in1=result[:, par],
                                               op0=ALU.mult, op1=ALU.add).then_inc(result_ready, 1)

            def shared_tile(m, nm):
                last = nm == t_n - 1
                hide(2 * m)
                beside(m, nm, 0)
                if not last:
                    x_norm(m + 1, nm + 1)
                if nm >= 1:
                    add_shared(m - 1)
                h_part(2 * m)
                beside(m, nm, 1)
                if nm >= 1 and not routed:
                    dve.wait_ge(y_read, m)
                    combine(2 * m - 1, nm, 1, m - 1, m - 1 + t_first)
                hide(2 * m + 1)
                beside(m, nm, 2)
                if routed or not last:
                    x_part(m + 1)
                h_part(2 * m + 1)
                beside(m, nm, 3)
                combine(2 * m, 2 * nm, 0, m, m)

            x_norm(0, 0)
            x_part(0)
            shared_tile(0, 0)
            if routed:
                for m in range(1, SORT_AT + 1):
                    shared_tile(m, m)
                with dve.Fori(SORT_AT + 1, SORT_AT + SORT_TILES) as m:
                    shared_tile(m, SORT_AT + 1)
                for m in range(SORT_AT + SORT_TILES, t_n - 1):
                    shared_tile(m, m)
            else:
                shared_tile(1, 1)
                with dve.Fori(2, t_n - 1) as m:
                    shared_tile(m, 2)
            shared_tile(t_n - 1, t_n - 1)
            if routed:
                def copy_y(i, ni):
                    dve.wait_ge(down_done, units + i + 1)
                    if ni >= 2:
                        dve.wait_ge(y_stored[ni % 2], 8 * (i - ni % 2))
                    else:
                        dve.wait_ge(sorted_[ni], 16 * TOP * NT // 2)
                    nc.vector.tensor_copy(y_out[:, ni % 2], ps_y[:]).then_inc(y_read, 1)

                def routed_tile(i, ni):
                    hide(units + i)
                    if ni < r_n - 1:
                        x_part(t_n + i + 1)
                    if ni == 0:
                        add_shared(t_n - 1)
                    else:
                        copy_y(i - 1, ni - 1)
                    h_part(units + i)

                for i in range(3):
                    routed_tile(i, i)
                loops = (r_n - 4) // 2 * 2
                with dve.Fori(3, 3 + loops, 2) as i:
                    routed_tile(i, 3)
                    routed_tile(i + 1, 4)
                for i in range(3 + loops, r_n):
                    routed_tile(i, i)
                copy_y(r_n - 1, r_n - 1)
            else:
                add_shared(t_n - 1)
                dve.wait_ge(y_read, t_n)
                combine(2 * t_n - 1, 2, 1, t_n - 1, t_n - 1 + t_first)

        @block.tensor
        def _(pe):
            def turn_x(a, na, source):
                if na >= 1:
                    pe.wait_ge(x_split, a)
                for c in range(EC):
                    last = nc.tensor.transpose(ps_x[:, c], source[:, c * P:(c + 1) * P], ident[:])
                last.then_inc(x_turned, 1)

            def up(q, nq, a, high, low):
                pe.wait_ge(x_split, a + 1)
                if nq >= 1:
                    pe.wait_ge(hidden_ready, q)
                for bank, at in ((ps_g, 0), (ps_u, UP_AT)):
                    for c in range(EC):
                        cols = slice(at + c * HID, at + (c + 1) * HID)
                        for k, (x_part, w_part) in enumerate(((x_high, high), (x_high, low), (x_low, high))):
                            last = nc.tensor.matmul(bank[:, 0:HID], x_part[:, c], w_part(P, cols), start=(c == 0 and k == 0),
                                                    stop=(c == EC - 1 and k == 2))
                last.then_inc(up_done, 1)

            def turn_h(q, nq):
                pe.wait_ge(hidden_ready, q + 1)
                if nq >= 1:
                    pe.wait_ge(h_split, q)
                for c in range(HC):
                    last = nc.tensor.transpose(ps_h[:, c], hidden[:, c * P:(c + 1) * P], ident[:])
                last.then_inc(h_turned, 1)

            def down(q, high, low, first, final):
                pe.wait_ge(h_split, q + 1)
                for c in range(HC):
                    rows = P if c < HC - 1 else HID_TAIL
                    cols = slice(DOWN_AT + c * E, DOWN_AT + (c + 1) * E)
                    for k, (h_part, w_part) in enumerate(((h_high, high), (h_high, low), (h_low, high))):
                        last = nc.tensor.matmul(ps_y[:], h_part[0:rows, c], w_part(rows, cols), start=(first and c == 0 and k == 0),
                                                stop=(final and c == HC - 1 and k == 2))
                last.then_inc(down_done, 1)

            def shared(s):
                return (lambda rows, cols: sh[0:rows, s, cols]), (lambda rows, cols: sl[0:rows, s, cols])

            def turn_routed(i, ni):
                pe.wait_ge(x_loaded[ni % 2], 8 * (i - ni % 2) + 16)
                turn_x(t_n + i, 1, x_in[:, 1 - ni % 2])

            def shared_tile(m, nm, last):
                up(2 * m, nm, m, *shared(0))
                if routed and nm == 1:
                    routing.count(pe)
                if nm >= 1:
                    down(2 * m - 1, *shared(1), False, True)
                turn_h(2 * m, nm)
                up(2 * m + 1, 1, m, *shared(1))
                if not last:
                    pe.wait_ge(x_normed, m + 2)
                    turn_x(m + 1, 1, tokens(nm + 1))
                elif routed:
                    turn_routed(0, 0)
                if nm >= 1:
                    pe.wait_ge(y_read, m)
                down(2 * m, *shared(0), True, False)
                turn_h(2 * m + 1, 1)

            pe.wait_ge(pad_set, 1)
            pe.wait_ge(x_normed, 1)
            turn_x(0, 0, tokens(0))
            shared_tile(0, 0, False)
            shared_tile(1, 1, False)
            with pe.Fori(2, t_n - 1) as m:
                shared_tile(m, 2, False)
            shared_tile(t_n - 1, 1, True)
            if not routed:
                down(units - 1, *shared(1), False, True)
                return

            def planned(i):
                _, (expert, slot) = nc.values_load_multi_w_load_instructions(plan[0:1, bass.ds(i, 1), :].rearrange("p o k -> p (o k)"),
                                                                           engines=[mybir.EngineType.PE], min_val=0, max_val=NE)
                slot = nc.s_assert_within(slot, 0, 1, skip_runtime_bounds_check_because="the table holds the lowest bit of the expert's number")

                def of(w):
                    return lambda rows, cols: w[0:rows, bass.ds(slot, 1), cols].rearrange("p o c -> p (o c)")

                return expert, of(w_high), of(w_low)

            def routed_up(i, tile):
                expert, high, low = tile
                pe.wait_ge(weights_split, expert * PIECES + 2)
                up(units + i, 1, t_n + i, high, low)

            def routed_down(i, tile):
                expert, high, low = tile
                pe.wait_ge(y_read, t_n + i)
                pe.wait_ge(weights_split, expert * PIECES + PIECES)
                down(units + i, high, low, True, True)

            def routed_step(i, ni):
                if ni >= 1:
                    last_tile = planned(i - 1)
                turn_routed(i + 1, ni + 1)
                if ni >= 1:
                    routed_down(i - 1, last_tile)
                else:
                    down(units - 1, *shared(1), False, True)
                next_tile = planned(i + 1)
                turn_h(units + i, 1)
                routed_up(i + 1, next_tile)

            pe.wait_ge(plan_ready, 3)
            routed_up(0, planned(0))
            routed_step(0, 0)
            loops = (r_n - 2) // LOOP_TILES * LOOP_TILES
            with pe.Fori(1, 1 + loops, LOOP_TILES) as i:
                for k in range(LOOP_TILES):
                    routed_step(i + k, 1 + k)
            for i in range(1 + loops, r_n - 1):
                routed_step(i, i)
            last_tiles = planned(r_n - 2), planned(r_n - 1)
            routed_down(r_n - 2, last_tiles[0])
            turn_h(units + r_n - 1, 1)
            routed_down(r_n - 1, last_tiles[1])


def build(nc, x, ctx512, gate_w, w_gate, w_up, w_down, sw_gate, sw_up, sw_down, out):
    q_scr = nc.dram_tensor("q_scr", (B, E, TERMS, S), BF16, kind="Internal").ap()
    k_scr = nc.dram_tensor("k_scr", (B, KV * D, TERMS, S), BF16, kind="Internal").ap()
    xg = nc.dram_tensor("x_sorted", (SLOT_ROWS, E), F32, kind="Internal").ap()
    y = nc.dram_tensor("y_sorted", (SLOT_TILES * P, E), F32, kind="Internal").ap()
    with ExitStack() as ctx:
        def sb(name, shape, dt=F32):
            return ctx.enter_context(nc.sbuf_tensor(name, shape, dt))

        x_res = sb("x_res", [P, NT, E])
        ident = sb("ident", [P, P])
        ident_bf = sb("ident_bf", [P, P], BF16)
        mean2, rstd2 = sb("mean2", [P, NT]), sb("rstd2", [P, NT])
        exps, top_w = sb("exps", [P, NT, NE]), sb("top_w", [P, NT, TOP])
        slots = sb("slots", [P, TOP, NT], U32)
        plan, ends = sb("plan", [1, SLOT_TILES + LOOP_TILES, 2], I32), sb("ends", [1, NE], I32)
        sh, sl = sb("shared_high", [P, SETS, W_COLS], F32R), sb("shared_low", [P, SETS, W_COLS], F32R)

        attention(nc, x_res, ident, ident_bf, (mean2, rstd2), x, ctx512, q_scr, k_scr, xg, sh, sl, (sw_gate, sw_up, sw_down),
                  gate_w, exps)
        y_stored = [ctx.enter_context(nc.semaphore(f"y_stored{i}")) for i in range(2)]
        common = (x_res, ident, (mean2, rstd2), (sh, sl), slots, plan, ends, xg, y, y_stored)
        feed_forward(nc, (0, NA), True, exps, *common, None, top_w, (w_gate, w_up, w_down))
        feed_forward(nc, (NA, NT - NA), False, None, *common, out.rearrange("b s e -> (b s) e"), top_w, None)


_INS = ["x", "ctx_512", "L0_ffn_gate_w", "L0_ffn_w_gate", "L0_ffn_w_up", "L0_ffn_w_down", "L0_ffn_sw_gate", "L0_ffn_sw_up", "L0_ffn_sw_down"]


def kernel(**inputs):
    import numpy as _np
    import concourse.bacc as _bacc
    from concourse import mybir as _mybir
    from concourse.bass_utils import run_bass_kernel_spmd as _run

    nc = _bacc.Bacc("TRN2", target_bir_lowering=False, num_devices=1)
    arrays, args = {}, []
    for name in _INS:
        a = _np.ascontiguousarray(inputs[name])
        arrays[f"in_{name}_dram"] = a
        args.append(nc.dram_tensor(f"in_{name}_dram", a.shape, _mybir.dt.from_np(a.dtype), kind="ExternalInput").ap())
    out = nc.dram_tensor("out_dram", (B, S, E), _mybir.dt.float32, kind="ExternalOutput").ap()
    build(nc, *args, out)
    r = _run(nc, [arrays], core_ids=[0])
    return r.results[0]["out_dram"]
```
